# Optimizing a Trainium2 kernel written in Bass

```python
import numpy as np
import jax
import jax.numpy as jnp

def _softmax(x, axis=-1):
    return jax.nn.softmax(x, axis=axis)

def _gelu(x):
    return jax.nn.gelu(x, approximate=True)

def _silu(x):
    return jax.nn.silu(x)

def _sigmoid(x):
    return jax.nn.sigmoid(x)

def _layernorm(x, axis=-1, eps=1e-05):
    m = jnp.mean(x, axis=axis, keepdims=True)
    v = jnp.var(x, axis=axis, keepdims=True)
    return (x - m) / jnp.sqrt(v + eps)

def _scatter_add(tgt, idx, src, axis=0):
    return tgt.at[idx].add(src)

def _segment_sum(src, seg, n):
    return jax.ops.segment_sum(src, seg, n)
kernel_name = 'mk_audio_tower_d2_tok_audfeat768_r4_a696b9'

def setup_inputs(seed: int=0):
    np.random.seed(seed)
    _w = jnp.asarray

    def _rec_inputs():
        import jax
        import jax.numpy as jnp
        _rk = jax.random.key(seed)
        x = -0.000253961 + 1 * jax.random.normal(jax.random.fold_in(_rk, 1), (64, 90, 750), jnp.float32)
        return x
    x = _rec_inputs()

    def _L0_tok_setup():
        import jax, jax.numpy as jnp
        import numpy as np
        CHANNELS = 90
        PATCH = 16
        EMBED = 192
        key = jax.random.key(seed)
        k_x, k_w, k_b = jax.random.split(key, 3)
        in_feat = CHANNELS * PATCH
        x = jax.random.normal(k_x, (128, CHANNELS, 512), dtype=jnp.float32)
        bound = 1.0 / np.sqrt(in_feat)
        W = jax.random.uniform(k_w, (EMBED, in_feat), dtype=jnp.float32, minval=-bound, maxval=bound)
        b = jax.random.uniform(k_b, (EMBED,), dtype=jnp.float32, minval=-bound, maxval=bound)
        return {'x': x, 'W': W, 'b': b}
    _L0_tok_all = _L0_tok_setup()
    _L0_tok_in = {k: v for k, v in _L0_tok_all.items() if k in ('W', 'b')}
    del _L0_tok_all

    def _L0_attn_setup():
        import jax, jax.numpy as jnp
        import numpy as np
        ALPHA = 0.35

        def _round_ln_pow2(x):
            y = jnp.floor(jnp.log2(x))
            up = x - 2.0 ** y > 2.0 ** (y + 1.0) - x
            return 2.0 ** (y + up.astype(x.dtype))
        key = jax.random.key(seed)
        k1, k2, k3, k4, k5 = jax.random.split(key, 5)
        B, N, C = (64, 197, 192)
        return {'x': jax.random.normal(k1, (B, N, C), dtype=jnp.float32), 'qkv_weight': jax.random.normal(k2, (3 * C, C), dtype=jnp.float32) * 0.02, 'qkv_bias': jax.random.normal(k3, (3 * C,), dtype=jnp.float32) * 0.02, 'proj_weight': jax.random.normal(k4, (C, C), dtype=jnp.float32) * 0.02, 'proj_bias': jax.random.normal(k5, (C,), dtype=jnp.float32) * 0.02}
    _L0_attn_all = _L0_attn_setup()
    _L0_attn_in = {k: v for k, v in _L0_attn_all.items() if k in ('qkv_weight', 'qkv_bias', 'proj_weight', 'proj_bias')}
    del _L0_attn_all

    def _L0_ffn_setup():
        import jax, jax.numpy as jnp
        import numpy as np
        B, N, C, H, E = (8, 256, 192, 768, 4)
        key = jax.random.key(seed)
        ks = jax.random.split(key, 8)
        s_in = 1.0 / np.sqrt(C)
        s_h = 1.0 / np.sqrt(H)
        return {'x': jax.random.normal(ks[0], (B, N, C), dtype=jnp.float32), 'gate_w': jax.random.normal(ks[1], (C, E), dtype=jnp.float32) * 0.01, 'gate_b': jnp.zeros((E,), dtype=jnp.float32), 'gate_center': jnp.zeros((E,), dtype=jnp.float32), 'w1': jax.random.uniform(ks[2], (E, C, H), jnp.float32, -s_in, s_in), 'b1': jax.random.uniform(ks[3], (E, H), jnp.float32, -s_in, s_in), 'w2': jax.random.uniform(ks[4], (E, H, C), jnp.float32, -s_h, s_h), 'b2': jax.random.uniform(ks[5], (E, C), jnp.float32, -s_h, s_h)}
    _L0_ffn_all = _L0_ffn_setup()
    _L0_ffn_in = {k: v for k, v in _L0_ffn_all.items() if k in ('gate_w', 'gate_b', 'gate_center', 'w1', 'b1', 'w2', 'b2')}
    del _L0_ffn_all

    def _L1_attn_setup():
        import jax, jax.numpy as jnp
        import numpy as np
        N_HEADS = 12

        def gconv1x1(x, w, b, groups):
            B, C, T, S = x.shape
            O, I = w.shape
            xr = x.reshape(B, groups, C // groups, T, S)
            wr = w.reshape(groups, O // groups, I)
            y = jnp.einsum('bgits,goi->bgots', xr, wr).reshape(B, O, T, S)
            return y + b[None, :, None, None]
        key = jax.random.key(seed)
        ks = jax.random.split(key, 16)
        B, T, E = (2, 128, 192)
        H = N_HEADS
        s = 0.02
        inp = {'x': jax.random.normal(ks[0], (B, T, E), jnp.float32), 'wq': jax.random.normal(ks[1], (E, E), jnp.float32) * s, 'bq': jax.random.normal(ks[2], (E,), jnp.float32) * s, 'wk': jax.random.normal(ks[3], (E, E), jnp.float32) * s, 'bk': jax.random.normal(ks[4], (E,), jnp.float32) * s, 'wv': jax.random.normal(ks[5], (E, E), jnp.float32) * s, 'bv': jax.random.normal(ks[6], (E,), jnp.float32) * s, 'w1': jax.random.normal(ks[7], (8 * H, H), jnp.float32) * s, 'b1': jax.random.normal(ks[8], (8 * H,), jnp.float32) * s, 'w2': jax.random.normal(ks[9], (H, 8), jnp.float32) * s, 'b2': jax.random.normal(ks[10], (H,), jnp.float32) * s, 'w3': jax.random.normal(ks[11], (4 * H, 1), jnp.float32) * s, 'b3': jax.random.normal(ks[12], (4 * H,), jnp.float32) * s, 'w4': jax.random.normal(ks[13], (H, 4), jnp.float32) * s, 'b4': jax.random.normal(ks[14], (H,), jnp.float32) * s}
        return inp
    _L1_attn_all = _L1_attn_setup()
    _L1_attn_in = {k: v for k, v in _L1_attn_all.items() if k in ('wq', 'bq', 'wk', 'bk', 'wv', 'bv', 'w1', 'b1', 'w2', 'b2', 'w3', 'b3', 'w4', 'b4')}
    del _L1_attn_all

    def _L1_ffn_setup():
        import jax, jax.numpy as jnp
        import numpy as np
        E = 8
        TOP_K = 2
        C = 192
        F = 4 * C
        key = jax.random.key(seed)
        ks = jax.random.split(key, 8)
        s_in = 1.0 / np.sqrt(C)
        s_hid = 1.0 / np.sqrt(F)
        x = jax.random.normal(ks[0], (4, 512, C), dtype=jnp.float32)
        Wg = jax.random.uniform(ks[1], (C, E), jnp.float32, -s_in, s_in)
        bg = jax.random.uniform(ks[2], (E,), jnp.float32, -s_in, s_in)
        W1 = jax.random.uniform(ks[3], (E, C, F), jnp.float32, -s_in, s_in)
        b1 = jax.random.uniform(ks[4], (E, F), jnp.float32, -s_in, s_in)
        W2 = jax.random.uniform(ks[5], (E, F, C), jnp.float32, -s_hid, s_hid)
        b2 = jax.random.uniform(ks[6], (E, C), jnp.float32, -s_hid, s_hid)
        return {'x': x, 'Wg': Wg, 'bg': bg, 'W1': W1, 'b1': b1, 'W2': W2, 'b2': b2}
    _L1_ffn_all = _L1_ffn_setup()
    _L1_ffn_in = {k: v for k, v in _L1_ffn_all.items() if k in ('Wg', 'bg', 'W1', 'b1', 'W2', 'b2')}
    del _L1_ffn_all
    return {'x': x, 'L0_tok_W': _L0_tok_in['W'], 'L0_tok_b': _L0_tok_in['b'], 'L0_attn_qkv_weight': _L0_attn_in['qkv_weight'], 'L0_attn_qkv_bias': _L0_attn_in['qkv_bias'], 'L0_attn_proj_weight': _L0_attn_in['proj_weight'], 'L0_attn_proj_bias': _L0_attn_in['proj_bias'], 'L0_ffn_gate_w': _L0_ffn_in['gate_w'], 'L0_ffn_gate_b': _L0_ffn_in['gate_b'], 'L0_ffn_gate_center': _L0_ffn_in['gate_center'], 'L0_ffn_w1': _L0_ffn_in['w1'], 'L0_ffn_b1': _L0_ffn_in['b1'], 'L0_ffn_w2': _L0_ffn_in['w2'], 'L0_ffn_b2': _L0_ffn_in['b2'], 'L1_attn_wq': _L1_attn_in['wq'], 'L1_attn_bq': _L1_attn_in['bq'], 'L1_attn_wk': _L1_attn_in['wk'], 'L1_attn_bk': _L1_attn_in['bk'], 'L1_attn_wv': _L1_attn_in['wv'], 'L1_attn_bv': _L1_attn_in['bv'], 'L1_attn_w1': _L1_attn_in['w1'], 'L1_attn_b1': _L1_attn_in['b1'], 'L1_attn_w2': _L1_attn_in['w2'], 'L1_attn_b2': _L1_attn_in['b2'], 'L1_attn_w3': _L1_attn_in['w3'], 'L1_attn_b3': _L1_attn_in['b3'], 'L1_attn_w4': _L1_attn_in['w4'], 'L1_attn_b4': _L1_attn_in['b4'], 'L1_ffn_Wg': _L1_ffn_in['Wg'], 'L1_ffn_bg': _L1_ffn_in['bg'], 'L1_ffn_W1': _L1_ffn_in['W1'], 'L1_ffn_b1': _L1_ffn_in['b1'], 'L1_ffn_W2': _L1_ffn_in['W2'], 'L1_ffn_b2': _L1_ffn_in['b2']}

def reference(x, L0_tok_W, L0_tok_b, L0_attn_qkv_weight, L0_attn_qkv_bias, L0_attn_proj_weight, L0_attn_proj_bias, L0_ffn_gate_w, L0_ffn_gate_b, L0_ffn_gate_center, L0_ffn_w1, L0_ffn_b1, L0_ffn_w2, L0_ffn_b2, L1_attn_wq, L1_attn_bq, L1_attn_wk, L1_attn_bk, L1_attn_wv, L1_attn_bv, L1_attn_w1, L1_attn_b1, L1_attn_w2, L1_attn_b2, L1_attn_w3, L1_attn_b3, L1_attn_w4, L1_attn_b4, L1_ffn_Wg, L1_ffn_bg, L1_ffn_W1, L1_ffn_b1, L1_ffn_W2, L1_ffn_b2):
    import jax
    import jax.numpy as jnp

    def _L0_tok_ref(x, W, b):
        import jax, jax.numpy as jnp
        import numpy as np
        CHANNELS = 90
        PATCH = 16
        EMBED = 192
        B, C, T = x.shape
        n = T // PATCH
        patches = x[:, :, :n * PATCH].reshape(B, C, n, PATCH)
        patches = patches.transpose(0, 2, 1, 3).reshape(B, n, C * PATCH)
        return jnp.einsum('bnf,ef->bne', patches, W) + b

    def _L0_attn_ref(x, qkv_weight, qkv_bias, proj_weight, proj_bias):
        import jax, jax.numpy as jnp
        import numpy as np
        ALPHA = 0.35

        def _round_ln_pow2(x):
            y = jnp.floor(jnp.log2(x))
            up = x - 2.0 ** y > 2.0 ** (y + 1.0) - x
            return 2.0 ** (y + up.astype(x.dtype))
        B, N, C = x.shape
        num_heads = 12
        head_dim = C // num_heads
        scale = head_dim ** (-0.5)
        global_max_x = jnp.abs(x).max(axis=(0, 1))
        max_weight = jnp.abs(qkv_weight).max(axis=0)
        channel_scale = _round_ln_pow2(global_max_x ** ALPHA / max_weight ** (1.0 - ALPHA))
        x_smoothed = x / channel_scale[None, None, :]
        weight_smoothed = qkv_weight * channel_scale[None, :]
        h = jnp.einsum('bnc,mc->bnm', x_smoothed, weight_smoothed) + qkv_bias
        qkv = h.reshape(B, N, 3, num_heads, head_dim).transpose(2, 0, 3, 1, 4)
        q, k, v = (qkv[0], qkv[1], qkv[2])
        attn = jnp.einsum('bhnd,bhmd->bhnm', q, k) * scale
        attn = jax.nn.softmax(attn, axis=-1)
        out = jnp.einsum('bhnm,bhmd->bhnd', attn, v)
        out = out.transpose(0, 2, 1, 3).reshape(B, N, C)
        out = jnp.einsum('bnc,mc->bnm', out, proj_weight) + proj_bias
        return out

    def _L0_ffn_ref(x, gate_w, gate_b, gate_center, w1, b1, w2, b2):
        import jax, jax.numpy as jnp
        import numpy as np
        B, N, C, H, E = (8, 256, 192, 768, 4)
        b, n, c = x.shape
        scores = jnp.einsum('bnc,ce->bne', x, gate_w) + gate_b
        p_experts = jax.nn.softmax(scores - gate_center, axis=-1)
        expert = jnp.argmax(p_experts, axis=-1).reshape(-1)
        xt = x.reshape(-1, c)
        h = jax.nn.gelu(jnp.einsum('tc,ech->eth', xt, w1) + b1[:, None, :], approximate=False)
        out_all = jnp.einsum('eth,ehc->etc', h, w2) + b2[:, None, :]
        out = jnp.take_along_axis(out_all, expert[None, :, None], axis=0)[0]
        return out.reshape(b, n, c)

    def _L1_attn_ref(x, wq, bq, wk, bk, wv, bv, w1, b1, w2, b2, w3, b3, w4, b4):
        import jax, jax.numpy as jnp
        import numpy as np
        N_HEADS = 12

        def gconv1x1(x, w, b, groups):
            B, C, T, S = x.shape
            O, I = w.shape
            xr = x.reshape(B, groups, C // groups, T, S)
            wr = w.reshape(groups, O // groups, I)
            y = jnp.einsum('bgits,goi->bgots', xr, wr).reshape(B, O, T, S)
            return y + b[None, :, None, None]
        B, T, E = x.shape
        H = N_HEADS
        hd = E // H
        scale = E ** 0.5

        def heads(y):
            return y.reshape(B, T, H, hd).transpose(2, 0, 1, 3)
        q = heads(x @ wq.T + bq)
        k = heads(x @ wk.T + bk)
        v = heads(x @ wv.T + bv)
        attn = jnp.einsum('qbld,kbtd->qkblt', q, k) / scale
        attn = attn.transpose(2, 0, 1, 3, 4).reshape(B, H * H, T, T)
        a = jax.nn.relu(gconv1x1(attn, w1, b1, H))
        a = gconv1x1(a, w2, b2, H)
        a = jax.nn.relu(gconv1x1(a, w3, b3, H))
        a = gconv1x1(a, w4, b4, H)
        ctx = jnp.einsum('bhlt,hbtd->blhd', a, v).reshape(B, T, E)
        return ctx

    def _L1_ffn_ref(x, Wg, bg, W1, b1, W2, b2):
        import jax, jax.numpy as jnp
        import numpy as np
        E = 8
        TOP_K = 2
        C = 192
        F = 4 * C
        B, T, Cc = x.shape
        x_flat = x.reshape(-1, Cc)
        logits = x_flat @ Wg + bg
        gates, indices = jax.lax.top_k(logits, TOP_K)
        gates = jax.nn.softmax(gates, axis=-1)
        onehot = jax.nn.one_hot(indices, E, dtype=x_flat.dtype)
        weights = jnp.einsum('nk,nke->ne', gates, onehot)
        out = jnp.zeros_like(x_flat)
        for e in range(E):
            h = jax.nn.relu(x_flat @ W1[e] + b1[e])
            y = h @ W2[e] + b2[e]
            out = out + weights[:, e:e + 1] * y
        return out.reshape(B, T, Cc)
    h = _L0_tok_ref(x, L0_tok_W, L0_tok_b)
    h = h + _L0_attn_ref(_layernorm(h, axis=-1), L0_attn_qkv_weight, L0_attn_qkv_bias, L0_attn_proj_weight, L0_attn_proj_bias)
    h = h + _L0_ffn_ref(_layernorm(h, axis=-1), L0_ffn_gate_w, L0_ffn_gate_b, L0_ffn_gate_center, L0_ffn_w1, L0_ffn_b1, L0_ffn_w2, L0_ffn_b2)
    h = h + _L1_attn_ref(_layernorm(h, axis=-1), L1_attn_wq, L1_attn_bq, L1_attn_wk, L1_attn_bk, L1_attn_wv, L1_attn_bv, L1_attn_w1, L1_attn_b1, L1_attn_w2, L1_attn_b2, L1_attn_w3, L1_attn_b3, L1_attn_w4, L1_attn_b4)
    h = h + _L1_ffn_ref(_layernorm(h, axis=-1), L1_ffn_Wg, L1_ffn_bg, L1_ffn_W1, L1_ffn_b1, L1_ffn_W2, L1_ffn_b2)
    return h

_drawn_inputs = setup_inputs


def setup_inputs(seed=0):
    import zlib

    import numpy as np

    out = dict(_drawn_inputs(seed))
    spreads = {'L0_ffn_gate_b': (0.0, 0.1), 'L0_ffn_gate_center': (0.0, 0.1)}
    factors = {'L1_attn_wq': 8.0,
     'L1_attn_bq': 51.167,
     'L1_attn_wk': 8.0,
     'L1_attn_bk': 42.078,
     'L1_attn_w1': 8.0,
     'L1_attn_b1': 26.557,
     'L1_attn_w2': 8.0,
     'L1_attn_b2': 8.0,
     'L1_attn_w3': 8.0,
     'L1_attn_b3': 6.824,
     'L1_attn_w4': 6.349,
     'L1_ffn_b1': 2.936}
    for name, (base, spread) in spreads.items():
        noise = np.random.default_rng([zlib.crc32(name.encode()), seed]).standard_normal(out[name].shape)
        drawn = base * np.exp(spread * noise) if base else spread * noise
        out[name] = jnp.asarray(drawn.astype(out[name].dtype))
    for name, factor in factors.items():
        out[name] = (out[name] * factor).astype(out[name].dtype)
    return out
```

```python
from contextlib import ExitStack

import concourse.bass as bass
from concourse import mybir

F32 = mybir.dt.float32
BF16 = mybir.dt.bfloat16
I32 = mybir.dt.int32
U32 = mybir.dt.uint32
ALU = mybir.AluOpType
ACT = mybir.ActivationFunctionType
AX = mybir.AxisListType

B, CH, T_IN = 64, 90, 750
PATCH, N = 16, 46
C = 192
CA, CB = C // 2, C // 2
TOK = B * N
GB = 8
G = B // GB
GT = GB * N
H, HD = 12, 16
PAIRS = H // 2
PB = PAIRS // 2
NN = 2 * N
F = 768
FC = F // 128
EPS = 1e-5
O1, O3 = 8, 4
Q3 = 3
ROWS = [128, 128, GT - 256]
RT = G * Q3
TILES0 = (TOK + 4 * 127) // 128
TILES1 = (2 * TOK + 8 * 127) // 128


def seg(block):
    return (slice(0, CA), CA) if block == 0 else (slice(CA, C), CB)


class Tower:

    def __init__(self, nc, inp, out):
        self.nc, self.inp, self.out = nc, inp, out
        self.used = []

    def semaphore(self, scope, name):
        handle = scope.enter_context(self.nc.semaphore(name))
        self.used.append(handle)
        return handle

    def clear_semaphores(self):
        with self.nc.Block() as block:
            @block.gpsimd
            def _(pool):
                for handle in self.used:
                    pool.sem_clear(handle)
        self.used = []

    def constants(self):
        nc = self.nc
        with ExitStack() as ctx:
            made = self.semaphore(ctx, "const_made")
            block = ctx.enter_context(nc.Block())
            ident, head, pairsel = self.ident, self.head_mask, self.pair_rows

            @block.gpsimd
            def _(pool):
                steps = 0

                def after(ins):
                    nonlocal steps
                    ins.then_inc(made, 1)
                    steps += 1
                    pool.wait_ge(made, steps)

                after(pool.memset(ident[:, :], 0.0))
                after(pool.affine_select(out=ident[:, :], in_=ident[:, :], compare_op=ALU.not_equal, fill=1.0,
                                         base=0, pattern=[[-1, 128]], channel_multiplier=1))
                after(pool.memset(head[:, :], 1.0))
                after(pool.affine_select(out=head[:, :], in_=head[:, :], compare_op=ALU.is_ge, fill=0.0,
                                         base=0, pattern=[[-HD, 8]], channel_multiplier=1))
                after(pool.affine_select(out=head[:, :], in_=head[:, :], compare_op=ALU.is_ge, fill=0.0,
                                         base=HD - 1, pattern=[[HD, 8]], channel_multiplier=-1))
                after(pool.memset(pairsel[:, :], 1.0))
                after(pool.affine_select(out=pairsel[:, :], in_=pairsel[:, :], compare_op=ALU.is_ge, fill=0.0,
                                         base=0, pattern=[[1, NN]], channel_multiplier=-N))
                after(pool.affine_select(out=pairsel[:, :], in_=pairsel[:, :], compare_op=ALU.is_ge, fill=0.0,
                                         base=N - 1, pattern=[[-1, NN]], channel_multiplier=N))
                after(pool.memset(self.ones[:, :], 1.0))
                after(pool.memset(self.mean_w[:, :], 1.0 / C))
                after(pool.memset(self.below[:, :], 1.0))
                after(pool.affine_select(out=self.below[:, :], in_=self.below[:, :], compare_op=ALU.is_gt, fill=0.0,
                                         base=0, pattern=[[1, 128]], channel_multiplier=-1))
                after(pool.memset(self.xT[1][CB:CB + 1, :], 1.0))
                after(pool.memset(self.zeros[:, :], 0.0))
                after(pool.memset(self.eps[:, :], EPS))
                after(pool.memset(self.row_valid[:, :, :], 1.0))
                after(pool.affine_select(out=self.row_valid[:, :, Q3 - 1:Q3], in_=self.row_valid[:, :, Q3 - 1:Q3],
                                         compare_op=ALU.is_ge, fill=0.0, base=ROWS[2] - 1,
                                         pattern=[[0, G], [0, 1]], channel_multiplier=-1))

            @block.vector
            def _(dve):
                dve.wait_ge(made, 5)
                dve.tensor_reduce(self.half_mask[:, :], head[:, :].rearrange("p (r s) -> p s r", s=2), AX.X, ALU.add)

    def embed(self):
        nc, inp, hT = self.nc, self.inp, self.hT
        x_d = inp["x"][:, :, 0:N * PATCH]
        with ExitStack() as ctx:
            sb = lambda name, shape, dt=F32: ctx.enter_context(nc.sbuf_tensor(name, shape, dt))
            sem = lambda name: self.semaphore(ctx, name)
            w_nat = sb("tok_w", [96, 2, CH * PATCH])
            wT = sb("tok_wT", [96, PATCH, C])
            bias = sb("tok_bias", [128, 2])
            xs = [sb(f"x_group{i}", [96, GB, N * PATCH]) for i in range(2)]
            psT = [ctx.enter_context(nc.psum_tensor(f"tok_psT{i}", [128, 512], F32)) for i in range(2)]
            psY = [[ctx.enter_context(nc.psum_tensor(f"tok_y{i}{k}", [128, 512], F32)) for k in range(2)]
                   for i in range(2)]
            w_in, b_in = sem("tok_w_in"), sem("tok_b_in")
            x_in = [sem(f"x_in{i}") for i in range(2)]
            turned, wT_made = sem("tok_turned"), sem("tok_wT_made")
            padded = sem("tok_padded")
            y_done = [sem(f"y_done{i}") for i in range(2)]
            y_kept_act = [sem(f"y_kept_act{i}") for i in range(2)]
            y_kept_dve = [sem(f"y_kept_dve{i}") for i in range(2)]
            block = ctx.enter_context(nc.Block())

            @block.sync
            def _(sp):
                sp.dma_start(w_nat[:, :, :], inp["L0_tok_W"].rearrange("(h e) f -> e h f", h=2)).then_inc(w_in, 16)
                sp.dma_start(bias[0:CA, 0:1], inp["L0_tok_b"][0:CA].rearrange("(e a) -> e a", a=1)).then_inc(b_in, 16)
                sp.dma_start(bias[0:CB, 1:2], inp["L0_tok_b"][CA:C].rearrange("(e a) -> e a", a=1)).then_inc(b_in, 16)
                sp.wait_ge(padded, 3)
                for s in range(2):
                    sp.dma_start(xs[s][0:CH, :, :], x_d[s * GB:(s + 1) * GB].rearrange("b c t -> c b t"))\
                      .then_inc(x_in[s], 16)
                with sp.Fori(0, G // 2 - 1) as i:
                    for s in range(2):
                        sp.wait_ge(y_done[s], i + 1)
                        sp.dma_start(xs[s][0:CH, :, :],
                                     x_d[bass.ds((i * 2 + 2 + s) * GB, GB)].rearrange("b c t -> c b t"))\
                          .then_inc(x_in[s], 16)

            @block.gpsimd
            def _(pool):
                pool.memset(xs[0][64:96, :, :], 0.0).then_inc(padded, 1)
                pool.memset(xs[1][64:96, :, :], 0.0).then_inc(padded, 1)
                pool.memset(wT[64:96, :, :], 0.0).then_inc(padded, 1)

            @block.tensor
            def _(pe):
                pe.wait_ge(w_in, 16)
                for k in range(PATCH // 2):
                    if k >= 2:
                        pe.wait_ge(wT_made, k - 1)
                    for j in range(4):
                        p, half = 2 * k + j // 2, j % 2
                        src = w_nat[:, half, :].rearrange("e (c p) -> e p c", p=PATCH)[:, p, :]
                        mm = pe.transpose(psT[k % 2][0:CH, 96 * j:96 * j + 96], src, self.ident[0:96, 0:96])
                    mm.then_inc(turned, 1)
                pe.wait_ge(wT_made, PATCH // 2)
                with pe.Fori(0, G // 2) as i:
                    for s in range(2):
                        pe.wait_ge(x_in[s], i * 16 + 16)
                        pe.wait_ge(y_kept_act[s], i + 1)
                        pe.wait_ge(y_kept_dve[s], i + 1)
                        for k in range(2):
                            cols, rows = seg(k)
                            for p in range(PATCH):
                                mm = pe.matmul(psY[s][k][0:rows, 0:GT], wT[:, p, cols],
                                               xs[s][:, :, p:N * PATCH:PATCH], start=(p == 0), stop=(p == PATCH - 1))
                        mm.then_inc(y_done[s], 1)

            @block.vector
            def _(dve):
                for k in range(PATCH // 2):
                    dve.wait_ge(turned, k + 1)
                    if k == 0:
                        dve.wait_ge(padded, 3)
                    dve.tensor_copy(wT[0:CH, 2 * k:2 * k + 2, :].rearrange("c p e -> c (p e)"),
                                    psT[k % 2][0:CH, 0:384]).then_inc(wT_made, 1)
                dve.wait_ge(b_in, 32)
                for s in range(2):
                    dve.sem_inc(y_kept_dve[s], 1)
                with dve.Fori(0, G // 2) as i:
                    for s in range(2):
                        dve.wait_ge(y_done[s], i + 1)
                        dve.tensor_scalar(hT[1][0:CB, bass.ds((i * 2 + s) * GT, GT)], psY[s][1][0:CB, 0:GT],
                                          bias[0:CB, 1:2], None, ALU.add).then_inc(y_kept_dve[s], 1)

            @block.scalar
            def _(act):
                act.wait_ge(b_in, 32)
                for s in range(2):
                    act.sem_inc(y_kept_act[s], 1)
                with act.Fori(0, G // 2) as i:
                    for s in range(2):
                        act.wait_ge(y_done[s], i + 1)
                        act.activation(hT[0][:, bass.ds((i * 2 + s) * GT, GT)], psY[s][0][0:CA, 0:GT], ACT.Identity,
                                       bias=bias[0:CA, 0:1]).then_inc(y_kept_act[s], 1)

    def layernorm(self, name):
        nc, hT, xT = self.nc, self.hT, self.xT
        with ExitStack() as ctx:
            sb = lambda n, shape, dt=F32: ctx.enter_context(nc.sbuf_tensor(f"{name}_{n}", shape, dt))
            sem = lambda n: self.semaphore(ctx, f"{name}_{n}")
            cen = [[sb(f"centred{s}{k}", [128, GT]) for k in range(2)] for s in range(2)]
            sq = [[sb(f"square{s}{k}", [128, GT]) for k in range(2)] for s in range(2)]
            dev = [sb(f"dev{s}", [128, GT]) for s in range(2)]
            inv = [sb(f"inv{s}", [128, GT]) for s in range(2)]
            psM = [ctx.enter_context(nc.psum_tensor(f"{name}_mean{s}", [128, 512], F32)) for s in range(2)]
            psV = [ctx.enter_context(nc.psum_tensor(f"{name}_var{s}", [128, 512], F32)) for s in range(2)]
            mean = [sem(f"mean{s}") for s in range(2)]
            centred = [sem(f"centred{s}") for s in range(2)]
            squared = [sem(f"squared{s}") for s in range(2)]
            var = [sem(f"var{s}") for s in range(2)]
            rooted = [sem(f"rooted{s}") for s in range(2)]
            inverted = [sem(f"inverted{s}") for s in range(2)]
            normed = [sem(f"normed{s}") for s in range(2)]
            block = ctx.enter_context(nc.Block())


            @block.tensor
            def _(pe):
                for s in range(2):
                    pe.sem_inc(var[s], 1)
                with pe.Fori(0, G // 2) as i:
                    for s in range(2):
                        pe.wait_ge(centred[s], i * 2 + 2)
                        for k in range(2):
                            mm = pe.matmul(psM[s][0:CA, 0:GT], self.mean_w[0:CA, 0:CA],
                                           hT[k][0:CA, bass.ds((i * 2 + s) * GT, GT)], start=(k == 0), stop=(k == 1))
                        mm.then_inc(mean[s], 1)
                    for s in range(2):
                        pe.wait_ge(squared[s], i * 2 + 4)
                        pe.wait_ge(rooted[s], i + 1)
                        for k in range(2):
                            mm = pe.matmul(psV[s][0:CA, 0:GT], self.mean_w[0:CA, 0:CA], sq[s][k][0:CA, :],
                                           start=(k == 0), stop=(k == 1))
                        mm.then_inc(var[s], 1)

            @block.vector
            def _(dve):
                for s in range(2):
                    dve.sem_inc(centred[s], 2)
                    dve.sem_inc(inverted[s], 1)
                    dve.sem_inc(normed[s], 2)
                with dve.Fori(0, G // 2) as i:
                    for s in range(2):
                        dve.wait_ge(mean[s], i + 1)
                        dve.wait_ge(squared[s], i * 2 + 2)
                        dve.wait_ge(normed[s], i * 2 + 2)
                        for k in range(2):
                            dve.tensor_tensor(cen[s][k][0:CA, :], hT[k][0:CA, bass.ds((i * 2 + s) * GT, GT)],
                                              psM[s][0:CA, 0:GT], ALU.subtract).then_inc(centred[s], 1)
                    for s in range(2):
                        dve.wait_ge(rooted[s], i + 2)
                        dve.reciprocal(inv[s][0:CA, :], dev[s][0:CA, :]).then_inc(inverted[s], 1)
                        dve.wait_ge(inverted[s], i + 2)
                        for k in range(2):
                            dve.tensor_tensor(xT[k][0:CA, bass.ds((i * 2 + s) * GT, GT)], cen[s][k][0:CA, :],
                                              inv[s][0:CA, :], ALU.mult).then_inc(normed[s], 1)

            @block.gpsimd
            def _(pool):
                for s in range(2):
                    pool.sem_inc(squared[s], 2)
                with pool.Fori(0, G // 2) as i:
                    for s in range(2):
                        pool.wait_ge(centred[s], i * 2 + 4)
                        pool.wait_ge(var[s], i + 1)
                        for k in range(2):
                            pool.tensor_tensor(sq[s][k][0:CA, :], cen[s][k][0:CA, :], cen[s][k][0:CA, :],
                                               ALU.mult).then_inc(squared[s], 1)

            @block.scalar
            def _(act):
                for s in range(2):
                    act.sem_inc(rooted[s], 1)
                with act.Fori(0, G // 2) as i:
                    for s in range(2):
                        act.wait_ge(var[s], i + 2)
                        act.wait_ge(inverted[s], i + 1)
                        act.activation(dev[s][0:CA, :], psV[s][0:CA, 0:GT], ACT.Sqrt, bias=self.eps[0:CA, 0:1])\
                           .then_inc(rooted[s], 1)

    def turn_blocks(self, pe, bank, src, cols):
        for j in range(len(src)):
            mm = pe.transpose(bank[0:CA, 96 * j:96 * j + 96], src[j], self.ident[0:96, 0:96])
        return mm

    def attention0(self):
        nc, inp, hT, xT = self.nc, self.inp, self.hT, self.xT
        ROUNDS = 4
        JOBS = 10
        HALF = GB // 2
        with ExitStack() as ctx:
            sb = lambda n, shape, dt=F32: ctx.enter_context(nc.sbuf_tensor(f"a0_{n}", shape, dt))
            ps = lambda n, shape: ctx.enter_context(nc.psum_tensor(f"a0_{n}", shape, F32))
            sem = lambda n: self.semaphore(ctx, f"a0_{n}")
            w_nat = sb("w_nat", [96, 8, C])
            wT = [sb(f"wT{k}", [97, 4, C]) for k in range(2)]
            wmax, gmax = sb("wmax", [96, 2]), sb("gmax", [96, 2])
            lnw, lng = sb("lnw", [96, 2]), sb("lng", [96, 2])
            expo, raw = sb("expo", [96, 2]), sb("raw", [96, 2])
            pow2, above, below = sb("pow2", [96, 2]), sb("above", [96, 2]), sb("below", [96, 2])
            up, scale, inv_scale = sb("up", [96, 2]), sb("scale", [96, 2]), sb("inv_scale", [96, 2])
            xg = sb("xg", [97, 2, GT])
            qT, kT = sb("qT", [96, 2, GT]), sb("kT", [96, 2, GT])
            qm = sb("q_masked", [96, 2, 3, GB, NN])
            v = sb("v", [96, GB, C])
            shifted = [sb(f"shifted{e}", [NN, 2, PAIRS, N]) for e in range(2)]
            top = [sb(f"top{e}", [NN, 2, PAIRS]) for e in range(2)]
            total = [sb(f"total{e}", [NN, 2, PAIRS]) for e in range(2)]
            inv_total = [sb(f"inv_total{e}", [NN, 2, PAIRS]) for e in range(2)]
            pT = [sb(f"pT{e}", [96, 3, NN]) for e in range(2)]
            oT = sb("oT", [97, 2, GT])
            ring = [ps(f"ring{s}", [128, 2, 512]) for s in range(2)]
            psT = [ps(f"turn{e}", [128, 512]) for e in range(2)]
            psO = [ps(f"o{k}", [128, 512]) for k in range(2)]

            w_in, rows_in, w_turned, wT_made = sem("w_in"), sem("rows_in"), sem("w_turned"), sem("wT_made")
            maxed, scale_step, logs, raised2 = sem("maxed"), sem("scale_step"), sem("logs"), sem("raised2")
            zeroed, w_scaled, x_scaled = sem("zeroed"), sem("w_scaled"), sem("x_scaled")
            full = [sem(f"ring_full{s}") for s in range(2)]
            kept = [sem(f"ring_kept{s}") for s in range(2)]
            xg_made, q_masked = sem("xg_made"), sem("q_masked")
            soft = [sem(f"soft_step{e}") for e in range(2)]
            raised = [sem(f"raised{e}") for e in range(2)]
            p_made = [sem(f"p_made{e}") for e in range(2)]
            p_turned = [sem(f"p_turned{k}") for k in range(2)]
            pT_made = [sem(f"pT_made{k}") for k in range(2)]
            pT_used = [sem(f"pT_used{k}") for k in range(2)]
            o_half, o_kept = sem("o_half"), sem("o_kept")
            block = ctx.enter_context(nc.Block())
            TURNED = 3
            QJOB, KJOB, VJOB, SJOB, PJOB = 0, 1, 2, 4, 8
            per = JOBS // 2
            slot_free = lambda i, job: i * per + job // 2 + 1
            job_full = lambda i, job: i * per + job // 2 + 1
            job_kept = lambda i, job: i * per + job // 2 + 2

            @block.sync
            def _(sp):
                sp.dma_start(w_nat[:, 0:6, :], inp["L0_attn_qkv_weight"].rearrange("(r e) c -> e r c", e=96)).then_inc(w_in, 16)
                sp.dma_start(w_nat[:, 6:8, :], inp["L0_attn_proj_weight"].rearrange("(r e) c -> e r c", e=96)).then_inc(w_in, 16)
                sp.dma_start(wT[1][96:97, 0:3, :], inp["L0_attn_qkv_bias"].rearrange("(a r c) -> a r c", a=1, r=3)).then_inc(rows_in, 16)
                sp.dma_start(wT[1][96:97, 3, :], inp["L0_attn_proj_bias"].rearrange("(a c) -> a c", a=1)).then_inc(rows_in, 16)

            @block.gpsimd
            def _(pool):
                pool.memset(v[:, :, :], 0.0).then_inc(zeroed, 1)
                for k in range(2):
                    pool.memset(pT[k][:, :, :], 0.0).then_inc(zeroed, 1)
                pool.wait_ge(zeroed, 3)
                pool.memset(oT[96:97, 1, :], 1.0).then_inc(zeroed, 1)
                pool.memset(xg[96:97, 1, :], 1.0).then_inc(zeroed, 1)
                pool.wait_ge(zeroed, 5)
                for s in range(2):
                    pool.sem_inc(kept[s], 1)
                pool.wait_ge(x_scaled, 2)
                with pool.Fori(0, G) as i:
                    for s in range(2):
                        pool.wait_ge(kept[s], i * per + 1)
                    for k in range(2):
                        pool.tensor_copy(xg[0:CA, k, :], xT[k][0:CA, bass.ds(i * GT, GT)]).then_inc(xg_made, 1)
                    pool.wait_ge(kept[QJOB % 2], job_kept(i, QJOB))
                    for k in range(2):
                        for h in range(PAIRS):
                            pool.tensor_tensor(
                                qm[:, k, h // 2, :, :].rearrange("c b (s n) -> c b s n", s=2)[:, :, h % 2, :],
                                qT[:, k, :].rearrange("c (b n) -> c b n", b=GB),
                                self.head_mask[0:96, h:h + 1].rearrange("c (b n) -> c b n", b=1)
                                    .to_broadcast([96, GB, N]), ALU.mult).then_inc(q_masked, 1)

            @block.tensor
            def _(pe):
                pe.wait_ge(w_in, 32)
                for r in range(ROUNDS):
                    if r >= 2:
                        pe.wait_ge(wT_made, 2 * r - 2)
                    srcs = [w_nat[:, 2 * r + a, CA * k:CA * k + CA] for k in range(2) for a in range(2)]
                    self.turn_blocks(pe, psT[r % 2], srcs, 96).then_inc(w_turned, 1)
                pe.wait_ge(w_scaled, 2)
                pe.wait_ge(x_scaled, 2)
                pe.wait_ge(wT_made, 2 * ROUNDS)
                pe.wait_ge(rows_in, 32)
                pe.wait_ge(zeroed, 5)
                for k in range(2):
                    pe.sem_inc(p_turned[k], TURNED)
                    pe.sem_inc(pT_used[k], 1)
                with pe.Fori(0, G) as i:
                    def project(job, what, blocks):
                        pe.wait_ge(kept[job % 2], slot_free(i, job))
                        for j, m in enumerate(blocks):
                            for k in range(2):
                                r = CA + k
                                rhs = oT[0:r, k, :] if what == 3 else xT[k][0:r, bass.ds(i * GT, GT)]
                                mm = pe.matmul(ring[job % 2][0:CA, j, 0:GT], wT[k][0:r, what, CA * m:CA * m + CA], rhs,
                                               start=(k == 0), stop=(k == 1))
                        mm.then_inc(full[job % 2], 1)

                    project(QJOB, 0, [0, 1])
                    project(KJOB, 1, [0, 1])
                    pe.wait_ge(xg_made, i * 2 + 2)
                    for d in range(2):
                        job = VJOB + d
                        pe.wait_ge(kept[job % 2], slot_free(i, job))
                        for n in range(4):
                            b = 4 * d + n
                            for k in range(2):
                                r = CA + k
                                mm = pe.matmul(ring[job % 2][0:N, n // 2, C * (n % 2):C * (n % 2) + C],
                                               xg[0:r, k, N * b:N * b + N], wT[k][0:r, 2, :],
                                               start=(k == 0), stop=(k == 1))
                        mm.then_inc(full[job % 2], 1)

                    def scores(bb):
                        job = SJOB + bb
                        pe.wait_ge(kept[job % 2], slot_free(i, job))
                        for j in range(2):
                            b = 2 * bb + j
                            for pr in range(PAIRS):
                                mm = pe.matmul(ring[job % 2][0:NN, j, N * pr:N * pr + N], qm[:, pr // 3, pr % 3, b, :],
                                               kT[:, pr // 3, N * b:N * b + N], start=True, stop=True)
                        mm.then_inc(full[job % 2], 1)

                    pe.wait_ge(kept[KJOB % 2], job_kept(i, KJOB))
                    pe.wait_ge(q_masked, i * H + H)
                    for m in range(2):
                        pe.wait_ge(pT_made[m], i * GB + 1)
                    scores(0)
                    scores(1)
                    for b in range(GB):
                        bb = b // 2
                        if b % 2 == 0 and bb + 2 < HALF:
                            pe.wait_ge(p_made[bb % 2], i * 2 + bb // 2 + 1)
                            scores(bb + 2)
                        for k in range(2):
                            for r in range(3):
                                mm = pe.transpose(psT[k][0:N, NN * r:NN * r + NN],
                                                  shifted[bb % 2][:, b % 2, 3 * k + r, :], self.ident[0:NN, 0:NN])
                            mm.then_inc(p_turned[k], 1)
                        if b % 4 == 0:
                            pe.wait_ge(o_kept, i * 4 + b // 2 + 2)
                        if b % 2 == 1 and bb + 1 < HALF and bb + 3 >= HALF:
                            pe.wait_ge(p_made[(bb + 1) % 2], i * 2 + (bb + 1) // 2 + 1)
                        for k in range(2):
                            pe.wait_ge(pT_made[k], i * GB + b + 2)
                            for r in range(3):
                                mm = pe.matmul(psO[k][32 * r:32 * r + 32, NN * (b % 4):NN * (b % 4) + NN],
                                               v[:, b, CA * k + 32 * r:CA * k + 32 * r + 32], pT[k][:, r, :],
                                               start=True, stop=True)
                            mm.then_inc(pT_used[k], 1)
                    pe.wait_ge(o_kept, i * 4 + 6)
                    for m in range(2):
                        project(PJOB + m, 3, [m])

            @block.scalar
            def _(act):
                act.wait_ge(maxed, 2)
                act.activation(lng[:, :], gmax[:, :], ACT.Ln).then_inc(logs, 1)
                act.wait_ge(maxed, 4)
                act.activation(lnw[:, :], wmax[:, :], ACT.Ln).then_inc(logs, 1)
                act.wait_ge(scale_step, 2)
                act.activation(raw[:, :], expo[:, :], ACT.Exp).then_inc(raised2, 1)
                for k in range(2):
                    act.sem_inc(pT_made[k], 1)
                act.wait_ge(zeroed, 5)
                with act.Fori(0, G) as i:
                    act.wait_ge(full[QJOB % 2], job_full(i, QJOB))
                    act.activation(qT[:, :, :], ring[QJOB % 2][0:CA, :, 0:GT], ACT.Copy, scale=HD ** -0.5)\
                       .then_inc(kept[QJOB % 2], 1)
                    for d in range(2):
                        job = VJOB + d
                        act.wait_ge(full[job % 2], job_full(i, job))
                        act.activation(v[0:N, 4 * d:4 * d + 4, :].rearrange("n (j a) c -> n j (a c)", j=2),
                                       ring[job % 2][0:N, :, 0:2 * C], ACT.Copy).then_inc(kept[job % 2], 1)

                    def raise_(bb):
                        act.wait_ge(kept[(SJOB + bb) % 2], job_kept(i, SJOB + bb))
                        act.activation(shifted[bb % 2][:, :, :, :], shifted[bb % 2][:, :, :, :], ACT.Exp)\
                           .then_inc(raised[bb % 2], 1)

                    raise_(0)
                    raise_(1)
                    for b in range(GB):
                        for k in range(2):
                            act.wait_ge(p_turned[k], i * GB + b + 1 + TURNED)
                            act.wait_ge(pT_used[k], i * GB + b + 1)
                            act.activation(pT[k][0:N, :, :].rearrange("n r m -> n (r m)"), psT[k][0:N, 0:3 * NN], ACT.Copy)\
                               .then_inc(pT_made[k], 1)
                        if b % 2 == 0 and b // 2 + 2 < HALF:
                            raise_(b // 2 + 2)

            @block.vector
            def _(dve):
                for k in range(2):
                    dve.tensor_reduce(gmax[:, k:k + 1], xT[k][0:CA, :], AX.X, ALU.max, apply_absolute_value=True)\
                       .then_inc(maxed, 1)
                for r in range(ROUNDS):
                    dve.wait_ge(w_turned, r + 1)
                    for k in range(2):
                        dve.tensor_copy(wT[k][0:CA, r, :], psT[r % 2][0:CA, C * k:C * k + C]).then_inc(wT_made, 1)
                dve.wait_ge(wT_made, 6)
                for k in range(2):
                    dve.tensor_reduce(wmax[:, k:k + 1], wT[k][0:CA, 0:3, :], AX.XY, ALU.max, apply_absolute_value=True)\
                       .then_inc(maxed, 1)
                dve.wait_ge(logs, 2)
                dve.tensor_scalar(expo[:, :], lnw[:, :], -0.65, None, ALU.mult).then_inc(scale_step, 1)
                dve.wait_ge(scale_step, 1)
                dve.scalar_tensor_tensor(out=expo[:, :], in0=lng[:, :], scalar=0.35, in1=expo[:, :], op0=ALU.mult,
                                         op1=ALU.add).then_inc(scale_step, 1)
                dve.wait_ge(raised2, 1)
                dve.tensor_scalar(pow2[:, :].bitcast(I32), raw[:, :].bitcast(I32), 0x7F800000, None, ALU.bitwise_and)\
                   .then_inc(scale_step, 1)
                dve.wait_ge(scale_step, 3)
                dve.tensor_tensor(above[:, :], raw[:, :], pow2[:, :], ALU.subtract).then_inc(scale_step, 1)
                dve.scalar_tensor_tensor(out=below[:, :], in0=pow2[:, :], scalar=2.0, in1=raw[:, :], op0=ALU.mult,
                                         op1=ALU.subtract).then_inc(scale_step, 1)
                dve.wait_ge(scale_step, 5)
                dve.tensor_tensor(up[:, :], above[:, :], below[:, :], ALU.is_gt).then_inc(scale_step, 1)
                dve.wait_ge(scale_step, 6)
                dve.scalar_tensor_tensor(out=scale[:, :], in0=up[:, :], scalar=1.0, in1=pow2[:, :], op0=ALU.add,
                                         op1=ALU.mult).then_inc(scale_step, 1)
                dve.wait_ge(scale_step, 7)
                dve.reciprocal(inv_scale[:, :], scale[:, :]).then_inc(scale_step, 1)
                for k in range(2):
                    dve.tensor_scalar(wT[k][0:CA, 0:3, :], wT[k][0:CA, 0:3, :], scale[:, k:k + 1], None, ALU.mult)\
                       .then_inc(w_scaled, 1)
                dve.wait_ge(scale_step, 8)
                for k in range(2):
                    dve.tensor_scalar(xT[k][0:CA, :], xT[k][0:CA, :], inv_scale[:, k:k + 1], None, ALU.mult)\
                       .then_inc(x_scaled, 1)
                dve.sem_inc(o_kept, 2)
                with dve.Fori(0, G) as i:
                    dve.wait_ge(full[KJOB % 2], job_full(i, KJOB))
                    dve.tensor_copy(kT[:, :, :], ring[KJOB % 2][0:CA, :, 0:GT]).then_inc(kept[KJOB % 2], 1)

                    def shift(bb):
                        e, job, n = bb % 2, SJOB + bb, (i * 2 + bb // 2) * 3
                        src = ring[job % 2][0:NN, :, 0:PAIRS * N].rearrange("m j (p n) -> m j p n", p=PAIRS)
                        dve.wait_ge(full[job % 2], job_full(i, job))
                        dve.wait_ge(p_turned[1], i * GB + 2 * bb + 1)
                        dve.tensor_reduce(top[e][:, :, :], src, AX.X, ALU.max).then_inc(soft[e], 1)
                        dve.wait_ge(soft[e], n + 1)
                        dve.tensor_tensor(shifted[e][:, :, :, :], src,
                                          top[e][:, :, :].rearrange("m j (p a) -> m j p a", a=1).to_broadcast([NN, 2, PAIRS, N]),
                                          ALU.subtract).then_inc(kept[job % 2], 1)

                    def normalise(bb):
                        e, n = bb % 2, (i * 2 + bb // 2) * 3
                        dve.wait_ge(raised[e], i * 2 + bb // 2 + 1)
                        dve.tensor_reduce(total[e][:, :, :], shifted[e][:, :, :, :], AX.X, ALU.add).then_inc(soft[e], 1)
                        dve.wait_ge(soft[e], n + 2)
                        dve.reciprocal(inv_total[e][:, :, :], total[e][:, :, :]).then_inc(soft[e], 1)
                        dve.wait_ge(soft[e], n + 3)
                        dve.tensor_tensor(shifted[e][:, :, :, :], shifted[e][:, :, :, :],
                                          inv_total[e][:, :, :].rearrange("m j (p a) -> m j p a", a=1).to_broadcast([NN, 2, PAIRS, N]),
                                          ALU.mult).then_inc(p_made[e], 1)

                    def keep_outputs(d):
                        for k in range(2):
                            src = psO[k][0:CA, 0:4 * NN].rearrange("c (b s n) -> c b s n", b=4, s=2)
                            dst = oT[0:CA, k, 4 * N * d:4 * N * d + 4 * N].rearrange("c (b n) -> c b n", b=4)
                            dve.wait_ge(pT_used[k], i * GB + 4 * d + 4 + 1)
                            dve.tensor_scalar(dst, src[:, :, 0, :], self.half_mask[0:CA, 0:1], None, ALU.mult)\
                               .then_inc(o_half, 1)
                            dve.wait_ge(o_half, i * 4 + 2 * d + k + 1)
                            dve.scalar_tensor_tensor(out=dst, in0=src[:, :, 1, :], scalar=self.half_mask[0:CA, 1:2],
                                                     in1=dst, op0=ALU.mult, op1=ALU.add).then_inc(o_kept, 1)

                    shift(0)
                    shift(1)
                    normalise(0)
                    shift(2)
                    normalise(1)
                    shift(3)
                    normalise(2)
                    keep_outputs(0)
                    normalise(3)
                    keep_outputs(1)
                    for m in range(2):
                        job = PJOB + m
                        dve.wait_ge(full[job % 2], job_full(i, job))
                        h_at = hT[m][0:CA, bass.ds(i * GT, GT)]
                        dve.tensor_tensor(h_at, h_at, ring[job % 2][0:CA, 0, 0:GT], ALU.add).then_inc(kept[job % 2], 1)


    def attention1(self):
        nc, inp, hT, xT = self.nc, self.inp, self.hT, self.xT
        JOBS = 36
        QJOB, KJOB, VJOB, AJOB = 0, 2, 10, 12
        NC = 22
        W2, B2, W3, B3, W4, B4 = 0, 8, 9, 13, 17, 21
        HB = H // 2
        KR = 96 + HB
        HALF = 4
        with ExitStack() as ctx:
            sb = lambda n, shape, dt=F32: ctx.enter_context(nc.sbuf_tensor(f"a1_{n}", shape, dt))
            ps = lambda n, shape: ctx.enter_context(nc.psum_tensor(f"a1_ps_{n}", shape, F32))
            sem = lambda n: self.semaphore(ctx, f"a1_{n}")
            wT = [sb(f"wT{k}", [97, 2, C]) for k in range(2)]
            kmixT = [sb(f"kmixT{k}", [97, O1, C]) for k in range(2)]
            wide = sb("conv_wide", [NN, PAIRS, NC])
            kmix = sb("kmix", [KR, 2, GB, O1, N])
            qm = sb("q_masked", [KR, 2, 3, GB, NN])
            qT, xg = sb("qT", [96, 2, GT]), sb("xg", [97, 2, GT])
            v, aT = sb("v", [96, GB, C]), sb("aT", [96, GB, NN])
            ring = [ps(f"ring{s}", [128, 2, 512]) for s in range(2)]
            psT = [ps(f"turn{h}", [128, 512]) for h in range(2)]
            psO = ps("o", [128, 2, 512])
            self.attention1_weights(wT, kmixT, wide, kmix, qm, qT, xg, v, aT, ring, psT)

            maps = [sb(f"maps{s}", [NN, GB, O1, N]) for s in range(2)]
            mid = [sb(f"mid{s}", [NN, GB, N]) for s in range(2)]
            fine = [sb(f"fine{s}", [NN, O3, GT]) for s in range(2)]
            amap = [sb(f"amap{s}", [NN, GB, N]) for s in range(2)]
            full = [sem(f"ring_full{s}") for s in range(2)]
            kept = [sem(f"ring_kept{s}") for s in range(2)]
            xg_made, q_masked = sem("xg_made"), sem("q_masked")
            mid_step, mid_made = sem("mid_step"), sem("mid_made")
            fine_made = sem("fine_made")
            amap_step, amap_made = sem("amap_step"), sem("amap_made")
            turned = [sem(f"turned{h}") for h in range(2)]
            aT_made = [sem(f"aT_made{h}") for h in range(2)]
            o_done = [sem(f"o_done{h}") for h in range(2)]
            o_half, o_kept = sem("o_half"), sem("o_kept")
            block = ctx.enter_context(nc.Block())
            per = JOBS // 2
            slot_free = lambda i, job: i * per + job // 2 + 1
            job_full = lambda i, job: i * per + job // 2 + 1
            job_kept = lambda i, job: i * per + job // 2 + 2
            const = lambda p, c: wide[:, p, c:c + 1]

            @block.gpsimd
            def _(pool):
                for s in range(2):
                    pool.sem_inc(kept[s], 1)
                with pool.Fori(0, G) as i:
                    for s in range(2):
                        pool.wait_ge(kept[s], i * per + 1)
                    for k in range(2):
                        pool.tensor_copy(xg[0:CA, k, :], xT[k][0:CA, bass.ds(i * GT, GT)]).then_inc(xg_made, 1)
                    for k in range(2):
                        pool.wait_ge(kept[(QJOB + k) % 2], job_kept(i, QJOB + k))
                        for h in range(HB):
                            pool.tensor_tensor(
                                qm[0:CA, k, h // 2, :, :].rearrange("c b (s n) -> c b s n", s=2)[:, :, h % 2, :],
                                qT[:, k, :].rearrange("c (b n) -> c b n", b=GB),
                                self.head_mask[0:96, h:h + 1].rearrange("c (b n) -> c b n", b=1)
                                    .to_broadcast([96, GB, N]), ALU.mult).then_inc(q_masked, 1)

            @block.tensor
            def _(pe):
                for h in range(2):
                    pe.sem_inc(turned[h], 2)
                    pe.sem_inc(o_done[h], 1)
                with pe.Fori(0, G) as i:
                    x_at = bass.ds(i * GT, GT)
                    for m in range(2):
                        job = QJOB + m
                        pe.wait_ge(kept[job % 2], slot_free(i, job))
                        for k in range(2):
                            r = CA + k
                            mm = pe.matmul(ring[job % 2][0:CA, 0, 0:GT], wT[k][0:r, 0, CA * m:CA * m + CA],
                                           xT[k][0:r, x_at], start=(k == 0), stop=(k == 1))
                        mm.then_inc(full[job % 2], 1)
                    for o in range(O1):
                        job = KJOB + o
                        pe.wait_ge(kept[job % 2], slot_free(i, job))
                        for m in range(2):
                            for k in range(2):
                                r = CA + k
                                mm = pe.matmul(ring[job % 2][0:CA, m, 0:GT], kmixT[k][0:r, o, CA * m:CA * m + CA],
                                               xT[k][0:r, x_at], start=(k == 0), stop=(k == 1))
                        mm.then_inc(full[job % 2], 1)
                    pe.wait_ge(xg_made, i * 2 + 2)
                    for d in range(2):
                        job = VJOB + d
                        pe.wait_ge(kept[job % 2], slot_free(i, job))
                        for n in range(4):
                            b = 4 * d + n
                            for k in range(2):
                                r = CA + k
                                mm = pe.matmul(ring[job % 2][0:N, n // 2, C * (n % 2):C * (n % 2) + C],
                                               xg[0:r, k, N * b:N * b + N], wT[k][0:r, 1, :],
                                               start=(k == 0), stop=(k == 1))
                        mm.then_inc(full[job % 2], 1)

                    def first_maps(p, bb):
                        job = AJOB + 4 * p + bb
                        pe.wait_ge(kept[job % 2], slot_free(i, job))
                        for j in range(2):
                            b = 2 * bb + j
                            mm = pe.matmul(ring[job % 2][0:NN, j, 0:O1 * N], qm[:, p // 3, p % 3, b, :],
                                           kmix[:, p // 3, b, :, :], start=True, stop=True)
                        mm.then_inc(full[job % 2], 1)

                    def turn(p, product_first):
                        for h in range(2):
                            for b in range(4 * h, 4 * h + 4):
                                at = psT[h][0:N, NN * (b % 4):NN * (b % 4) + NN]
                                if product_first and b % 4 == 0:
                                    mm = pe.matmul(at, amap[p % 2][:, b, :], self.ident[0:NN, 0:NN], start=True, stop=True)
                                else:
                                    mm = pe.transpose(at, amap[p % 2][:, b, :], self.ident[0:NN, 0:NN])
                            mm.then_inc(turned[h], 1)

                    def turn_waits(p):
                        pe.wait_ge(amap_made, i * PAIRS + p + 1 + 2)
                        for h in range(2):
                            pe.wait_ge(aT_made[h], i * PAIRS + p + 1)

                    def outputs(p):
                        k, r = p // 3, p % 3
                        if r == 0:
                            pe.wait_ge(o_kept, i * 4 + 2 * k + 2)
                        for h in range(2):
                            pe.wait_ge(aT_made[h], i * PAIRS + p + 2)
                            for b in range(4 * h, 4 * h + 4):
                                mm = pe.matmul(psO[32 * r:32 * r + 32, h, NN * (b % 4):NN * (b % 4) + NN],
                                               v[:, b, 32 * p:32 * p + 32], aT[:, b, :], start=True, stop=True)
                            mm.then_inc(o_done[h], 1)

                    for k in range(2):
                        pe.wait_ge(kept[k], job_kept(i, VJOB + k))
                    pe.wait_ge(q_masked, i * H + H)
                    for p in range(PAIRS):
                        if p >= 2:
                            turn_waits(p - 2)
                        first_maps(p, 0)
                        if p >= 2:
                            turn(p - 2, False)
                        first_maps(p, 1)
                        first_maps(p, 2)
                        if p >= 2:
                            outputs(p - 2)
                        first_maps(p, 3)
                    for p in (PAIRS - 2, PAIRS - 1):
                        turn_waits(p)
                        turn(p, True)
                        outputs(p)

            @block.scalar
            def _(act):
                act.sem_inc(fine_made, 2 * O3)
                with act.Fori(0, G) as i:
                    for m in range(2):
                        job = QJOB + m
                        act.wait_ge(full[job % 2], job_full(i, job))
                        act.activation(qT[:, m, :], ring[job % 2][0:CA, 0, 0:GT], ACT.Copy, scale=C ** -0.5)\
                           .then_inc(kept[job % 2], 1)
                    for o in range(0, O1, 2):
                        job = KJOB + o
                        act.wait_ge(full[job % 2], job_full(i, job))
                        act.activation(kmix[0:CA, :, :, o, :], ring[job % 2][0:CA, :, 0:GT].rearrange("c k (b n) -> c k b n", b=GB),
                                       ACT.Copy).then_inc(kept[job % 2], 1)
                    for d in range(2):
                        job = VJOB + d
                        act.wait_ge(full[job % 2], job_full(i, job))
                        act.activation(v[0:N, 4 * d:4 * d + 4, :].rearrange("n (j a) c -> n j (a c)", j=2),
                                       ring[job % 2][0:N, :, 0:2 * C], ACT.Copy).then_inc(kept[job % 2], 1)

                    def third(p):
                        act.wait_ge(mid_made, i * PAIRS + p + 1 + 2)
                        act.wait_ge(amap_made, i * PAIRS + p + 1)
                        for j in range(O3):
                            act.activation(fine[p % 2][:, j, :], mid[p % 2][:, :, :].rearrange("m b n -> m (b n)"), ACT.Relu,
                                           bias=const(p, B3 + j), scale=const(p, W3 + j)).then_inc(fine_made, 1)

                    for p in range(PAIRS):
                        act.wait_ge(mid_made, i * PAIRS + p + 1)
                        for bb in range(4):
                            job = AJOB + 4 * p + bb
                            act.wait_ge(full[job % 2], job_full(i, job))
                            act.activation(maps[p % 2][:, 2 * bb:2 * bb + 2, :, :].rearrange("m j o n -> m j (o n)"),
                                           ring[job % 2][0:NN, :, 0:O1 * N], ACT.Relu).then_inc(kept[job % 2], 1)
                            if bb == 1 and p >= 1:
                                third(p - 1)
                    third(PAIRS - 1)

            @block.vector
            def _(dve):
                dve.sem_inc(mid_made, 2)
                dve.sem_inc(amap_made, 2)
                dve.sem_inc(o_kept, 2)
                for h in range(2):
                    dve.sem_inc(aT_made[h], 1)
                with dve.Fori(0, G) as i:
                    for o in range(1, O1, 2):
                        job = KJOB + o
                        dve.wait_ge(full[job % 2], job_full(i, job))
                        dve.tensor_copy(kmix[0:CA, :, :, o, :], ring[job % 2][0:CA, :, 0:GT].rearrange("c k (b n) -> c k b n", b=GB))\
                           .then_inc(kept[job % 2], 1)

                    def second(p):
                        m = maps[p % 2]
                        for s in range(2):
                            dve.wait_ge(kept[s], job_kept(i, AJOB + 4 * p + 2 + s))
                        dve.wait_ge(fine_made, (i * PAIRS + p) * O3 + O3)
                        for o in range(O1):
                            n = (i * PAIRS + p) * (O1 - 1) + o
                            if o == 0:
                                ins = dve.tensor_scalar(mid[p % 2][:, :, :], m[:, :, 0, :], const(p, W2), const(p, B2), ALU.mult, ALU.add)
                            else:
                                dve.wait_ge(mid_step, n)
                                ins = dve.scalar_tensor_tensor(out=mid[p % 2][:, :, :], in0=m[:, :, o, :], scalar=const(p, W2 + o),
                                                               in1=mid[p % 2][:, :, :], op0=ALU.mult, op1=ALU.add)
                            ins.then_inc(mid_step if o < O1 - 1 else mid_made, 1)

                    def fourth(p):
                        f = fine[p % 2]
                        out = amap[p % 2][:, :, :].rearrange("m b n -> m (b n)")
                        dve.wait_ge(fine_made, (i * PAIRS + p) * O3 + O3 + 2 * O3)
                        dve.wait_ge(turned[1], i * PAIRS + p + 1)
                        for j in range(O3):
                            n = (i * PAIRS + p) * (O3 - 1) + j
                            if j == 0:
                                ins = dve.tensor_scalar(out, f[:, 0, :], const(p, W4), const(p, B4), ALU.mult, ALU.add)
                            else:
                                dve.wait_ge(amap_step, n)
                                ins = dve.scalar_tensor_tensor(out=out, in0=f[:, j, :], scalar=const(p, W4 + j), in1=out,
                                                               op0=ALU.mult, op1=ALU.add)
                            ins.then_inc(amap_step if j < O3 - 1 else amap_made, 1)

                    def keep_turned(p):
                        for h in range(2):
                            dve.wait_ge(turned[h], i * PAIRS + p + 1 + 2)
                            dve.wait_ge(o_done[h], i * PAIRS + p + 1)
                            dve.tensor_copy(aT[0:N, 4 * h:4 * h + 4, :].rearrange("n b m -> n (b m)"), psT[h][0:N, 0:4 * NN])\
                               .then_inc(aT_made[h], 1)

                    def keep_outputs(k):
                        for h in range(2):
                            src = psO[0:CA, h, 0:4 * NN].rearrange("c (b s n) -> c b s n", b=4, s=2)
                            dst = hT[k][0:CA, bass.ds(i * GT + h * (GT // 2), GT // 2)].rearrange("c (b n) -> c b n", b=4)
                            dve.wait_ge(o_done[h], i * PAIRS + 3 * k + 3 + 1)
                            dve.scalar_tensor_tensor(out=dst, in0=src[:, :, 0, :], scalar=self.half_mask[0:CA, 0:1], in1=dst,
                                                     op0=ALU.mult, op1=ALU.add).then_inc(o_half, 1)
                            dve.wait_ge(o_half, i * 4 + 2 * k + h + 1)
                            dve.scalar_tensor_tensor(out=dst, in0=src[:, :, 1, :], scalar=self.half_mask[0:CA, 1:2], in1=dst,
                                                     op0=ALU.mult, op1=ALU.add).then_inc(o_kept, 1)

                    for p in range(PAIRS):
                        if p == PAIRS - 1:
                            keep_outputs(0)
                        if p >= 2:
                            keep_turned(p - 2)
                        second(p)
                        if p >= 1:
                            fourth(p - 1)
                    keep_turned(PAIRS - 2)
                    fourth(PAIRS - 1)
                    keep_turned(PAIRS - 1)
                    keep_outputs(1)

    def attention1_weights(self, wT, kmixT, wide, kmix, qm, qT, xg, v, aT, ring, psT):
        nc, inp = self.nc, self.inp
        HB, KR = H // 2, 96 + H // 2
        NC = wide.shape[2]
        with ExitStack() as ctx:
            sb = lambda n, shape, dt=F32: ctx.enter_context(nc.sbuf_tensor(f"a1w_{n}", shape, dt))
            sem = lambda n: self.semaphore(ctx, f"a1w_{n}")
            w_nat = sb("w_nat", [96, 4, C])
            wk_nat = sb("wk_nat", [96, 2, C + 1])
            w1_nat = sb("w1_nat", [96, H])
            b1_rows = sb("b1_rows", [KR, 2, O1])
            conv = sb("conv", [2, PAIRS, NC])
            small = sb("small", [HB, 3, 96])
            spread = sb("spread", [96, 2, H, O1])
            diag = sb("diag", [96, HD])
            mixer = sb("mixer", [96, 2, O1, H, HD])
            w_in, rows_in, conv_in, b1_in = sem("w_in"), sem("rows_in"), sem("conv_in"), sem("b1_in")
            zeroed, turned, small_made, spread_done = sem("zeroed"), sem("turned"), sem("small_made"), sem("spread_done")
            wT_made, diag_made, spread_made, mixer_made = sem("wT_made"), sem("diag_made"), sem("spread_made"), sem("mixer_made")
            folded, folded_kept, wide_made, rows_made = sem("folded"), sem("folded_kept"), sem("wide_made"), sem("rows_made")
            block = ctx.enter_context(nc.Block())

            @block.sync
            def _(sp):
                for a, n in enumerate(("q", "v")):
                    sp.dma_start(w_nat[:, 2 * a:2 * a + 2, :], inp[f"L1_attn_w{n}"].rearrange("(r e) c -> e r c", e=96)).then_inc(w_in, 16)
                    sp.dma_start(wT[1][96:97, a, :], inp[f"L1_attn_b{n}"].rearrange("(a c) -> a c", a=1)).then_inc(rows_in, 16)
                sp.dma_start(wk_nat[:, :, 0:C], inp["L1_attn_wk"].rearrange("(r e) c -> e r c", e=96)).then_inc(w_in, 16)
                with nc.allow_non_contiguous_dma(reason="one bias value for each row"):
                    sp.dma_start(wk_nat[:, :, C:C + 1], inp["L1_attn_bk"].rearrange("(r e a) -> e r a", e=96, a=1)).then_inc(w_in, 16)
                    sp.dma_start(w1_nat[:, :], inp["L1_attn_w1"]).then_inc(w_in, 16)
                    sp.dma_start(b1_rows[96:KR, :, :], inp["L1_attn_b1"].rearrange("(k h o) -> h k o", k=2, o=O1)).then_inc(b1_in, 16)
                    at = 0
                    for n, width in (("w2", 8), ("b2", 1), ("w3", 4), ("b3", 4), ("w4", 4), ("b4", 1)):
                        src = inp[f"L1_attn_{n}"]
                        if len(src.shape) == 2:
                            src = src.rearrange("a b -> (a b)")
                        sp.dma_start(conv[:, :, at:at + width], src.rearrange("(r s o) -> s r o", s=2, o=width)).then_inc(conv_in, 16)
                        at += width

            @block.gpsimd
            def _(pool):
                pool.memset(v[:, :, :], 0.0).then_inc(zeroed, 1)
                pool.memset(aT[:, :, :], 0.0).then_inc(zeroed, 1)
                pool.memset(xg[96:97, 1, :], 1.0).then_inc(zeroed, 1)

            @block.tensor
            def _(pe):
                pe.wait_ge(w_in, 16 * 5)
                pe.wait_ge(rows_in, 32)
                for r in range(2):
                    srcs = [w_nat[:, 2 * r + a, CA * k:CA * k + CA] for k in range(2) for a in range(2)]
                    self.turn_blocks(pe, psT[r], srcs, 96).then_inc(turned, 1)
                bank = ring[0]
                pe.transpose(bank[0:HB, 0, 0:96], self.head_mask[0:96, 0:HB], self.ident[0:96, 0:96])
                for k in range(2):
                    mm = pe.transpose(bank[0:HB, 0, 96 + 96 * k:192 + 96 * k], w1_nat[:, HB * k:HB * k + HB], self.ident[0:96, 0:96])
                mm.then_inc(turned, 1)
                pe.wait_ge(small_made, 1)
                for k in range(2):
                    mm = pe.matmul(bank[0:96, 1, 96 * k:96 * k + 96], small[:, 0, :], small[:, 1 + k, :], start=True, stop=True)
                mm.then_inc(spread_done, 1)
                pe.wait_ge(conv_in, 16 * 6)
                pe.matmul(ring[1][0:NN, 0, 0:PAIRS * NC], self.pair_rows[:, :], conv[:, :, :], start=True, stop=True)\
                  .then_inc(spread_done, 1)
                pe.wait_ge(mixer_made, 2 * O1)
                pe.wait_ge(wT_made, 4)
                for o in range(O1):
                    if o >= 2:
                        pe.wait_ge(folded_kept, 2 * (o - 1))
                    for m in range(2):
                        rows = CA + m
                        for k in range(2):
                            mm = pe.matmul(psT[o % 2][0:rows, C * m:C * m + C], wk_nat[:, k, CA * m:CA * m + rows],
                                           mixer[:, k, o, :, :], start=(k == 0), stop=(k == 1))
                    mm.then_inc(folded, 1)

            @block.vector
            def _(dve):
                dve.tensor_reduce(diag[:, :], self.ident[0:96, 0:96].rearrange("p (h d) -> p d h", d=HD), AX.X, ALU.add).then_inc(diag_made, 1)
                for r in range(2):
                    dve.wait_ge(turned, r + 1)
                    for k in range(2):
                        dve.tensor_copy(wT[k][0:CA, r, :], psT[r][0:CA, C * k:C * k + C]).then_inc(wT_made, 1)
                dve.wait_ge(turned, 3)
                dve.tensor_copy(small[:, :, :].rearrange("h a e -> h (a e)"), ring[0][0:HB, 0, 0:288]).then_inc(small_made, 1)
                dve.wait_ge(spread_done, 1)
                dve.tensor_copy(spread[:, :, :, :].rearrange("e k g o -> e (k g o)"), ring[0][0:96, 1, 0:192]).then_inc(spread_made, 1)
                dve.wait_ge(spread_done, 2)
                dve.tensor_copy(wide[:, :, :].rearrange("m p c -> m (p c)"), ring[1][0:NN, 0, 0:PAIRS * NC]).then_inc(wide_made, 1)
                dve.wait_ge(spread_made, 1)
                dve.wait_ge(diag_made, 1)
                for k in range(2):
                    for o in range(O1):
                        ins = dve.tensor_tensor(mixer[:, k, o, :, :], spread[:, k, :, o:o + 1].to_broadcast([96, H, HD]),
                                                diag[:, :].rearrange("p (a d) -> p a d", a=1).to_broadcast([96, H, HD]), ALU.mult)
                        ins.then_inc(mixer_made, 1)
                dve.wait_ge(b1_in, 16)
                for k in range(2):
                    for b in range(GB):
                        dve.tensor_copy(kmix[96:KR, k, b, :, :],
                                        b1_rows[96:KR, k, :].rearrange("h (o n) -> h o n", n=1).to_broadcast([HB, O1, N])).then_inc(rows_made, 1)
                    for h in range(HB):
                        dve.tensor_copy(qm[96:KR, k, h // 2, :, :].rearrange("c b (s n) -> c b s n", s=2)[:, :, h % 2, :],
                                        self.ident[96:KR, 96 + h:97 + h].rearrange("c (b n) -> c b n", b=1).to_broadcast([HB, GB, N]))\
                           .then_inc(rows_made, 1)
                for o in range(O1):
                    dve.wait_ge(folded, o + 1)
                    dve.tensor_copy(kmixT[0][0:CA, o, :], psT[o % 2][0:CA, 0:C]).then_inc(folded_kept, 1)
                    dve.tensor_copy(kmixT[1][0:CA + 1, o, :], psT[o % 2][0:CA + 1, C:2 * C]).then_inc(folded_kept, 1)

    def experts(self, name, gate, tiles, last):
        nc, inp, hT, xT = self.nc, self.inp, self.hT, self.xT
        gate_w, gate_b, centre, w1_d, b1_d, w2_d, b2_d = [None if n is None else inp[n] for n in gate]
        E = gate_w.shape[1]
        TOPK = 2 if last else 1
        func = ACT.Relu if last else ACT.Gelu
        sorted_x = nc.dram_tensor(f"{name}_sorted_x", (tiles * 128, C), F32, kind="Internal").ap()
        sorted_y = nc.dram_tensor(f"{name}_sorted_y", (tiles * 128, C), F32, kind="Internal").ap()
        with ExitStack() as outer:
            sb0 = lambda n, shape, dt=F32: outer.enter_context(nc.sbuf_tensor(f"{name}_{n}", shape, dt))
            w1 = [sb0(f"w1_{k}", [97, E, F]) for k in range(2)]
            w2 = sb0("w2", [128, E, FC, C])
            b2 = sb0("b2", [1, E, C])
            pos = [sb0(f"pos{t}", [128, RT], U32) for t in range(TOPK)]
            weight = [sb0(f"weight{t}", [128, RT]) for t in range(TOPK)]
            expert_of = sb0("expert_of", [128, tiles], I32)
            h_rows = sb0("h_rows", [128, RT, C]) if last else None
            weights_in = self.semaphore(outer, f"{name}_weights_in")
            self.route(name, E, TOPK, tiles, gate_w, gate_b, centre, pos, weight, expert_of, h_rows, sorted_x,
                       (w1, w2, b2, w1_d, b1_d, w2_d, b2_d, weights_in))
            self.run_experts(name, E, tiles, func, w1, w2, b2, expert_of, weights_in, sorted_x, sorted_y)
            self.gather(name, TOPK, pos, weight, h_rows, sorted_y)

    def route(self, name, E, TOPK, tiles, gate_w, gate_b, centre, pos, weight, expert_of, h_rows, sorted_x, loads):
        nc, hT, xT = self.nc, self.hT, self.xT
        w1, w2, b2, w1_d, b1_d, w2_d, b2_d, weights_in = loads
        sources = [xT, hT] if h_rows is not None else [xT]
        S = len(sources)
        with ExitStack() as ctx:
            sb = lambda n, shape, dt=F32: ctx.enter_context(nc.sbuf_tensor(f"{name}_{n}", shape, dt))
            ps = lambda n, shape: ctx.enter_context(nc.psum_tensor(f"{name}_ps_{n}", shape, F32))
            sem = lambda n: self.semaphore(ctx, f"{name}_{n}")
            gw = [sb(f"gate{k}", [97, E]) for k in range(2)]
            centre_row = sb("centre", [97, E])
            staged = [[sb(f"staged{s}_{a}", [97, 2, GT]) for a in range(S)] for s in range(2)]
            x_rows = sb("x_rows", [128, RT, C])
            rows = [x_rows, h_rows]
            score = sb("score", [128, RT, E])
            e_code = sb("e_code", [128, E])
            t_index = sb("t_index", [128, tiles])
            e_int, t_int = sb("e_int", [128, E], I32), sb("t_int", [128, tiles], I32)
            best = [sb(f"best{t}", [128, RT]) for t in range(TOPK)]
            code = sb("code", [128, RT])
            pick = [sb(f"pick{t}", [128, RT, E]) for t in range(TOPK)]
            chosen, work = sb("chosen", [128, RT, E]), sb("work", [128, RT, E])
            sums = [sb(f"sums{a}", [128, RT, E]) for a in range(2)]
            row_of = sb("row_of", [128, RT, E])
            n_tiles_i, n_tiles = sb("n_tiles_i", [128, E], I32), sb("n_tiles", [128, E])
            ends = [sb(f"ends{a}", [128, E]) for a in range(2)]
            starts = sb("starts", [128, E])
            passed, count_of = sb("passed", [128, tiles, E]), sb("count_of", [128, tiles])
            pos_f = sb("pos_f", [128, RT])
            psS = [ps(f"scores{s}", [128, 512]) for s in range(2)]
            psR = [ps(f"rows{s}", [128, 2, 512]) for s in range(2)]
            psP, psC = ps("before", [128, 512]), ps("counts", [128, 512])
            gate_in, centre_in = sem("gate_in"), sem("centre_in")
            zeroed, cleared, iota_made, gate_made = sem("zeroed"), sem("cleared"), sem("iota_made"), sem("gate_made")
            staged_in = [sem(f"staged_in{s}") for s in range(2)]
            turned = [[sem(f"turned{s}_{a}") for a in range(S)] for s in range(2)]
            rows_kept = [sem(f"rows_kept{s}") for s in range(2)]
            score_kept = [sem(f"score_kept{s}") for s in range(2)]
            scored = [sem(f"scored{s}") for s in range(2)]
            step_done, picked, counted = sem("step_done"), sem("picked"), sem("counted")
            exp_needed, exp_made, placed, scattered = sem("exp_needed"), sem("exp_made"), sem("placed"), self.scattered[name]
            block = ctx.enter_context(nc.Block())

            @block.sync
            def _(sp):
                for k in range(2):
                    sp.dma_start(gw[k][0:CA, :], gate_w[CA * k:CA * k + CA, :]).then_inc(gate_in, 16)
                sp.dma_start(gw[1][CA:CA + 1, :], gate_b.rearrange("(a e) -> a e", a=1)).then_inc(gate_in, 16)
                if centre is not None:
                    sp.dma_start(centre_row[CA:CA + 1, :], centre.rearrange("(a e) -> a e", a=1)).then_inc(centre_in, 16)
                sp.dma_start(sorted_x.rearrange("(t p) c -> p t c", p=128),
                             self.zeros[:, :].rearrange("p (t c) -> p t c", t=1).to_broadcast([128, tiles, C])).then_inc(cleared, 16)
                for k in range(2):
                    sp.dma_start(w1[k][0:CA, :, :], w1_d[:, CA * k:CA * k + CA, :].rearrange("e c f -> c e f")).then_inc(weights_in, 16)
                sp.dma_start(w1[1][CA:CA + 1, :, :], b1_d.rearrange("(a e) f -> a e f", a=1)).then_inc(weights_in, 16)
                for e in range(E):
                    sp.dma_start(w2[:, e, :, :], w2_d[e].rearrange("(q p) c -> p q c", p=128)).then_inc(weights_in, 16)
                sp.dma_start(b2[:, :, :], b2_d.rearrange("(a e) c -> a e c", a=1)).then_inc(weights_in, 16)

            @block.gpsimd
            def _(pool):
                pool.iota(e_int[:, :], pattern=[[1, E]], base=-100, channel_multiplier=0).then_inc(iota_made, 1)
                pool.iota(t_int[:, :], pattern=[[1, tiles]], base=0, channel_multiplier=0).then_inc(iota_made, 1)
                pool.memset(score[:, :, :], 0.0).then_inc(zeroed, 1)
                pool.wait_ge(zeroed, 1)
                pool.wait_ge(iota_made, 2)
                for s in range(2):
                    pool.memset(staged[s][0][CA:CA + 1, 1, :], 1.0).then_inc(zeroed, 1)
                pool.wait_ge(zeroed, 3)
                pool.wait_ge(iota_made, 2)
                with pool.Fori(0, G // 2) as i:
                    for s in range(2):
                        pool.wait_ge(scored[s], i + 1)
                        for a in range(S):
                            for k in range(2):
                                pool.tensor_copy(staged[s][a][0:CA, k, :], sources[a][k][0:CA, bass.ds((i * 2 + s) * GT, GT)])\
                                    .then_inc(staged_in[s], 1)
                pool.wait_ge(cleared, 16)
                pool.wait_ge(placed, TOPK)
                for s in range(2):
                    pool.wait_ge(rows_kept[s], S * (G // 2) + S)
                for t in range(TOPK):
                    for j in range(RT):
                        r = ROWS[j % Q3]
                        pool.indirect_dma_start(out=sorted_x, out_offset=bass.IndirectOffsetOnAxis(ap=pos[t][0:r, j:j + 1], axis=0),
                                                in_=x_rows[0:r, j, :], in_offset=None).then_inc(scattered, 16)
                pool.wait_ge(scattered, 16 * TOPK * RT)

            @block.tensor
            def _(pe):
                pe.wait_ge(gate_made, 1)
                pe.wait_ge(zeroed, 3)
                for s in range(2):
                    pe.sem_inc(scored[s], 1)
                with pe.Fori(0, G // 2) as i:
                    for s in range(2):
                        pe.wait_ge(rows_kept[s], i * S + S)
                        pe.wait_ge(score_kept[s], i + 1)
                        pe.wait_ge(staged_in[s], i * 2 * S + 2 * S)
                        for q in range(Q3):
                            for k in range(2):
                                r = CA + k
                                mm = pe.matmul(psS[s][0:ROWS[q], E * q:E * q + E], staged[s][0][0:r, k, 128 * q:128 * q + ROWS[q]],
                                               gw[k][0:r, :], start=(k == 0), stop=(k == 1))
                        for a in range(S):
                            if a == 1:
                                pe.wait_ge(rows_kept[s], i * S + S + 1)
                            for q in range(Q3):
                                for k in range(2):
                                    mm = pe.transpose(psR[s][0:ROWS[q], q // 2, C * (q % 2) + CA * k:C * (q % 2) + CA * k + CA],
                                                      staged[s][a][0:CA, k, 128 * q:128 * q + ROWS[q]], self.ident[0:CA, 0:CA])
                            mm.then_inc(scored[s] if a == S - 1 else turned[s][a], 1)
                pe.wait_ge(picked, 1)
                pe.matmul(psP[:, 0:RT * E], self.below[:, :], chosen[:, :, :], start=True, stop=True)
                pe.matmul(psC[:, 0:RT * E], self.ones[:, :], chosen[:, :, :], start=True, stop=True).then_inc(counted, 1)

            @block.scalar
            def _(act):
                for s in range(2):
                    act.sem_inc(rows_kept[s], S)
                with act.Fori(0, G // 2) as i:
                    for s in range(2):
                        for a in range(S):
                            if a == S - 1:
                                act.wait_ge(scored[s], i + 2)
                            else:
                                act.wait_ge(turned[s][a], i + 1)
                            act.activation(rows[a][:, bass.ds((i * 2 + s) * Q3, 2), :].rearrange("p q c -> p (q c)"),
                                           psR[s][:, 0, 0:2 * C], ACT.Copy)
                            act.activation(rows[a][0:ROWS[2], bass.ds((i * 2 + s) * Q3 + 2, 1), :].rearrange("p q c -> p (q c)"),
                                           psR[s][0:ROWS[2], 1, 0:C], ACT.Copy).then_inc(rows_kept[s], 1)
                if TOPK == 2:
                    act.wait_ge(exp_needed, 1)
                    act.activation(weight[1][:, :], best[1][:, :], ACT.Exp).then_inc(exp_made, 1)

            @block.vector
            def _(dve):
                steps = 0

                def step(ins):
                    nonlocal steps
                    ins.then_inc(step_done, 1)
                    steps += 1
                    dve.wait_ge(step_done, steps)

                over_e = lambda m: m[:, :].rearrange("p (j a) -> p j a", a=1).to_broadcast([128, RT, E])
                over_j = lambda m: m[:, :].rearrange("p (a e) -> p a e", a=1).to_broadcast([128, RT, E])
                dve.wait_ge(gate_in, 48)
                if centre is not None:
                    dve.wait_ge(centre_in, 16)
                    dve.tensor_tensor(gw[1][CA:CA + 1, :], gw[1][CA:CA + 1, :], centre_row[CA:CA + 1, :], ALU.subtract)\
                       .then_inc(gate_made, 1)
                else:
                    dve.sem_inc(gate_made, 1)
                dve.wait_ge(iota_made, 2)
                step(dve.tensor_copy(e_code[:, :], e_int[:, :]))
                step(dve.tensor_copy(t_index[:, :], t_int[:, :]))
                dve.wait_ge(zeroed, 3)
                for s in range(2):
                    dve.sem_inc(score_kept[s], 1)
                with dve.Fori(0, G // 2) as i:
                    for s in range(2):
                        j = (i * 2 + s) * Q3
                        dve.wait_ge(scored[s], i + 2)
                        dve.tensor_copy(score[:, bass.ds(j, 2), :].rearrange("p q e -> p (q e)"), psS[s][:, 0:2 * E])
                        dve.tensor_copy(score[0:ROWS[2], bass.ds(j + 2, 1), :].rearrange("p q e -> p (q e)"),
                                        psS[s][0:ROWS[2], 2 * E:3 * E]).then_inc(score_kept[s], 1)
                for s in range(2):
                    dve.wait_ge(score_kept[s], G // 2 + 1)
                for t in range(TOPK):
                    step(dve.tensor_reduce(best[t][:, :], score[:, :, :], AX.X, ALU.max))
                    step(dve.tensor_tensor(work[:, :, :], score[:, :, :], over_e(best[t]), ALU.is_equal))
                    step(dve.tensor_tensor(work[:, :, :], work[:, :, :], over_j(e_code), ALU.mult))
                    step(dve.tensor_reduce(code[:, :], work[:, :, :], AX.X, ALU.min))
                    step(dve.tensor_tensor(pick[t][:, :, :], over_e(code), over_j(e_code), ALU.is_equal))
                    step(dve.tensor_tensor(pick[t][:, :, :], pick[t][:, :, :],
                                           self.row_valid[:, :, :].rearrange("p g (q a) -> p (g q) a", a=1).to_broadcast([128, RT, E]),
                                           ALU.mult))
                    if t < TOPK - 1:
                        step(dve.scalar_tensor_tensor(out=score[:, :, :], in0=pick[t][:, :, :], scalar=-3.0e38,
                                                      in1=score[:, :, :], op0=ALU.mult, op1=ALU.add))
                if TOPK == 2:
                    step(dve.tensor_tensor(best[1][:, :], best[1][:, :], best[0][:, :], ALU.subtract))
                    dve.sem_inc(exp_needed, 1)
                    dve.wait_ge(exp_made, 1)
                    step(dve.tensor_scalar(best[0][:, :], weight[1][:, :], 1.0, None, ALU.add))
                    step(dve.reciprocal(weight[0][:, :], best[0][:, :]))
                    step(dve.tensor_tensor(weight[1][:, :], weight[1][:, :], weight[0][:, :], ALU.mult))
                    dve.tensor_tensor(chosen[:, :, :], pick[0][:, :, :], pick[1][:, :, :], ALU.add).then_inc(picked, 1)
                else:
                    dve.tensor_copy(chosen[:, :, :], pick[0][:, :, :]).then_inc(picked, 1)
                dve.wait_ge(counted, 1)
                flat = lambda m: m[:, :, :].rearrange("p j e -> p (j e)")
                step(dve.tensor_copy(flat(sums[0]), psC[:, 0:RT * E]))
                src, d = 0, 1
                while d < RT:
                    a, b = sums[src], sums[1 - src]
                    step(dve.tensor_copy(b[:, 0:d, :], a[:, 0:d, :]))
                    step(dve.tensor_tensor(b[:, d:RT, :], a[:, d:RT, :], a[:, 0:RT - d, :], ALU.add))
                    src, d = 1 - src, 2 * d
                total = sums[src]
                step(dve.tensor_scalar(n_tiles_i[:, :], total[:, RT - 1, :], 127.0, None, ALU.add))
                step(dve.tensor_scalar(n_tiles_i[:, :], n_tiles_i[:, :], 7, None, ALU.logical_shift_right))
                step(dve.tensor_copy(n_tiles[:, :], n_tiles_i[:, :]))
                step(dve.tensor_copy(ends[0][:, :], n_tiles[:, :]))
                es, d = 0, 1
                while d < E:
                    a, b = ends[es], ends[1 - es]
                    step(dve.tensor_copy(b[:, 0:d], a[:, 0:d]))
                    step(dve.tensor_tensor(b[:, d:E], a[:, d:E], a[:, 0:E - d], ALU.add))
                    es, d = 1 - es, 2 * d
                end = ends[es]
                step(dve.tensor_tensor(starts[:, :], end[:, :], n_tiles[:, :], ALU.subtract))
                step(dve.tensor_scalar(starts[:, :], starts[:, :], 128.0, None, ALU.mult))
                step(dve.tensor_tensor(flat(row_of), flat(total), psC[:, 0:RT * E], ALU.subtract))
                step(dve.tensor_tensor(flat(row_of), flat(row_of), psP[:, 0:RT * E], ALU.add))
                step(dve.tensor_tensor(row_of[:, :, :], row_of[:, :, :], over_j(starts), ALU.add))
                for t in range(TOPK):
                    step(dve.tensor_tensor(work[:, :, :], row_of[:, :, :], pick[t][:, :, :], ALU.mult))
                    step(dve.tensor_reduce(pos_f[:, :], work[:, :, :], AX.X, ALU.add))
                    dve.tensor_copy(pos[t][:, :], pos_f[:, :]).then_inc(placed, 1)
                    dve.wait_ge(placed, t + 1)
                in_t = [128, tiles, E]
                step(dve.tensor_tensor(passed[:, :, :], t_index[:, :].rearrange("p (t a) -> p t a", a=1).to_broadcast(in_t),
                                       end[:, :].rearrange("p (a e) -> p a e", a=1).to_broadcast(in_t), ALU.is_ge))
                step(dve.tensor_reduce(count_of[:, :], passed[:, :, :], AX.X, ALU.add))
                step(dve.tensor_scalar(expert_of[:, :], count_of[:, :], float(E - 1), None, ALU.min))

    def run_experts(self, name, E, tiles, func, w1, w2, b2, expert_of, weights_in, sorted_x, sorted_y):
        nc = self.nc
        BODY = (tiles - 2) // 2
        with ExitStack() as ctx:
            sb = lambda n, shape, dt=F32: ctx.enter_context(nc.sbuf_tensor(f"{name}_{n}", shape, dt))
            ps = lambda n, shape: ctx.enter_context(nc.psum_tensor(f"{name}_ps_{n}", shape, F32))
            sem = lambda n: self.semaphore(ctx, f"{name}_{n}")
            x_in_buf = [sb(f"x_tile{s}", [128, C]) for s in range(2)]
            xt = [sb(f"xt{s}", [97, 2, 128]) for s in range(2)]
            hid = [sb(f"hid{s}", [128, F]) for s in range(2)]
            hidT = sb("hidT", [128, FC, 128])
            y = [sb(f"y{s}", [128, C]) for s in range(2)]
            psX, psY = ps("x_turned", [128, 2, 256]), ps("y", [128, 2, 256])
            psH = [ps(f"hid{s}", [128, 2, 512]) for s in range(2)]
            psT = ps("hid_turned", [128, 2, 512])
            ones_made = sem("ones_made")
            x_in = [sem(f"x_in{s}") for s in range(2)]
            x_turned = [sem(f"x_turned{s}") for s in range(2)]
            x_kept = [sem(f"x_kept{s}") for s in range(2)]
            h_done = [sem(f"h_done{s}") for s in range(2)]
            h_kept = [sem(f"h_kept{s}") for s in range(2)]
            t_done = [sem(f"t_done{s}") for s in range(2)]
            t_kept = [sem(f"t_kept{s}") for s in range(2)]
            y_done = [sem(f"y_done{s}") for s in range(2)]
            y_kept = [sem(f"y_kept{s}") for s in range(2)]
            y_out = [sem(f"y_out{s}") for s in range(2)]
            block = ctx.enter_context(nc.Block())

            def over_tiles(eng, first, step, fori_to, peeled_to):
                with eng.Fori(0, fori_to) as i:
                    for s in range(2):
                        step(i, s)
                for t in range(2 * fori_to, peeled_to):
                    step(t // 2, t % 2)

            @block.sync
            def _(sp):
                def load(n, s, ahead=0):
                    sp.dma_start(x_in_buf[s][:, :], sorted_x[bass.ds((n * 2 + s + ahead) * 128, 128), :]).then_inc(x_in[s], 16)

                def store(n, s):
                    sp.wait_ge(y_kept[s], n + 2)
                    sp.dma_start(sorted_y[bass.ds((n * 2 + s) * 128, 128), :], y[s][:, :]).then_inc(y_out[s], 16)

                def step(n, s):
                    sp.wait_ge(x_turned[s], n + 1)
                    load(n, s, 2)
                    store(n, s)

                load(0, 0)
                load(0, 1)
                over_tiles(sp, 0, step, BODY, tiles - 2)
                for t in range(tiles - 2, tiles):
                    store(t // 2, t % 2)
                for s in range(2):
                    sp.wait_ge(y_out[s], 16 + 16 * ((tiles + 1 - s) // 2))

            @block.gpsimd
            def _(pool):
                for s in range(2):
                    pool.memset(xt[s][CA:CA + 1, 1, :], 1.0).then_inc(ones_made, 1)

            @block.tensor
            def _(pe):
                def turn_x(n, s):
                    pe.wait_ge(x_in[s], n * 16 + 16)
                    for k in range(2):
                        mm = pe.transpose(psX[0:CA, s, 128 * k:128 * k + 128], x_in_buf[s][:, CA * k:CA * k + CA], self.ident[:, :])
                    mm.then_inc(x_turned[s], 1)

                def expert(n, s):
                    return pe.value_load(expert_of[0:1, bass.ds(n * 2 + s, 1)], min_val=0, max_val=E - 1)

                def first_product(n, s):
                    e = expert(n, s)
                    pe.wait_ge(x_kept[s], n + 1)
                    for half in range(2):
                        for k in range(2):
                            r = CA + k
                            mm = pe.matmul(psH[s][:, half, 0:F // 2], xt[s][0:r, k, :],
                                           w1[k][0:r, :, :].rearrange("c e f -> c (e f)")[:, bass.ds(e * F + half * (F // 2), F // 2)],
                                           start=(k == 0), stop=(k == 1))
                    mm.then_inc(h_done[s], 1)

                def turn_hidden(n, s):
                    pe.wait_ge(h_kept[s], n + 1)
                    for q in range(FC):
                        mm = pe.transpose(psT[:, q // 3, 128 * (q % 3):128 * (q % 3) + 128], hid[s][:, 128 * q:128 * q + 128],
                                          self.ident[:, :])
                    mm.then_inc(t_done[s], 1)

                def second_product(n, s):
                    e = expert(n, s)
                    pe.wait_ge(y_kept[1 - s], n + 1 + s)
                    pe.wait_ge(t_kept[s], n + 1)
                    for q in range(FC):
                        pe.matmul(psY[:, s, 0:C], hidT[:, q, :],
                                  w2[:, :, :, :].rearrange("p e q c -> p (e q c)")[:, bass.ds(e * (FC * C) + q * C, C)],
                                  start=(q == 0), stop=False)
                    pe.matmul(psY[:, s, 0:C], self.ones[0:1, 0:128], b2[:, :, :].rearrange("a e c -> a (e c)")[:, bass.ds(e * C, C)],
                              start=False, stop=True).then_inc(y_done[s], 1)

                pe.wait_ge(weights_in, 16 * (4 + E))
                pe.wait_ge(ones_made, 2)
                turn_x(0, 0)
                pe.wait_ge(x_kept[0], 1)
                turn_x(0, 1)
                first_product(0, 0)

                def step(n, s):
                    first_product(n + s, 1 - s)
                    turn_hidden(n, s)
                    turn_x(n + 1, s)
                    second_product(n, s)

                over_tiles(pe, 0, step, BODY, tiles - 2)
                for t in range(tiles - 2, tiles):
                    n, s = t // 2, t % 2
                    if t + 1 < tiles:
                        first_product(n + s, 1 - s)
                    turn_hidden(n, s)
                    second_product(n, s)

            @block.scalar
            def _(act):
                def step(n, s):
                    act.wait_ge(h_done[s], n + 1)
                    act.activation(hid[s][:, :].rearrange("p (a f) -> p a f", a=2), psH[s][:, :, 0:F // 2], func).then_inc(h_kept[s], 1)

                over_tiles(act, 0, step, tiles // 2, tiles)

            @block.vector
            def _(dve):
                def keep_x(n, s):
                    dve.wait_ge(x_turned[s], n + 1)
                    dve.tensor_copy(xt[s][0:CA, :, :], psX[0:CA, s, :].rearrange("c (k p) -> c k p", k=2)).then_inc(x_kept[s], 1)

                def keep_hidden(n, s):
                    dve.wait_ge(t_done[s], n + 1)
                    dve.tensor_copy(hidT[:, :, :].rearrange("f (a q) p -> f a (q p)", a=2), psT[:, :, 0:384]).then_inc(t_kept[s], 1)

                def keep_y(n, s):
                    dve.wait_ge(y_done[s], n + 1)
                    dve.wait_ge(y_out[s], n * 16 + 16)
                    dve.tensor_copy(y[s][:, :], psY[:, s, 0:C]).then_inc(y_kept[s], 1)

                for s in range(2):
                    dve.sem_inc(y_kept[s], 1)
                    dve.sem_inc(y_out[s], 16)
                keep_x(0, 0)
                keep_x(0, 1)

                def step(n, s):
                    keep_hidden(n, s)
                    keep_x(n + 1, s)
                    keep_y(n, s)

                over_tiles(dve, 0, step, BODY, tiles - 2)
                for t in range(tiles - 2, tiles):
                    keep_hidden(t // 2, t % 2)
                    keep_y(t // 2, t % 2)

    def gather(self, name, TOPK, pos, weight, h_rows, sorted_y):
        nc, hT = self.nc, self.hT
        with ExitStack() as ctx:
            sb = lambda n, shape, dt=F32: ctx.enter_context(nc.sbuf_tensor(f"{name}_{n}", shape, dt))
            sem = lambda n: self.semaphore(ctx, f"{name}_{n}")
            got = [sb(f"got{t}", [128, RT, C]) for t in range(TOPK)]
            psG = [ctx.enter_context(nc.psum_tensor(f"{name}_back{s}", [128, 512], F32)) for s in range(2)]
            back = [sem(f"back{s}") for s in range(2)]
            added = [sem(f"added{s}") for s in range(2)]
            mixed, summed, stored = sem("mixed"), sem("summed"), sem("stored")
            ready = self.gather_ready[name]
            block = ctx.enter_context(nc.Block())
            per_group = 16 * Q3 * TOPK

            @block.gpsimd
            def _(pool):
                for j in range(RT):
                    for t in range(TOPK):
                        r = ROWS[j % Q3]
                        pool.indirect_dma_start(out=got[t][0:r, j, :], out_offset=None, in_=sorted_y,
                                                in_offset=bass.IndirectOffsetOnAxis(ap=pos[t][0:r, j:j + 1], axis=0))\
                            .then_inc(ready[j // Q3], 16)

            if h_rows is None:
                @block.tensor
                def _(pe):
                    for j in range(RT):
                        s, r = j % 2, ROWS[j % Q3]
                        if j % Q3 == 0:
                            pe.wait_ge(ready[j // Q3], per_group)
                        if j >= 2:
                            pe.wait_ge(added[s], 2 * (j // 2))
                        for k in range(2):
                            mm = pe.transpose(psG[s][0:CA, 128 * k:128 * k + r], got[0][0:r, j, CA * k:CA * k + CA],
                                              self.ident[0:r, 0:r])
                        mm.then_inc(back[s], 1)

                @block.vector
                def _(dve):
                    for j in range(RT):
                        s, r = j % 2, ROWS[j % Q3]
                        at = GT * (j // Q3) + 128 * (j % Q3)
                        dve.wait_ge(back[s], j // 2 + 1)
                        for k in range(2):
                            dve.tensor_tensor(hT[k][0:CA, at:at + r], hT[k][0:CA, at:at + r], psG[s][0:CA, 128 * k:128 * k + r],
                                              ALU.add).then_inc(added[s], 1)
            else:
                @block.vector
                def _(dve):
                    for j in range(RT):
                        r = ROWS[j % Q3]
                        if j % Q3 == 0:
                            dve.wait_ge(ready[j // Q3], per_group)
                        dve.scalar_tensor_tensor(out=got[0][0:r, j, :], in0=got[0][0:r, j, :], scalar=weight[0][0:r, j:j + 1],
                                                 in1=h_rows[0:r, j, :], op0=ALU.mult, op1=ALU.add).then_inc(mixed, 1)
                        if j >= 1:
                            finish = j - 1
                            rf = ROWS[finish % Q3]
                            dve.wait_ge(mixed, finish + 1)
                            dve.scalar_tensor_tensor(out=got[1][0:rf, finish, :], in0=got[1][0:rf, finish, :],
                                                     scalar=weight[1][0:rf, finish:finish + 1],
                                                     in1=got[0][0:rf, finish, :], op0=ALU.mult, op1=ALU.add).then_inc(summed, 1)
                    dve.wait_ge(mixed, RT)
                    dve.scalar_tensor_tensor(out=got[1][0:ROWS[2], RT - 1, :], in0=got[1][0:ROWS[2], RT - 1, :],
                                             scalar=weight[1][0:ROWS[2], RT - 1:RT],
                                             in1=got[0][0:ROWS[2], RT - 1, :], op0=ALU.mult, op1=ALU.add).then_inc(summed, 1)

                @block.sync
                def _(sp):
                    rows = self.out.rearrange("b n c -> (b n) c")
                    for g in range(G):
                        sp.wait_ge(summed, Q3 * (g + 1))
                        full = rows[GT * g:GT * g + 256, :].rearrange("(q p) c -> p q c", p=128)
                        sp.dma_start(full, got[1][:, Q3 * g:Q3 * g + 2, :]).then_inc(stored, 16)
                        sp.dma_start(rows[GT * g + 256:GT * g + GT, :], got[1][0:ROWS[2], Q3 * g + 2, :]).then_inc(stored, 16)
                    sp.wait_ge(stored, 32 * G)


def build(nc, inp, out):
    with ExitStack() as ctx:
        t = Tower(nc, inp, out)
        sb = lambda name, shape, dt=F32: ctx.enter_context(nc.sbuf_tensor(name, shape, dt))
        t.scattered, t.gather_ready = {}, {}
        for name in ("ffn0", "ffn1"):
            t.scattered[name] = ctx.enter_context(nc.semaphore(f"{name}_scattered"))
            t.gather_ready[name] = [ctx.enter_context(nc.semaphore(f"{name}_ready{g}")) for g in range(G)]
        t.hT = [sb("hT0", [CA, TOK]), sb("hT1", [CB, TOK])]
        t.xT = [sb("xT0", [CA, TOK]), sb("xT1", [CB + 1, TOK])]
        t.ident = sb("ident", [128, 128])
        t.head_mask = sb("head_mask", [128, 8])
        t.half_mask = sb("half_mask", [128, 2])
        t.pair_rows = sb("pair_rows", [2, NN])
        t.ones = sb("ones", [128, 128])
        t.mean_w = sb("mean_w", [128, 128])
        t.below = sb("below", [128, 128])
        t.zeros = sb("zeros", [128, C])
        t.eps = sb("eps", [128, 1])
        t.row_valid = sb("row_valid", [128, G, Q3])
        t.constants()
        t.embed()
        t.layernorm("norm1")
        t.attention0()
        t.layernorm("norm2")
        t.experts("ffn0", ["L0_ffn_gate_w", "L0_ffn_gate_b", "L0_ffn_gate_center", "L0_ffn_w1", "L0_ffn_b1", "L0_ffn_w2",
                           "L0_ffn_b2"], TILES0, last=False)
        t.layernorm("norm3")
        t.clear_semaphores()
        t.attention1()
        t.layernorm("norm4")
        t.experts("ffn1", ["L1_ffn_Wg", "L1_ffn_bg", None, "L1_ffn_W1", "L1_ffn_b1", "L1_ffn_W2", "L1_ffn_b2"],
                  TILES1, last=True)


_INS = ['x', 'L0_tok_W', 'L0_tok_b', 'L0_attn_qkv_weight', 'L0_attn_qkv_bias', 'L0_attn_proj_weight',
        'L0_attn_proj_bias', 'L0_ffn_gate_w', 'L0_ffn_gate_b', 'L0_ffn_gate_center', 'L0_ffn_w1', 'L0_ffn_b1',
        'L0_ffn_w2', 'L0_ffn_b2', 'L1_attn_wq', 'L1_attn_bq', 'L1_attn_wk', 'L1_attn_bk', 'L1_attn_wv',
        'L1_attn_bv', 'L1_attn_w1', 'L1_attn_b1', 'L1_attn_w2', 'L1_attn_b2', 'L1_attn_w3', 'L1_attn_b3',
        'L1_attn_w4', 'L1_attn_b4', 'L1_ffn_Wg', 'L1_ffn_bg', 'L1_ffn_W1', 'L1_ffn_b1', 'L1_ffn_W2', 'L1_ffn_b2']


def kernel(**inputs):
    import numpy as _np
    import concourse.bacc as _bacc
    from concourse import mybir as _mybir
    from concourse.bass_utils import run_bass_kernel_spmd as _run

    nc = _bacc.Bacc("TRN2", target_bir_lowering=False, num_devices=1)
    arrays, inp = {}, {}
    for name in _INS:
        a = _np.ascontiguousarray(inputs[name])
        arrays[f"in_{name}"] = a
        inp[name] = nc.dram_tensor(f"in_{name}", a.shape, _mybir.dt.from_np(a.dtype), kind="ExternalInput").ap()
    out = nc.dram_tensor("out_0", (B, N, C), F32, kind="ExternalOutput").ap()
    build(nc, inp, out)
    r = _run(nc, [arrays], core_ids=[0])
    return r.results[0]["out_0"]
```

```python
from contextlib import ExitStack

import concourse.bass as bass
from concourse import mybir

F32 = mybir.dt.float32
BF16 = mybir.dt.bfloat16
I32 = mybir.dt.int32
U32 = mybir.dt.uint32
ALU = mybir.AluOpType
ACT = mybir.ActivationFunctionType
AX = mybir.AxisListType

B, CH, T_IN = 64, 90, 750
PATCH, N = 16, 46
C = 192
CA, CB = C // 2, C // 2
TOK = B * N
GB = 8
G = B // GB
GT = GB * N
H, HD = 12, 16
PAIRS = H // 2
PB = PAIRS // 2
NN = 2 * N
F = 768
FC = F // 128
EPS = 1e-5
O1, O3 = 8, 4
Q3 = 3
ROWS = [128, 128, GT - 256]
RT = G * Q3
TILES0 = (TOK + 4 * 127) // 128
TILES1 = (2 * TOK + 8 * 127) // 128


def seg(block):
    return (slice(0, CA), CA) if block == 0 else (slice(CA, C), CB)


class Tower:

    def __init__(self, nc, inp, out):
        self.nc, self.inp, self.out = nc, inp, out
        self.used = []

    def semaphore(self, scope, name):
        handle = scope.enter_context(self.nc.semaphore(name))
        self.used.append(handle)
        return handle

    def clear_semaphores(self):
        with self.nc.Block() as block:
            @block.gpsimd
            def _(pool):
                for handle in self.used:
                    pool.sem_clear(handle)
        self.used = []

    def constants(self):
        nc = self.nc
        with ExitStack() as ctx:
            made = self.semaphore(ctx, "const_made")
            block = ctx.enter_context(nc.Block())
            ident, head, pairsel = self.ident, self.head_mask, self.pair_rows

            @block.gpsimd
            def _(pool):
                steps = 0

                def after(ins):
                    nonlocal steps
                    ins.then_inc(made, 1)
                    steps += 1
                    pool.wait_ge(made, steps)

                after(pool.memset(ident[:, :], 0.0))
                after(pool.affine_select(out=ident[:, :], in_=ident[:, :], compare_op=ALU.not_equal, fill=1.0,
                                         base=0, pattern=[[-1, 128]], channel_multiplier=1))
                after(pool.memset(head[:, :], 1.0))
                after(pool.affine_select(out=head[:, :], in_=head[:, :], compare_op=ALU.is_ge, fill=0.0,
                                         base=0, pattern=[[-HD, 8]], channel_multiplier=1))
                after(pool.affine_select(out=head[:, :], in_=head[:, :], compare_op=ALU.is_ge, fill=0.0,
                                         base=HD - 1, pattern=[[HD, 8]], channel_multiplier=-1))
                after(pool.memset(pairsel[:, :], 1.0))
                after(pool.affine_select(out=pairsel[:, :], in_=pairsel[:, :], compare_op=ALU.is_ge, fill=0.0,
                                         base=0, pattern=[[1, NN]], channel_multiplier=-N))
                after(pool.affine_select(out=pairsel[:, :], in_=pairsel[:, :], compare_op=ALU.is_ge, fill=0.0,
                                         base=N - 1, pattern=[[-1, NN]], channel_multiplier=N))
                after(pool.memset(self.ones[:, :], 1.0))
                after(pool.memset(self.mean_w[:, :], 1.0 / C))
                after(pool.memset(self.below[:, :], 1.0))
                after(pool.affine_select(out=self.below[:, :], in_=self.below[:, :], compare_op=ALU.is_gt, fill=0.0,
                                         base=0, pattern=[[1, 128]], channel_multiplier=-1))
                after(pool.memset(self.xT[1][CB:CB + 1, :], 1.0))
                after(pool.memset(self.zeros[:, :], 0.0))
                after(pool.memset(self.eps[:, :], EPS))
                after(pool.memset(self.row_valid[:, :, :], 1.0))
                after(pool.affine_select(out=self.row_valid[:, :, Q3 - 1:Q3], in_=self.row_valid[:, :, Q3 - 1:Q3],
                                         compare_op=ALU.is_ge, fill=0.0, base=ROWS[2] - 1,
                                         pattern=[[0, G], [0, 1]], channel_multiplier=-1))

            @block.vector
            def _(dve):
                dve.wait_ge(made, 5)
                dve.tensor_reduce(self.half_mask[:, :], head[:, :].rearrange("p (r s) -> p s r", s=2), AX.X, ALU.add)

    def embed(self):
        nc, inp, hT = self.nc, self.inp, self.hT
        x_d = inp["x"][:, :, 0:N * PATCH]
        with ExitStack() as ctx:
            sb = lambda name, shape, dt=F32: ctx.enter_context(nc.sbuf_tensor(name, shape, dt))
            sem = lambda name: self.semaphore(ctx, name)
            w_nat = sb("tok_w", [96, 2, CH * PATCH])
            wT = sb("tok_wT", [96, PATCH, C])
            bias = sb("tok_bias", [128, 2])
            xs = [sb(f"x_group{i}", [96, GB, N * PATCH]) for i in range(2)]
            psT = [ctx.enter_context(nc.psum_tensor(f"tok_psT{i}", [128, 512], F32)) for i in range(2)]
            psY = [[ctx.enter_context(nc.psum_tensor(f"tok_y{i}{k}", [128, 512], F32)) for k in range(2)]
                   for i in range(2)]
            w_in, b_in = sem("tok_w_in"), sem("tok_b_in")
            x_in = [sem(f"x_in{i}") for i in range(2)]
            turned, wT_made = sem("tok_turned"), sem("tok_wT_made")
            padded = sem("tok_padded")
            y_done = [sem(f"y_done{i}") for i in range(2)]
            y_kept_act = [sem(f"y_kept_act{i}") for i in range(2)]
            y_kept_dve = [sem(f"y_kept_dve{i}") for i in range(2)]
            block = ctx.enter_context(nc.Block())

            @block.sync
            def _(sp):
                sp.dma_start(w_nat[:, :, :], inp["L0_tok_W"].rearrange("(h e) f -> e h f", h=2)).then_inc(w_in, 16)
                sp.dma_start(bias[0:CA, 0:1], inp["L0_tok_b"][0:CA].rearrange("(e a) -> e a", a=1)).then_inc(b_in, 16)
                sp.dma_start(bias[0:CB, 1:2], inp["L0_tok_b"][CA:C].rearrange("(e a) -> e a", a=1)).then_inc(b_in, 16)
                sp.wait_ge(padded, 3)
                for s in range(2):
                    sp.dma_start(xs[s][0:CH, :, :], x_d[s * GB:(s + 1) * GB].rearrange("b c t -> c b t"))\
                      .then_inc(x_in[s], 16)
                with sp.Fori(0, G // 2 - 1) as i:
                    for s in range(2):
                        sp.wait_ge(y_done[s], i + 1)
                        sp.dma_start(xs[s][0:CH, :, :],
                                     x_d[bass.ds((i * 2 + 2 + s) * GB, GB)].rearrange("b c t -> c b t"))\
                          .then_inc(x_in[s], 16)

            @block.gpsimd
            def _(pool):
                pool.memset(xs[0][64:96, :, :], 0.0).then_inc(padded, 1)
                pool.memset(xs[1][64:96, :, :], 0.0).then_inc(padded, 1)
                pool.memset(wT[64:96, :, :], 0.0).then_inc(padded, 1)

            @block.tensor
            def _(pe):
                pe.wait_ge(w_in, 16)
                for k in range(PATCH // 2):
                    if k >= 2:
                        pe.wait_ge(wT_made, k - 1)
                    for j in range(4):
                        p, half = 2 * k + j // 2, j % 2
                        src = w_nat[:, half, :].rearrange("e (c p) -> e p c", p=PATCH)[:, p, :]
                        mm = pe.transpose(psT[k % 2][0:CH, 96 * j:96 * j + 96], src, self.ident[0:96, 0:96])
                    mm.then_inc(turned, 1)
                pe.wait_ge(wT_made, PATCH // 2)
                with pe.Fori(0, G // 2) as i:
                    for s in range(2):
                        pe.wait_ge(x_in[s], i * 16 + 16)
                        pe.wait_ge(y_kept_act[s], i + 1)
                        pe.wait_ge(y_kept_dve[s], i + 1)
                        for k in range(2):
                            cols, rows = seg(k)
                            for p in range(PATCH):
                                mm = pe.matmul(psY[s][k][0:rows, 0:GT], wT[:, p, cols],
                                               xs[s][:, :, p:N * PATCH:PATCH], start=(p == 0), stop=(p == PATCH - 1))
                        mm.then_inc(y_done[s], 1)

            @block.vector
            def _(dve):
                for k in range(PATCH // 2):
                    dve.wait_ge(turned, k + 1)
                    if k == 0:
                        dve.wait_ge(padded, 3)
                    dve.tensor_copy(wT[0:CH, 2 * k:2 * k + 2, :].rearrange("c p e -> c (p e)"),
                                    psT[k % 2][0:CH, 0:384]).then_inc(wT_made, 1)
                dve.wait_ge(b_in, 32)
                for s in range(2):
                    dve.sem_inc(y_kept_dve[s], 1)
                with dve.Fori(0, G // 2) as i:
                    for s in range(2):
                        dve.wait_ge(y_done[s], i + 1)
                        dve.tensor_scalar(hT[1][0:CB, bass.ds((i * 2 + s) * GT, GT)], psY[s][1][0:CB, 0:GT],
                                          bias[0:CB, 1:2], None, ALU.add).then_inc(y_kept_dve[s], 1)

            @block.scalar
            def _(act):
                act.wait_ge(b_in, 32)
                for s in range(2):
                    act.sem_inc(y_kept_act[s], 1)
                with act.Fori(0, G // 2) as i:
                    for s in range(2):
                        act.wait_ge(y_done[s], i + 1)
                        act.activation(hT[0][:, bass.ds((i * 2 + s) * GT, GT)], psY[s][0][0:CA, 0:GT], ACT.Identity,
                                       bias=bias[0:CA, 0:1]).then_inc(y_kept_act[s], 1)

    def layernorm(self, name):
        nc, hT, xT = self.nc, self.hT, self.xT
        SLOTS = 4
        TC, TT = GT // 4, 4
        with ExitStack() as ctx:
            sb = lambda n, shape, dt=F32: ctx.enter_context(nc.sbuf_tensor(f"{name}_{n}", shape, dt))
            sem = lambda n: self.semaphore(ctx, f"{name}_{n}")
            cen = [sb(f"centred{s}", [CA, 2, GT]) for s in range(SLOTS)]
            sq = [sb(f"square{s}", [CA, 2, GT]) for s in range(SLOTS)]
            dev = [sb(f"dev{s}", [TC, TT]) for s in range(SLOTS)]
            inv = [sb(f"inv{s}", [TC, TT]) for s in range(SLOTS)]
            diag = [sb(f"diag{s}", [96, TT, TC]) for s in range(SLOTS)]
            psM = [ctx.enter_context(nc.psum_tensor(f"{name}_mean{s}", [128, 512], F32)) for s in range(SLOTS)]
            psV = [ctx.enter_context(nc.psum_tensor(f"{name}_var{s}", [128, 512], F32)) for s in range(SLOTS)]
            zeroed, mean, centred, squared = sem("zeroed"), sem("mean"), sem("centred"), sem("squared")
            var, rooted, inverted, spread, normed = sem("var"), sem("rooted"), sem("inverted"), sem("spread"), sem("normed")
            block = ctx.enter_context(nc.Block())

            def turn(i, s, rounds):
                return (i + rounds) * SLOTS + s

            @block.tensor
            def _(pe):
                pe.sem_inc(spread, SLOTS)
                pe.sem_inc(var, SLOTS)
                with pe.Fori(0, G // SLOTS) as i:
                    for s in range(SLOTS):
                        pe.wait_ge(centred, 2 * turn(i, s, 0) + 2)
                        for k in range(2):
                            mm = pe.matmul(psM[s][0:CA, 0:GT], self.mean_w[0:CA, 0:CA],
                                           hT[k][0:CA, bass.ds((i * SLOTS + s) * GT, GT)], start=(k == 0), stop=(k == 1))
                        mm.then_inc(mean, 1)
                    for s in range(SLOTS):
                        pe.wait_ge(squared, turn(i, s, 1) + 1)
                        pe.wait_ge(normed, 2 * turn(i, s, 0) + 2)
                        for t in range(TT):
                            for k in range(2):
                                mm = pe.matmul(psV[s][0:TC, GT + t:GT + t + 1], sq[s][:, k, TC * t:TC * t + TC],
                                               self.mean_w[0:CA, 0:1], start=(k == 0), stop=(k == 1))
                        mm.then_inc(var, 1)
                    for s in range(SLOTS):
                        pe.wait_ge(inverted, 2 * turn(i, s, 1) + 2)
                        pe.matmul(psV[s][0:CA, 0:GT], self.ones[0:96, 0:CA], diag[s][:, :, :], start=True, stop=True)\
                          .then_inc(spread, 1)

            @block.vector
            def _(dve):
                dve.sem_inc(centred, 2 * SLOTS)
                dve.sem_inc(inverted, 2 * SLOTS)
                dve.sem_inc(normed, 2 * SLOTS)
                dve.wait_ge(zeroed, SLOTS)
                with dve.Fori(0, G // SLOTS) as i:
                    for s in range(SLOTS):
                        dve.wait_ge(mean, turn(i, s, 0) + 1)
                        dve.wait_ge(squared, turn(i, s, 0) + 1)
                        dve.wait_ge(normed, 2 * turn(i, s, 0) + 2)
                        for k in range(2):
                            dve.tensor_tensor(cen[s][:, k, :], hT[k][0:CA, bass.ds((i * SLOTS + s) * GT, GT)],
                                              psM[s][0:CA, 0:GT], ALU.subtract).then_inc(centred, 1)
                    for s in range(SLOTS):
                        dve.wait_ge(rooted, turn(i, s, 1) + 1)
                        dve.reciprocal(inv[s][:, :], dev[s][:, :]).then_inc(inverted, 1)
                        dve.wait_ge(inverted, 2 * turn(i, s, 1) + 1)
                        dve.wait_ge(spread, turn(i, s, 0) + 1)
                        dve.tensor_tensor(diag[s][0:TC, :, :],
                                          self.ident[0:TC, 0:TC].rearrange("p (a t) -> p a t", a=1).to_broadcast([TC, TT, TC]),
                                          inv[s][:, :].rearrange("p (t a) -> p t a", a=1).to_broadcast([TC, TT, TC]),
                                          ALU.mult).then_inc(inverted, 1)
                    for s in range(SLOTS):
                        dve.wait_ge(spread, turn(i, s, 1) + 1)
                        for k in range(2):
                            dve.tensor_tensor(xT[k][0:CA, bass.ds((i * SLOTS + s) * GT, GT)], cen[s][:, k, :],
                                              psV[s][0:CA, 0:GT], ALU.mult).then_inc(normed, 1)

            @block.gpsimd
            def _(pool):
                for s in range(SLOTS):
                    pool.memset(diag[s][64:96, :, :], 0.0).then_inc(zeroed, 1)

            @block.scalar
            def _(act):
                act.sem_inc(squared, SLOTS)
                act.sem_inc(rooted, SLOTS)
                with act.Fori(0, G // SLOTS) as i:
                    for s in range(SLOTS):
                        act.wait_ge(centred, 2 * turn(i, s, 1) + 2)
                        act.wait_ge(var, turn(i, s, 0) + 1)
                        act.activation(sq[s][:, :, :], cen[s][:, :, :], ACT.Square).then_inc(squared, 1)
                    for s in range(SLOTS):
                        act.wait_ge(var, turn(i, s, 1) + 1)
                        act.wait_ge(inverted, 2 * turn(i, s, 0) + 2)
                        act.activation(dev[s][:, :], psV[s][0:TC, GT:GT + TT], ACT.Sqrt, bias=self.eps[0:TC, 0:1])\
                           .then_inc(rooted, 1)

    def turn_blocks(self, pe, bank, src, cols):
        for j in range(len(src)):
            mm = pe.transpose(bank[0:CA, 96 * j:96 * j + 96], src[j], self.ident[0:96, 0:96])
        return mm

    def attention0(self):
        nc, inp, hT, xT = self.nc, self.inp, self.hT, self.xT
        ROUNDS = 4
        JOBS = 10
        HALF = GB // 2
        with ExitStack() as ctx:
            sb = lambda n, shape, dt=F32: ctx.enter_context(nc.sbuf_tensor(f"a0_{n}", shape, dt))
            ps = lambda n, shape: ctx.enter_context(nc.psum_tensor(f"a0_{n}", shape, F32))
            sem = lambda n: self.semaphore(ctx, f"a0_{n}")
            w_nat = sb("w_nat", [96, 8, C])
            wT = [sb(f"wT{k}", [97, 4, C]) for k in range(2)]
            wmax, gmax = sb("wmax", [96, 2]), sb("gmax", [96, 2])
            lnw, lng = sb("lnw", [96, 2]), sb("lng", [96, 2])
            expo, raw = sb("expo", [96, 2]), sb("raw", [96, 2])
            pow2, above, below = sb("pow2", [96, 2]), sb("above", [96, 2]), sb("below", [96, 2])
            up, scale, inv_scale = sb("up", [96, 2]), sb("scale", [96, 2]), sb("inv_scale", [96, 2])
            xg = sb("xg", [97, 2, GT])
            qT, kT = sb("qT", [96, 2, GT]), sb("kT", [96, 2, GT])
            qm = sb("q_masked", [96, 2, 3, GB, NN])
            v = sb("v", [96, GB, C])
            shifted = [sb(f"shifted{e}", [NN, 2, PAIRS, N]) for e in range(2)]
            top = [sb(f"top{e}", [NN, 2, PAIRS]) for e in range(2)]
            total = [sb(f"total{e}", [NN, 2, PAIRS]) for e in range(2)]
            inv_total = [sb(f"inv_total{e}", [NN, 2, PAIRS]) for e in range(2)]
            pT = [[sb(f"pT{k}{e}", [96, 3, NN]) for e in range(2)] for k in range(2)]
            oT = sb("oT", [97, 2, GT])
            ring = [ps(f"ring{s}", [128, 2, 512]) for s in range(2)]
            psT = [ps(f"turn{e}", [128, 512]) for e in range(2)]
            psO = [ps(f"o{k}", [128, 512]) for k in range(2)]

            w_in, rows_in, w_turned, wT_made = sem("w_in"), sem("rows_in"), sem("w_turned"), sem("wT_made")
            maxed, scale_step, logs, raised2 = sem("maxed"), sem("scale_step"), sem("logs"), sem("raised2")
            zeroed, w_scaled, x_scaled = sem("zeroed"), sem("w_scaled"), sem("x_scaled")
            full = [sem(f"ring_full{s}") for s in range(2)]
            kept = [sem(f"ring_kept{s}") for s in range(2)]
            xg_made, k_kept, q_masked = sem("xg_made"), sem("k_kept"), sem("q_masked")
            soft = [sem(f"soft_step{e}") for e in range(2)]
            raised = [sem(f"raised{e}") for e in range(2)]
            p_made = [sem(f"p_made{e}") for e in range(2)]
            p_turned = [sem(f"p_turned{k}") for k in range(2)]
            pT_made = [sem(f"pT_made{k}") for k in range(2)]
            pT_used = [sem(f"pT_used{k}") for k in range(2)]
            o_half, o_kept = sem("o_half"), sem("o_kept")
            block = ctx.enter_context(nc.Block())
            TURNED = 3
            SJOB, QJOB, KJOB, VJOB, NJOB, PJOB = 0, 2, 3, 4, 6, 8
            FIRST = 6
            per = JOBS // 2
            first_job = {QJOB: 0, KJOB: 1, VJOB: 2, VJOB + 1: 3, NJOB: 4, NJOB + 1: 5}

            def place(i, job):
                if isinstance(i, int) and i < 0:
                    return first_job[job] % 2, first_job[job] // 2
                return job % 2, FIRST // 2 + i * per + job // 2

            def score_place(i, bb):
                return place(i - 1, NJOB + bb) if bb < 2 else place(i, SJOB + bb - 2)

            def projection_job(m, more):
                return (PJOB if more else SJOB + 2) + m

            @block.sync
            def _(sp):
                sp.dma_start(w_nat[:, 0:6, :], inp["L0_attn_qkv_weight"].rearrange("(r e) c -> e r c", e=96)).then_inc(w_in, 16)
                sp.dma_start(w_nat[:, 6:8, :], inp["L0_attn_proj_weight"].rearrange("(r e) c -> e r c", e=96)).then_inc(w_in, 16)
                sp.dma_start(wT[1][96:97, 0:3, :], inp["L0_attn_qkv_bias"].rearrange("(a r c) -> a r c", a=1, r=3)).then_inc(rows_in, 16)
                sp.dma_start(wT[1][96:97, 3, :], inp["L0_attn_proj_bias"].rearrange("(a c) -> a c", a=1)).then_inc(rows_in, 16)

            @block.gpsimd
            def _(pool):
                pool.memset(v[:, :, :], 0.0).then_inc(zeroed, 1)
                for k in range(2):
                    for e in range(2):
                        pool.memset(pT[k][e][:, :, :], 0.0).then_inc(zeroed, 1)
                pool.wait_ge(zeroed, 5)
                pool.memset(oT[96:97, 1, :], 1.0).then_inc(zeroed, 1)
                pool.memset(xg[96:97, 1, :], 1.0).then_inc(zeroed, 1)
                pool.wait_ge(zeroed, 7)
                for s in range(2):
                    pool.sem_inc(kept[s], 1)
                pool.wait_ge(x_scaled, 2)
                for k in range(2):
                    pool.tensor_copy(xg[0:CA, k, :], xT[k][0:CA, 0:GT]).then_inc(xg_made, 1)
                for d in range(2):
                    pool.wait_ge(kept[d], place(-1, VJOB + d)[1] + 2)
                for k in range(2):
                    pool.tensor_copy(xg[0:CA, k, :], xT[k][0:CA, GT:2 * GT]).then_inc(xg_made, 1)
                with pool.Fori(0, G - 2) as i:
                    for d in range(2):
                        pool.wait_ge(kept[d], place(i, VJOB + d)[1] + 2)
                    for k in range(2):
                        pool.tensor_copy(xg[0:CA, k, :], xT[k][0:CA, bass.ds((i + 2) * GT, GT)]).then_inc(xg_made, 1)

            @block.tensor
            def _(pe):
                pe.wait_ge(w_in, 32)
                for r in range(ROUNDS):
                    if r >= 2:
                        pe.wait_ge(wT_made, 2 * r - 2)
                    srcs = [w_nat[:, 2 * r + a, CA * k:CA * k + CA] for k in range(2) for a in range(2)]
                    self.turn_blocks(pe, psT[r % 2], srcs, 96).then_inc(w_turned, 1)
                pe.wait_ge(w_scaled, 2)
                pe.wait_ge(x_scaled, 2)
                pe.wait_ge(wT_made, 2 * ROUNDS)
                pe.wait_ge(rows_in, 32)
                pe.wait_ge(zeroed, 7)
                for k in range(2):
                    pe.sem_inc(p_turned[k], TURNED)
                    pe.sem_inc(pT_used[k], 2)
                def project(i, what):
                    s, before = place(i, QJOB + what)
                    pe.wait_ge(kept[s], before + 1)
                    for m in range(2):
                        for k in range(2):
                            r = CA + k
                            mm = pe.matmul(ring[s][0:CA, m, 0:GT], wT[k][0:r, what, CA * m:CA * m + CA],
                                           xT[k][0:r, bass.ds((i + 1) * GT, GT)], start=(k == 0), stop=(k == 1))
                    mm.then_inc(full[s], 1)

                def values(i):
                    pe.wait_ge(xg_made, i * 2 + 4)
                    for d in range(2):
                        s, before = place(i, VJOB + d)
                        pe.wait_ge(kept[s], before + 1)
                        for n in range(4):
                            b = 4 * d + n
                            for k in range(2):
                                r = CA + k
                                mm = pe.matmul(ring[s][0:N, n // 2, C * (n % 2):C * (n % 2) + C],
                                               xg[0:r, k, N * b:N * b + N], wT[k][0:r, 2, :],
                                               start=(k == 0), stop=(k == 1))
                        mm.then_inc(full[s], 1)

                def scores(i, bb):
                    s, before = score_place(i, bb)
                    pe.wait_ge(kept[s], before + 1)
                    for j in range(2):
                        b = 2 * bb + j
                        for pr in range(PAIRS):
                            mm = pe.matmul(ring[s][0:NN, j, N * pr:N * pr + N], qm[:, pr // 3, pr % 3, b, :],
                                           kT[:, pr // 3, N * b:N * b + N], start=True, stop=True)
                    mm.then_inc(full[s], 1)

                def first_scores(i):
                    pe.wait_ge(k_kept, i + 1)
                    pe.wait_ge(q_masked, i * H + H)
                    scores(i, 0)
                    scores(i, 1)

                def turn(b, k):
                    bb = b // 2
                    for r in range(3):
                        mm = pe.transpose(psT[k][0:N, NN * r:NN * r + NN],
                                          shifted[bb % 2][:, b % 2, 3 * k + r, :], self.ident[0:NN, 0:NN])
                    mm.then_inc(p_turned[k], 1)

                def group(i, more):
                    for k in range(2):
                        pe.wait_ge(pT_made[k], i * GB + 1)
                    pe.wait_ge(p_made[0], i * 2 + 1)
                    scores(i, 2)
                    for k in range(2):
                        turn(0, k)
                    scores(i, 3)
                    for b in range(GB):
                        if more and b in (2, 4):
                            project(i, b // 2 - 1)
                        if b % 4 == 0:
                            pe.wait_ge(o_kept, i * 4 + b // 2 + 2)
                        for k in range(2):
                            pe.wait_ge(pT_made[k], i * GB + b + 2)
                            for r in range(3):
                                if b % 2 == 1 and b + 1 < GB and (k, r) == (0, 2):
                                    bb = (b + 1) // 2
                                    pe.wait_ge(p_made[bb % 2], i * 2 + bb // 2 + 1)
                                mm = pe.matmul(psO[k][32 * r:32 * r + 32, NN * (b % 4):NN * (b % 4) + NN],
                                               v[:, b, CA * k + 32 * r:CA * k + 32 * r + 32], pT[k][b % 2][:, r, :],
                                               start=True, stop=True)
                            mm.then_inc(pT_used[k], 1)
                            if b + 1 < GB:
                                turn(b + 1, k)
                    if more:
                        values(i)
                        first_scores(i + 1)
                    pe.wait_ge(o_kept, i * 4 + 6)
                    for m in range(2):
                        s, before = place(i, projection_job(m, more))
                        pe.wait_ge(kept[s], before + 1)
                        for k in range(2):
                            r = CA + k
                            mm = pe.matmul(ring[s][0:CA, 0, 0:GT], wT[k][0:r, 3, CA * m:CA * m + CA], oT[0:r, k, :],
                                           start=(k == 0), stop=(k == 1))
                        mm.then_inc(full[s], 1)

                for what in range(2):
                    project(-1, what)
                values(-1)
                first_scores(0)
                with pe.Fori(0, G - 1) as i:
                    group(i, True)
                group(G - 1, False)

            @block.scalar
            def _(act):
                act.wait_ge(maxed, 2)
                act.activation(lng[:, :], gmax[:, :], ACT.Ln).then_inc(logs, 1)
                act.wait_ge(maxed, 4)
                act.activation(lnw[:, :], wmax[:, :], ACT.Ln).then_inc(logs, 1)
                act.wait_ge(scale_step, 2)
                act.activation(raw[:, :], expo[:, :], ACT.Exp).then_inc(raised2, 1)
                for k in range(2):
                    act.sem_inc(pT_made[k], 1)
                act.wait_ge(zeroed, 7)
                def keep_queries(i):
                    s, before = place(i, QJOB)
                    act.wait_ge(full[s], before + 1)
                    act.activation(qT[:, :, :], ring[s][0:CA, :, 0:GT], ACT.Copy, scale=HD ** -0.5).then_inc(kept[s], 1)

                def keep_values(i):
                    for d in range(2):
                        s, before = place(i, VJOB + d)
                        act.wait_ge(full[s], before + 1)
                        act.activation(v[0:N, 4 * d:4 * d + 4, :].rearrange("n (j a) c -> n j (a c)", j=2),
                                       ring[s][0:N, :, 0:2 * C], ACT.Copy).then_inc(kept[s], 1)

                def raise_(i, bb):
                    s, before = score_place(i, bb)
                    act.wait_ge(kept[s], before + 2)
                    act.activation(shifted[bb % 2][:, :, :, :], shifted[bb % 2][:, :, :, :], ACT.Exp)\
                       .then_inc(raised[bb % 2], 1)

                def group(i, more):
                    for b in range(GB):
                        for k in range(2):
                            act.wait_ge(p_turned[k], i * GB + b + 1 + TURNED)
                            act.wait_ge(pT_used[k], i * GB + b + 1)
                            act.activation(pT[k][b % 2][0:N, :, :].rearrange("n r m -> n (r m)"), psT[k][0:N, 0:3 * NN], ACT.Copy)\
                               .then_inc(pT_made[k], 1)
                        if b == 1:
                            raise_(i, 2)
                        if b == 2 and more:
                            keep_queries(i)
                        if b == 4:
                            raise_(i, 3)
                    if more:
                        keep_values(i)
                        raise_(i + 1, 0)
                        raise_(i + 1, 1)

                keep_queries(-1)
                keep_values(-1)
                raise_(0, 0)
                raise_(0, 1)
                with act.Fori(0, G - 1) as i:
                    group(i, True)
                group(G - 1, False)

            @block.vector
            def _(dve):
                for k in range(2):
                    dve.tensor_reduce(gmax[:, k:k + 1], xT[k][0:CA, :], AX.X, ALU.max, apply_absolute_value=True)\
                       .then_inc(maxed, 1)
                for r in range(ROUNDS):
                    dve.wait_ge(w_turned, r + 1)
                    for k in range(2):
                        dve.tensor_copy(wT[k][0:CA, r, :], psT[r % 2][0:CA, C * k:C * k + C]).then_inc(wT_made, 1)
                dve.wait_ge(wT_made, 6)
                for k in range(2):
                    dve.tensor_reduce(wmax[:, k:k + 1], wT[k][0:CA, 0:3, :], AX.XY, ALU.max, apply_absolute_value=True)\
                       .then_inc(maxed, 1)
                dve.wait_ge(logs, 2)
                dve.tensor_scalar(expo[:, :], lnw[:, :], -0.65, None, ALU.mult).then_inc(scale_step, 1)
                dve.wait_ge(scale_step, 1)
                dve.scalar_tensor_tensor(out=expo[:, :], in0=lng[:, :], scalar=0.35, in1=expo[:, :], op0=ALU.mult,
                                         op1=ALU.add).then_inc(scale_step, 1)
                dve.wait_ge(raised2, 1)
                dve.tensor_scalar(pow2[:, :].bitcast(I32), raw[:, :].bitcast(I32), 0x7F800000, None, ALU.bitwise_and)\
                   .then_inc(scale_step, 1)
                dve.wait_ge(scale_step, 3)
                dve.tensor_tensor(above[:, :], raw[:, :], pow2[:, :], ALU.subtract).then_inc(scale_step, 1)
                dve.scalar_tensor_tensor(out=below[:, :], in0=pow2[:, :], scalar=2.0, in1=raw[:, :], op0=ALU.mult,
                                         op1=ALU.subtract).then_inc(scale_step, 1)
                dve.wait_ge(scale_step, 5)
                dve.tensor_tensor(up[:, :], above[:, :], below[:, :], ALU.is_gt).then_inc(scale_step, 1)
                dve.wait_ge(scale_step, 6)
                dve.scalar_tensor_tensor(out=scale[:, :], in0=up[:, :], scalar=1.0, in1=pow2[:, :], op0=ALU.add,
                                         op1=ALU.mult).then_inc(scale_step, 1)
                dve.wait_ge(scale_step, 7)
                dve.reciprocal(inv_scale[:, :], scale[:, :]).then_inc(scale_step, 1)
                for k in range(2):
                    dve.tensor_scalar(wT[k][0:CA, 0:3, :], wT[k][0:CA, 0:3, :], scale[:, k:k + 1], None, ALU.mult)\
                       .then_inc(w_scaled, 1)
                dve.wait_ge(scale_step, 8)
                for k in range(2):
                    dve.tensor_scalar(xT[k][0:CA, :], xT[k][0:CA, :], inv_scale[:, k:k + 1], None, ALU.mult)\
                       .then_inc(x_scaled, 1)
                dve.sem_inc(o_kept, 2)
                def keep_keys(i):
                    s, before = place(i, KJOB)
                    dve.wait_ge(full[s], before + 1)
                    dve.tensor_copy(kT[:, :, :], ring[s][0:CA, :, 0:GT]).then_inc(kept[s], 1)
                    dve.wait_ge(kept[s], before + 2)
                    dve.sem_inc(k_kept, 1)
                    s, before = place(i, QJOB)
                    dve.wait_ge(kept[s], before + 2)
                    for k in range(2):
                        for h in range(PAIRS):
                            dve.tensor_scalar(
                                qm[:, k, h // 2, :, :].rearrange("c b (s n) -> c b s n", s=2)[:, :, h % 2, :],
                                qT[:, k, :].rearrange("c (b n) -> c b n", b=GB), self.head_mask[0:96, h:h + 1], None,
                                ALU.mult).then_inc(q_masked, 1)

                def shift(i, bb):
                    e, n = bb % 2, (i * 2 + bb // 2) * 3
                    s, before = score_place(i, bb)
                    src = ring[s][0:NN, :, 0:PAIRS * N].rearrange("m j (p n) -> m j p n", p=PAIRS)
                    dve.wait_ge(full[s], before + 1)
                    dve.wait_ge(p_turned[1], i * GB + 2 * bb + 1)
                    dve.tensor_reduce(top[e][:, :, :], src, AX.X, ALU.max).then_inc(soft[e], 1)
                    dve.wait_ge(soft[e], n + 1)
                    dve.tensor_tensor(shifted[e][:, :, :, :], src,
                                      top[e][:, :, :].rearrange("m j (p a) -> m j p a", a=1).to_broadcast([NN, 2, PAIRS, N]),
                                      ALU.subtract).then_inc(kept[s], 1)

                def normalise(i, bb):
                    e, n = bb % 2, (i * 2 + bb // 2) * 3
                    dve.wait_ge(raised[e], i * 2 + bb // 2 + 1)
                    dve.tensor_reduce(total[e][:, :, :], shifted[e][:, :, :, :], AX.X, ALU.add).then_inc(soft[e], 1)
                    dve.wait_ge(soft[e], n + 2)
                    dve.reciprocal(inv_total[e][:, :, :], total[e][:, :, :]).then_inc(soft[e], 1)
                    dve.wait_ge(soft[e], n + 3)
                    dve.tensor_tensor(shifted[e][:, :, :, :], shifted[e][:, :, :, :],
                                      inv_total[e][:, :, :].rearrange("m j (p a) -> m j p a", a=1).to_broadcast([NN, 2, PAIRS, N]),
                                      ALU.mult).then_inc(p_made[e], 1)

                def keep_outputs(i, d):
                    for k in range(2):
                        src = psO[k][0:CA, 0:4 * NN].rearrange("c (b s n) -> c b s n", b=4, s=2)
                        dst = oT[0:CA, k, 4 * N * d:4 * N * d + 4 * N].rearrange("c (b n) -> c b n", b=4)
                        dve.wait_ge(pT_used[k], i * GB + 4 * d + 4 + 2)
                        dve.tensor_scalar(dst, src[:, :, 0, :], self.half_mask[0:CA, 0:1], None, ALU.mult)\
                           .then_inc(o_half, 1)
                        dve.wait_ge(o_half, i * 4 + 2 * d + k + 1)
                        dve.scalar_tensor_tensor(out=dst, in0=src[:, :, 1, :], scalar=self.half_mask[0:CA, 1:2],
                                                 in1=dst, op0=ALU.mult, op1=ALU.add).then_inc(o_kept, 1)

                def group(i, more):
                    normalise(i, 1)
                    shift(i, 2)
                    normalise(i, 2)
                    shift(i, 3)
                    keep_outputs(i, 0)
                    normalise(i, 3)
                    if more:
                        keep_keys(i)
                    keep_outputs(i, 1)
                    if more:
                        shift(i + 1, 0)
                        shift(i + 1, 1)
                        normalise(i + 1, 0)
                    for m in range(2):
                        s, before = place(i, projection_job(m, more))
                        dve.wait_ge(full[s], before + 1)
                        h_at = hT[m][0:CA, bass.ds(i * GT, GT)]
                        dve.tensor_tensor(h_at, h_at, ring[s][0:CA, 0, 0:GT], ALU.add).then_inc(kept[s], 1)

                keep_keys(-1)
                shift(0, 0)
                shift(0, 1)
                normalise(0, 0)
                with dve.Fori(0, G - 1) as i:
                    group(i, True)
                group(G - 1, False)

    def attention1(self):
        nc, inp, hT, xT = self.nc, self.inp, self.hT, self.xT
        JOBS = 36
        QJOB, KJOB, VJOB, AJOB = 0, 2, 10, 12
        NC = 22
        W2, B2, W3, B3, W4, B4 = 0, 8, 9, 13, 17, 21
        HB = H // 2
        KR = 96 + HB
        HALF = 4
        LAG = 3
        with ExitStack() as ctx:
            sb = lambda n, shape, dt=F32: ctx.enter_context(nc.sbuf_tensor(f"a1_{n}", shape, dt))
            ps = lambda n, shape: ctx.enter_context(nc.psum_tensor(f"a1_ps_{n}", shape, F32))
            sem = lambda n: self.semaphore(ctx, f"a1_{n}")
            wT = [sb(f"wT{k}", [97, 2, C]) for k in range(2)]
            kmixT = [sb(f"kmixT{k}", [97, O1, C]) for k in range(2)]
            wide = sb("conv_wide", [NN, PAIRS, NC])
            kmix = sb("kmix", [KR, 2, GB, O1, N])
            qm = sb("q_masked", [KR, 2, 3, GB, NN])
            qT, xg = sb("qT", [96, 2, GT]), sb("xg", [97, 2, GT])
            v, aT = sb("v", [96, GB, C]), sb("aT", [96, GB, NN])
            ring = [ps(f"ring{s}", [128, 2, 512]) for s in range(2)]
            psT = [ps(f"turn{h}", [128, 512]) for h in range(2)]
            psO = ps("o", [128, 2, 512])
            self.attention1_weights(wT, kmixT, wide, kmix, qm, qT, xg, v, aT, ring, psT)

            maps = [sb(f"maps{s}", [NN, GB, O1, N]) for s in range(2)]
            mid = [sb(f"mid{s}", [NN, GB, N]) for s in range(2)]
            fine = [sb(f"fine{s}", [NN, O3, GT]) for s in range(2)]
            amap = [sb(f"amap{s}", [NN, GB, N]) for s in range(2)]
            full = [sem(f"ring_full{s}") for s in range(2)]
            kept = [sem(f"ring_kept{s}") for s in range(2)]
            xg_made, q_masked = sem("xg_made"), sem("q_masked")
            mid_step, mid_made = sem("mid_step"), sem("mid_made")
            fine_made = sem("fine_made")
            amap_step, amap_made = sem("amap_step"), sem("amap_made")
            turned = [sem(f"turned{h}") for h in range(2)]
            aT_made = [sem(f"aT_made{h}") for h in range(2)]
            o_done = [sem(f"o_done{h}") for h in range(2)]
            o_half, o_kept = sem("o_half"), sem("o_kept")
            block = ctx.enter_context(nc.Block())
            per = JOBS // 2
            slot_free = lambda i, job: i * per + job // 2 + 1
            job_full = lambda i, job: i * per + job // 2 + 1
            job_kept = lambda i, job: i * per + job // 2 + 2
            const = lambda p, c: wide[:, p, c:c + 1]

            @block.gpsimd
            def _(pool):
                for s in range(2):
                    pool.sem_inc(kept[s], 1)
                for k in range(2):
                    pool.tensor_copy(xg[0:CA, k, :], xT[k][0:CA, 0:GT]).then_inc(xg_made, 1)
                with pool.Fori(0, G - 1) as i:
                    for s in range(2):
                        pool.wait_ge(kept[s], job_kept(i, VJOB + s))
                    for k in range(2):
                        pool.tensor_copy(xg[0:CA, k, :], xT[k][0:CA, bass.ds((i + 1) * GT, GT)]).then_inc(xg_made, 1)

            @block.tensor
            def _(pe):
                for h in range(2):
                    pe.sem_inc(turned[h], 2)
                    pe.sem_inc(o_done[h], 1)
                def queries(i):
                    for m in range(2):
                        job = QJOB + m
                        pe.wait_ge(kept[job % 2], slot_free(i, job))
                        for k in range(2):
                            r = CA + k
                            mm = pe.matmul(ring[job % 2][0:CA, 0, 0:GT], wT[k][0:r, 0, CA * m:CA * m + CA],
                                           xT[k][0:r, bass.ds(i * GT, GT)], start=(k == 0), stop=(k == 1))
                        mm.then_inc(full[job % 2], 1)

                def mixed_keys(i, o):
                    job = KJOB + o
                    pe.wait_ge(kept[job % 2], slot_free(i, job))
                    for m in range(2):
                        for k in range(2):
                            r = CA + k
                            mm = pe.matmul(ring[job % 2][0:CA, m, 0:GT], kmixT[k][0:r, o, CA * m:CA * m + CA],
                                           xT[k][0:r, bass.ds(i * GT, GT)], start=(k == 0), stop=(k == 1))
                    mm.then_inc(full[job % 2], 1)

                def values(i):
                    pe.wait_ge(xg_made, i * 2 + 2)
                    for d in range(2):
                        job = VJOB + d
                        pe.wait_ge(kept[job % 2], slot_free(i, job))
                        for n in range(4):
                            b = 4 * d + n
                            for k in range(2):
                                r = CA + k
                                mm = pe.matmul(ring[job % 2][0:N, n // 2, C * (n % 2):C * (n % 2) + C],
                                               xg[0:r, k, N * b:N * b + N], wT[k][0:r, 1, :],
                                               start=(k == 0), stop=(k == 1))
                        mm.then_inc(full[job % 2], 1)

                def first_maps(i, p, bb):
                    job = AJOB + 4 * p + bb
                    pe.wait_ge(kept[job % 2], slot_free(i, job))
                    for j in range(2):
                        b = 2 * bb + j
                        mm = pe.matmul(ring[job % 2][0:NN, j, 0:O1 * N], qm[:, p // 3, p % 3, b, :],
                                       kmix[:, p // 3, b, :, :], start=True, stop=True)
                    mm.then_inc(full[job % 2], 1)

                def turn_waits(i, p):
                    pe.wait_ge(amap_made, i * PAIRS + p + 1 + 2)
                    for h in range(2):
                        pe.wait_ge(aT_made[h], i * PAIRS + p + 1)

                def turn(p):
                    for h in range(2):
                        for b in range(4 * h, 4 * h + 4):
                            mm = pe.transpose(psT[h][0:N, NN * (b % 4):NN * (b % 4) + NN], amap[p % 2][:, b, :],
                                              self.ident[0:NN, 0:NN])
                        mm.then_inc(turned[h], 1)

                def outputs(i, p):
                    k, r = p // 3, p % 3
                    if r == 0:
                        pe.wait_ge(o_kept, i * 4 + 2 * k + 2)
                    for h in range(2):
                        pe.wait_ge(aT_made[h], i * PAIRS + p + 2)
                        for b in range(4 * h, 4 * h + 4):
                            mm = pe.matmul(psO[32 * r:32 * r + 32, h, NN * (b % 4):NN * (b % 4) + NN],
                                           v[:, b, 32 * p:32 * p + 32], aT[:, b, :], start=True, stop=True)
                        mm.then_inc(o_done[h], 1)

                def maps_of_group(i):
                    for k in range(2):
                        pe.wait_ge(kept[k], job_kept(i, VJOB + k))
                    pe.wait_ge(q_masked, i * H + H)
                    for p in range(PAIRS):
                        if p >= LAG:
                            turn_waits(i, p - LAG)
                        first_maps(i, p, 0)
                        if p >= LAG:
                            turn(p - LAG)
                        for bb in range(1, 4):
                            first_maps(i, p, bb)
                        if p >= LAG:
                            outputs(i, p - LAG)

                queries(0)
                for o in range(O1):
                    mixed_keys(0, o)
                values(0)
                with pe.Fori(0, G - 1) as i:
                    maps_of_group(i)
                    queries(i + 1)
                    turn_after = {1: PAIRS - 3, 4: PAIRS - 2, 7: PAIRS - 1}
                    outputs_after = {3: PAIRS - 3, 6: PAIRS - 2}
                    for o in range(O1):
                        if o in turn_after:
                            turn_waits(i, turn_after[o])
                        mixed_keys(i + 1, o)
                        if o in turn_after:
                            turn(turn_after[o])
                        if o in outputs_after:
                            outputs(i, outputs_after[o])
                    outputs(i, PAIRS - 1)
                    values(i + 1)
                maps_of_group(G - 1)
                for p in range(PAIRS - LAG, PAIRS):
                    turn_waits(G - 1, p)
                    turn(p)
                    outputs(G - 1, p)

            @block.scalar
            def _(act):
                act.sem_inc(fine_made, 2 * O3)
                def keep_queries(i):
                    for m in range(2):
                        job = QJOB + m
                        act.wait_ge(full[job % 2], job_full(i, job))
                        act.activation(qT[:, m, :], ring[job % 2][0:CA, 0, 0:GT], ACT.Copy, scale=C ** -0.5)\
                           .then_inc(kept[job % 2], 1)

                def keep_keys(i, o):
                    job = KJOB + o
                    act.wait_ge(full[job % 2], job_full(i, job))
                    act.activation(kmix[0:CA, :, :, o, :], ring[job % 2][0:CA, :, 0:GT].rearrange("c k (b n) -> c k b n", b=GB),
                                   ACT.Copy).then_inc(kept[job % 2], 1)

                def keep_values(i):
                    for d in range(2):
                        job = VJOB + d
                        act.wait_ge(full[job % 2], job_full(i, job))
                        act.activation(v[0:N, 4 * d:4 * d + 4, :].rearrange("n (j a) c -> n j (a c)", j=2),
                                       ring[job % 2][0:N, :, 0:2 * C], ACT.Copy).then_inc(kept[job % 2], 1)

                def third(i, p):
                    act.wait_ge(mid_made, i * PAIRS + p + 1 + 2)
                    act.wait_ge(amap_made, i * PAIRS + p + 1)
                    for j in range(O3):
                        act.activation(fine[p % 2][:, j, :], mid[p % 2][:, :, :].rearrange("m b n -> m (b n)"), ACT.Relu,
                                       bias=const(p, B3 + j), scale=const(p, W3 + j)).then_inc(fine_made, 1)

                def first_and_third(i):
                    for p in range(PAIRS):
                        act.wait_ge(mid_made, i * PAIRS + p + 1)
                        for bb in range(4):
                            job = AJOB + 4 * p + bb
                            act.wait_ge(full[job % 2], job_full(i, job))
                            act.activation(maps[p % 2][:, 2 * bb:2 * bb + 2, :, :].rearrange("m j o n -> m j (o n)"),
                                           ring[job % 2][0:NN, :, 0:O1 * N], ACT.Relu).then_inc(kept[job % 2], 1)
                        if p >= 1:
                            third(i, p - 1)

                keep_queries(0)
                for o in range(O1):
                    keep_keys(0, o)
                keep_values(0)
                with act.Fori(0, G - 1) as i:
                    first_and_third(i)
                    keep_queries(i + 1)
                    for o in range(O1):
                        if o == 2:
                            third(i, PAIRS - 1)
                        keep_keys(i + 1, o)
                    keep_values(i + 1)
                first_and_third(G - 1)
                third(G - 1, PAIRS - 1)

            @block.vector
            def _(dve):
                dve.sem_inc(mid_made, 2)
                dve.sem_inc(amap_made, 2)
                dve.sem_inc(o_kept, 2)
                for h in range(2):
                    dve.sem_inc(aT_made[h], 1)
                def mask_queries(i):
                    for k in range(2):
                        dve.wait_ge(kept[(QJOB + k) % 2], job_kept(i, QJOB + k))
                        for h in range(HB):
                            dve.tensor_scalar(
                                qm[0:CA, k, h // 2, :, :].rearrange("c b (s n) -> c b s n", s=2)[:, :, h % 2, :],
                                qT[:, k, :].rearrange("c (b n) -> c b n", b=GB), self.head_mask[0:96, h:h + 1], None,
                                ALU.mult).then_inc(q_masked, 1)

                def second(i, p):
                    m = maps[p % 2]
                    for s in range(2):
                        dve.wait_ge(kept[s], job_kept(i, AJOB + 4 * p + 2 + s))
                    dve.wait_ge(fine_made, (i * PAIRS + p) * O3 + O3)
                    for o in range(O1):
                        n = (i * PAIRS + p) * (O1 - 1) + o
                        if o == 0:
                            ins = dve.tensor_scalar(mid[p % 2][:, :, :], m[:, :, 0, :], const(p, W2), const(p, B2), ALU.mult, ALU.add)
                        else:
                            dve.wait_ge(mid_step, n)
                            ins = dve.scalar_tensor_tensor(out=mid[p % 2][:, :, :], in0=m[:, :, o, :], scalar=const(p, W2 + o),
                                                           in1=mid[p % 2][:, :, :], op0=ALU.mult, op1=ALU.add)
                        ins.then_inc(mid_step if o < O1 - 1 else mid_made, 1)

                def fourth(i, p):
                    f = fine[p % 2]
                    out = amap[p % 2][:, :, :].rearrange("m b n -> m (b n)")
                    dve.wait_ge(fine_made, (i * PAIRS + p) * O3 + O3 + 2 * O3)
                    dve.wait_ge(turned[1], i * PAIRS + p + 1)
                    for j in range(O3):
                        n = (i * PAIRS + p) * (O3 - 1) + j
                        if j == 0:
                            ins = dve.tensor_scalar(out, f[:, 0, :], const(p, W4), const(p, B4), ALU.mult, ALU.add)
                        else:
                            dve.wait_ge(amap_step, n)
                            ins = dve.scalar_tensor_tensor(out=out, in0=f[:, j, :], scalar=const(p, W4 + j), in1=out,
                                                           op0=ALU.mult, op1=ALU.add)
                        ins.then_inc(amap_step if j < O3 - 1 else amap_made, 1)

                def keep_turned(i, p):
                    for h in range(2):
                        dve.wait_ge(turned[h], i * PAIRS + p + 1 + 2)
                        dve.wait_ge(o_done[h], i * PAIRS + p + 1)
                        dve.tensor_copy(aT[0:N, 4 * h:4 * h + 4, :].rearrange("n b m -> n (b m)"), psT[h][0:N, 0:4 * NN])\
                           .then_inc(aT_made[h], 1)

                def keep_outputs(i, k):
                    for h in range(2):
                        src = psO[0:CA, h, 0:4 * NN].rearrange("c (b s n) -> c b s n", b=4, s=2)
                        dst = hT[k][0:CA, bass.ds(i * GT + h * (GT // 2), GT // 2)].rearrange("c (b n) -> c b n", b=4)
                        dve.wait_ge(o_done[h], i * PAIRS + 3 * k + 3 + 1)
                        dve.scalar_tensor_tensor(out=dst, in0=src[:, :, 0, :], scalar=self.half_mask[0:CA, 0:1], in1=dst,
                                                 op0=ALU.mult, op1=ALU.add).then_inc(o_half, 1)
                        dve.wait_ge(o_half, i * 4 + 2 * k + h + 1)
                        dve.scalar_tensor_tensor(out=dst, in0=src[:, :, 1, :], scalar=self.half_mask[0:CA, 1:2], in1=dst,
                                                 op0=ALU.mult, op1=ALU.add).then_inc(o_kept, 1)

                def second_and_fourth(i):
                    for p in range(PAIRS):
                        second(i, p)
                        if p == PAIRS - 1:
                            keep_outputs(i, 0)
                        if p >= 2:
                            keep_turned(i, p - 2)
                        if p >= 1:
                            fourth(i, p - 1)

                def finish(i):
                    fourth(i, PAIRS - 1)
                    keep_turned(i, PAIRS - 1)
                    keep_outputs(i, 1)

                mask_queries(0)
                with dve.Fori(0, G - 1) as i:
                    second_and_fourth(i)
                    mask_queries(i + 1)
                    keep_turned(i, PAIRS - 2)
                    finish(i)
                second_and_fourth(G - 1)
                keep_turned(G - 1, PAIRS - 2)
                finish(G - 1)

    def attention1_weights(self, wT, kmixT, wide, kmix, qm, qT, xg, v, aT, ring, psT):
        nc, inp = self.nc, self.inp
        HB, KR = H // 2, 96 + H // 2
        NC = wide.shape[2]
        with ExitStack() as ctx:
            sb = lambda n, shape, dt=F32: ctx.enter_context(nc.sbuf_tensor(f"a1w_{n}", shape, dt))
            sem = lambda n: self.semaphore(ctx, f"a1w_{n}")
            w_nat = sb("w_nat", [96, 4, C])
            wk_nat = sb("wk_nat", [96, 2, C + 1])
            w1_nat = sb("w1_nat", [96, H])
            b1_rows = sb("b1_rows", [KR, 2, O1])
            conv = sb("conv", [2, PAIRS, NC])
            small = sb("small", [HB, 3, 96])
            spread = sb("spread", [96, 2, H, O1])
            diag = sb("diag", [96, HD])
            mixer = sb("mixer", [96, 2, O1, H, HD])
            w_in, rows_in, conv_in, b1_in = sem("w_in"), sem("rows_in"), sem("conv_in"), sem("b1_in")
            zeroed, turned, small_made, spread_done = sem("zeroed"), sem("turned"), sem("small_made"), sem("spread_done")
            wT_made, diag_made, spread_made, mixer_made = sem("wT_made"), sem("diag_made"), sem("spread_made"), sem("mixer_made")
            folded, folded_kept, wide_made, rows_made = sem("folded"), sem("folded_kept"), sem("wide_made"), sem("rows_made")
            block = ctx.enter_context(nc.Block())

            @block.sync
            def _(sp):
                for a, n in enumerate(("q", "v")):
                    sp.dma_start(w_nat[:, 2 * a:2 * a + 2, :], inp[f"L1_attn_w{n}"].rearrange("(r e) c -> e r c", e=96)).then_inc(w_in, 16)
                    sp.dma_start(wT[1][96:97, a, :], inp[f"L1_attn_b{n}"].rearrange("(a c) -> a c", a=1)).then_inc(rows_in, 16)
                sp.dma_start(wk_nat[:, :, 0:C], inp["L1_attn_wk"].rearrange("(r e) c -> e r c", e=96)).then_inc(w_in, 16)
                with nc.allow_non_contiguous_dma(reason="one bias value for each row"):
                    sp.dma_start(wk_nat[:, :, C:C + 1], inp["L1_attn_bk"].rearrange("(r e a) -> e r a", e=96, a=1)).then_inc(w_in, 16)
                    sp.dma_start(w1_nat[:, :], inp["L1_attn_w1"]).then_inc(w_in, 16)
                    sp.dma_start(b1_rows[96:KR, :, :], inp["L1_attn_b1"].rearrange("(k h o) -> h k o", k=2, o=O1)).then_inc(b1_in, 16)
                    at = 0
                    for n, width in (("w2", 8), ("b2", 1), ("w3", 4), ("b3", 4), ("w4", 4), ("b4", 1)):
                        src = inp[f"L1_attn_{n}"]
                        if len(src.shape) == 2:
                            src = src.rearrange("a b -> (a b)")
                        sp.dma_start(conv[:, :, at:at + width], src.rearrange("(r s o) -> s r o", s=2, o=width)).then_inc(conv_in, 16)
                        at += width

            @block.gpsimd
            def _(pool):
                pool.memset(v[:, :, :], 0.0).then_inc(zeroed, 1)
                pool.memset(aT[:, :, :], 0.0).then_inc(zeroed, 1)
                pool.memset(xg[96:97, 1, :], 1.0).then_inc(zeroed, 1)

            @block.tensor
            def _(pe):
                pe.wait_ge(w_in, 16 * 5)
                pe.wait_ge(rows_in, 32)
                for r in range(2):
                    srcs = [w_nat[:, 2 * r + a, CA * k:CA * k + CA] for k in range(2) for a in range(2)]
                    self.turn_blocks(pe, psT[r], srcs, 96).then_inc(turned, 1)
                bank = ring[0]
                pe.transpose(bank[0:HB, 0, 0:96], self.head_mask[0:96, 0:HB], self.ident[0:96, 0:96])
                for k in range(2):
                    mm = pe.transpose(bank[0:HB, 0, 96 + 96 * k:192 + 96 * k], w1_nat[:, HB * k:HB * k + HB], self.ident[0:96, 0:96])
                mm.then_inc(turned, 1)
                pe.wait_ge(small_made, 1)
                for k in range(2):
                    mm = pe.matmul(bank[0:96, 1, 96 * k:96 * k + 96], small[:, 0, :], small[:, 1 + k, :], start=True, stop=True)
                mm.then_inc(spread_done, 1)
                pe.wait_ge(conv_in, 16 * 6)
                pe.matmul(ring[1][0:NN, 0, 0:PAIRS * NC], self.pair_rows[:, :], conv[:, :, :], start=True, stop=True)\
                  .then_inc(spread_done, 1)
                pe.wait_ge(mixer_made, 2 * O1)
                pe.wait_ge(wT_made, 4)
                for o in range(O1):
                    if o >= 2:
                        pe.wait_ge(folded_kept, 2 * (o - 1))
                    for m in range(2):
                        rows = CA + m
                        for k in range(2):
                            mm = pe.matmul(psT[o % 2][0:rows, C * m:C * m + C], wk_nat[:, k, CA * m:CA * m + rows],
                                           mixer[:, k, o, :, :], start=(k == 0), stop=(k == 1))
                    mm.then_inc(folded, 1)

            @block.vector
            def _(dve):
                dve.tensor_reduce(diag[:, :], self.ident[0:96, 0:96].rearrange("p (h d) -> p d h", d=HD), AX.X, ALU.add).then_inc(diag_made, 1)
                for r in range(2):
                    dve.wait_ge(turned, r + 1)
                    for k in range(2):
                        dve.tensor_copy(wT[k][0:CA, r, :], psT[r][0:CA, C * k:C * k + C]).then_inc(wT_made, 1)
                dve.wait_ge(turned, 3)
                dve.tensor_copy(small[:, :, :].rearrange("h a e -> h (a e)"), ring[0][0:HB, 0, 0:288]).then_inc(small_made, 1)
                dve.wait_ge(spread_done, 1)
                dve.tensor_copy(spread[:, :, :, :].rearrange("e k g o -> e (k g o)"), ring[0][0:96, 1, 0:192]).then_inc(spread_made, 1)
                dve.wait_ge(spread_done, 2)
                dve.tensor_copy(wide[:, :, :].rearrange("m p c -> m (p c)"), ring[1][0:NN, 0, 0:PAIRS * NC]).then_inc(wide_made, 1)
                dve.wait_ge(spread_made, 1)
                dve.wait_ge(diag_made, 1)
                for k in range(2):
                    for o in range(O1):
                        ins = dve.tensor_tensor(mixer[:, k, o, :, :], spread[:, k, :, o:o + 1].to_broadcast([96, H, HD]),
                                                diag[:, :].rearrange("p (a d) -> p a d", a=1).to_broadcast([96, H, HD]), ALU.mult)
                        ins.then_inc(mixer_made, 1)
                dve.wait_ge(b1_in, 16)
                for k in range(2):
                    for b in range(GB):
                        dve.tensor_copy(kmix[96:KR, k, b, :, :],
                                        b1_rows[96:KR, k, :].rearrange("h (o n) -> h o n", n=1).to_broadcast([HB, O1, N])).then_inc(rows_made, 1)
                    for h in range(HB):
                        dve.tensor_copy(qm[96:KR, k, h // 2, :, :].rearrange("c b (s n) -> c b s n", s=2)[:, :, h % 2, :],
                                        self.ident[96:KR, 96 + h:97 + h].rearrange("c (b n) -> c b n", b=1).to_broadcast([HB, GB, N]))\
                           .then_inc(rows_made, 1)
                for o in range(O1):
                    dve.wait_ge(folded, o + 1)
                    dve.tensor_copy(kmixT[0][0:CA, o, :], psT[o % 2][0:CA, 0:C]).then_inc(folded_kept, 1)
                    dve.tensor_copy(kmixT[1][0:CA + 1, o, :], psT[o % 2][0:CA + 1, C:2 * C]).then_inc(folded_kept, 1)

    def experts(self, name, gate, tiles, last):
        nc, inp, hT, xT = self.nc, self.inp, self.hT, self.xT
        gate_w, gate_b, centre, w1_d, b1_d, w2_d, b2_d = [None if n is None else inp[n] for n in gate]
        E = gate_w.shape[1]
        TOPK = 2 if last else 1
        func = ACT.Relu if last else ACT.Gelu
        sorted_x = nc.dram_tensor(f"{name}_sorted_x", (tiles * 128, C), F32, kind="Internal").ap()
        sorted_y = nc.dram_tensor(f"{name}_sorted_y", (tiles * 128, C), F32, kind="Internal").ap()
        with ExitStack() as outer:
            sb0 = lambda n, shape, dt=F32: outer.enter_context(nc.sbuf_tensor(f"{name}_{n}", shape, dt))
            w1 = [sb0(f"w1_{k}", [97, E, F]) for k in range(2)]
            w2 = sb0("w2", [128, E, FC, C])
            b2 = sb0("b2", [1, E, C])
            pos = [sb0(f"pos{t}", [128, RT], U32) for t in range(TOPK)]
            weight = [sb0(f"weight{t}", [128, RT]) for t in range(TOPK)]
            expert_of = sb0("expert_of", [128, tiles], I32)
            h_rows = sb0("h_rows", [128, RT, C]) if last else None
            weights_in = self.semaphore(outer, f"{name}_weights_in")
            self.route(name, E, TOPK, tiles, gate_w, gate_b, centre, pos, weight, expert_of, h_rows, sorted_x,
                       (w1, w2, b2, w1_d, b1_d, w2_d, b2_d, weights_in))
            self.run_experts(name, E, tiles, func, w1, w2, b2, expert_of, weights_in, sorted_x, sorted_y)
            self.gather(name, TOPK, pos, weight, h_rows, sorted_y)

    def route(self, name, E, TOPK, tiles, gate_w, gate_b, centre, pos, weight, expert_of, h_rows, sorted_x, loads):
        nc, hT, xT = self.nc, self.hT, self.xT
        w1, w2, b2, w1_d, b1_d, w2_d, b2_d, weights_in = loads
        sources = [xT, hT] if h_rows is not None else [xT]
        S = len(sources)
        with ExitStack() as ctx:
            sb = lambda n, shape, dt=F32: ctx.enter_context(nc.sbuf_tensor(f"{name}_{n}", shape, dt))
            ps = lambda n, shape: ctx.enter_context(nc.psum_tensor(f"{name}_ps_{n}", shape, F32))
            sem = lambda n: self.semaphore(ctx, f"{name}_{n}")
            gw = [sb(f"gate{k}", [97, E]) for k in range(2)]
            centre_row = sb("centre", [97, E])
            staged = [[sb(f"staged{s}_{a}", [97, 2, GT]) for a in range(S)] for s in range(2)]
            x_rows = sb("x_rows", [128, RT, C])
            rows = [x_rows, h_rows]
            score = sb("score", [128, RT, E])
            e_code = sb("e_code", [128, E])
            t_index = sb("t_index", [128, tiles])
            e_int, t_int = sb("e_int", [128, E], I32), sb("t_int", [128, tiles], I32)
            best = [sb(f"best{t}", [128, RT]) for t in range(TOPK)]
            code = sb("code", [128, RT])
            pick = [sb(f"pick{t}", [128, RT, E]) for t in range(TOPK)]
            chosen, work = sb("chosen", [128, RT, E]), sb("work", [128, RT, E])
            sums = [sb(f"sums{a}", [128, RT, E]) for a in range(2)]
            row_of = sb("row_of", [128, RT, E])
            n_tiles_i, n_tiles = sb("n_tiles_i", [128, E], I32), sb("n_tiles", [128, E])
            ends = [sb(f"ends{a}", [128, E]) for a in range(2)]
            starts = sb("starts", [128, E])
            passed, count_of = sb("passed", [128, tiles, E]), sb("count_of", [128, tiles])
            pos_f = sb("pos_f", [128, RT])
            psS = [ps(f"scores{s}", [128, 512]) for s in range(2)]
            psR = [ps(f"rows{u}", [128, 2, 512]) for u in range(2)]
            psP, psC = ps("before", [128, 512]), ps("counts", [128, 512])
            gate_in, centre_in = sem("gate_in"), sem("centre_in")
            zeroed, cleared, iota_made, gate_made = sem("zeroed"), sem("cleared"), sem("iota_made"), sem("gate_made")
            staged_in = [sem(f"staged_in{s}") for s in range(2)]
            turned = [[sem(f"turned{s}_{a}") for a in range(S)] for s in range(2)]
            rows_kept = [sem(f"rows_kept{u}") for u in range(2)]
            score_kept = [sem(f"score_kept{s}") for s in range(2)]
            scored = [sem(f"scored{s}") for s in range(2)]
            step_done, picked, counted = sem("step_done"), sem("picked"), sem("counted")
            exp_needed, exp_made, placed, scattered = sem("exp_needed"), sem("exp_made"), sem("placed"), self.scattered[name]
            block = ctx.enter_context(nc.Block())

            bank = lambda s, a: (s + a) % 2 if S == 1 else a
            bank_uses = lambda i, s: i if S == 1 else i * 2 + s

            @block.sync
            def _(sp):
                for k in range(2):
                    sp.dma_start(gw[k][0:CA, :], gate_w[CA * k:CA * k + CA, :]).then_inc(gate_in, 16)
                sp.dma_start(gw[1][CA:CA + 1, :], gate_b.rearrange("(a e) -> a e", a=1)).then_inc(gate_in, 16)
                if centre is not None:
                    sp.dma_start(centre_row[CA:CA + 1, :], centre.rearrange("(a e) -> a e", a=1)).then_inc(centre_in, 16)
                sp.dma_start(sorted_x.rearrange("(t p) c -> p t c", p=128),
                             self.zeros[:, :].rearrange("p (t c) -> p t c", t=1).to_broadcast([128, tiles, C])).then_inc(cleared, 16)
                for k in range(2):
                    sp.dma_start(w1[k][0:CA, :, :], w1_d[:, CA * k:CA * k + CA, :].rearrange("e c f -> c e f")).then_inc(weights_in, 16)
                sp.dma_start(w1[1][CA:CA + 1, :, :], b1_d.rearrange("(a e) f -> a e f", a=1)).then_inc(weights_in, 16)
                for e in range(E):
                    sp.dma_start(w2[:, e, :, :], w2_d[e].rearrange("(q p) c -> p q c", p=128)).then_inc(weights_in, 16)
                sp.dma_start(b2[:, :, :], b2_d.rearrange("(a e) c -> a e c", a=1)).then_inc(weights_in, 16)

            @block.gpsimd
            def _(pool):
                pool.iota(e_int[:, :], pattern=[[1, E]], base=-100, channel_multiplier=0).then_inc(iota_made, 1)
                pool.iota(t_int[:, :], pattern=[[1, tiles]], base=0, channel_multiplier=0).then_inc(iota_made, 1)
                pool.memset(score[:, :, :], 0.0).then_inc(zeroed, 1)
                pool.wait_ge(zeroed, 1)
                pool.wait_ge(iota_made, 2)
                for s in range(2):
                    pool.memset(staged[s][0][CA:CA + 1, 1, :], 1.0).then_inc(zeroed, 1)
                pool.wait_ge(zeroed, 3)
                pool.wait_ge(iota_made, 2)
                pool.wait_ge(cleared, 16)
                pool.wait_ge(placed, TOPK)
                for s in range(2):
                    pool.wait_ge(rows_kept[s], S * (G // 2) + 1)
                for t in range(TOPK):
                    for j in range(RT):
                        r = ROWS[j % Q3]
                        pool.indirect_dma_start(out=sorted_x, out_offset=bass.IndirectOffsetOnAxis(ap=pos[t][0:r, j:j + 1], axis=0),
                                                in_=x_rows[0:r, j, :], in_offset=None).then_inc(scattered, 16)
                pool.wait_ge(scattered, 16 * TOPK * RT)

            @block.tensor
            def _(pe):
                pe.wait_ge(gate_made, 1)
                pe.wait_ge(zeroed, 3)
                with pe.Fori(0, G // 2) as i:
                    for s in range(2):
                        pe.wait_ge(score_kept[s], i + 1)
                        pe.wait_ge(staged_in[s], i * 2 * S + 2 * S)
                        for q in range(Q3):
                            for k in range(2):
                                r = CA + k
                                mm = pe.matmul(psS[s][0:ROWS[q], E * q:E * q + E], staged[s][0][0:r, k, 128 * q:128 * q + ROWS[q]],
                                               gw[k][0:r, :], start=(k == 0), stop=(k == 1))
                        for a in range(S):
                            pe.wait_ge(rows_kept[bank(s, a)], bank_uses(i, s) + 1)
                            for q in range(Q3):
                                for k in range(2):
                                    mm = pe.transpose(psR[bank(s, a)][0:ROWS[q], q // 2, C * (q % 2) + CA * k:C * (q % 2) + CA * k + CA],
                                                      staged[s][a][0:CA, k, 128 * q:128 * q + ROWS[q]], self.ident[0:CA, 0:CA])
                            mm.then_inc(scored[s] if a == S - 1 else turned[s][a], 1)
                pe.wait_ge(picked, 1)
                pe.matmul(psP[:, 0:RT * E], self.below[:, :], chosen[:, :, :], start=True, stop=True)
                pe.matmul(psC[:, 0:RT * E], self.ones[:, :], chosen[:, :, :], start=True, stop=True).then_inc(counted, 1)

            @block.scalar
            def _(act):
                for s in range(2):
                    act.sem_inc(rows_kept[s], 1)
                with act.Fori(0, G // 2) as i:
                    for s in range(2):
                        for a in range(S):
                            if a == S - 1:
                                act.wait_ge(scored[s], i + 1)
                            else:
                                act.wait_ge(turned[s][a], i + 1)
                            act.activation(rows[a][:, bass.ds((i * 2 + s) * Q3, 2), :].rearrange("p q c -> p (q c)"),
                                           psR[bank(s, a)][:, 0, 0:2 * C], ACT.Copy)
                            act.activation(rows[a][0:ROWS[2], bass.ds((i * 2 + s) * Q3 + 2, 1), :].rearrange("p q c -> p (q c)"),
                                           psR[bank(s, a)][0:ROWS[2], 1, 0:C], ACT.Copy)\
                               .then_inc(rows_kept[bank(s, a)], 1)
                if TOPK == 2:
                    act.wait_ge(exp_needed, 1)
                    act.activation(weight[1][:, :], best[1][:, :], ACT.Exp).then_inc(exp_made, 1)

            @block.vector
            def _(dve):
                steps = 0

                def step(ins):
                    nonlocal steps
                    ins.then_inc(step_done, 1)
                    steps += 1
                    dve.wait_ge(step_done, steps)

                over_e = lambda m: m[:, :].rearrange("p (j a) -> p j a", a=1).to_broadcast([128, RT, E])
                over_j = lambda m: m[:, :].rearrange("p (a e) -> p a e", a=1).to_broadcast([128, RT, E])
                dve.wait_ge(gate_in, 48)
                if centre is not None:
                    dve.wait_ge(centre_in, 16)
                    dve.tensor_tensor(gw[1][CA:CA + 1, :], gw[1][CA:CA + 1, :], centre_row[CA:CA + 1, :], ALU.subtract)\
                       .then_inc(gate_made, 1)
                else:
                    dve.sem_inc(gate_made, 1)
                dve.wait_ge(iota_made, 2)
                step(dve.tensor_copy(e_code[:, :], e_int[:, :]))
                step(dve.tensor_copy(t_index[:, :], t_int[:, :]))
                dve.wait_ge(zeroed, 3)

                def stage(i, s):
                    for a in range(S):
                        for k in range(2):
                            dve.tensor_copy(staged[s][a][0:CA, k, :], sources[a][k][0:CA, bass.ds((i * 2 + s) * GT, GT)])\
                               .then_inc(staged_in[s], 1)

                def keep_scores(i, s):
                    j = (i * 2 + s) * Q3
                    dve.wait_ge(scored[s], i + 1)
                    dve.tensor_copy(score[:, bass.ds(j, 2), :].rearrange("p q e -> p (q e)"), psS[s][:, 0:2 * E])
                    dve.tensor_copy(score[0:ROWS[2], bass.ds(j + 2, 1), :].rearrange("p q e -> p (q e)"),
                                    psS[s][0:ROWS[2], 2 * E:3 * E]).then_inc(score_kept[s], 1)

                for s in range(2):
                    dve.sem_inc(score_kept[s], 1)
                    stage(0, s)
                with dve.Fori(0, G // 2 - 1) as i:
                    for s in range(2):
                        keep_scores(i, s)
                        stage(i + 1, s)
                for s in range(2):
                    keep_scores(G // 2 - 1, s)
                for s in range(2):
                    dve.wait_ge(score_kept[s], G // 2 + 1)
                for t in range(TOPK):
                    step(dve.tensor_reduce(best[t][:, :], score[:, :, :], AX.X, ALU.max))
                    step(dve.tensor_tensor(work[:, :, :], score[:, :, :], over_e(best[t]), ALU.is_equal))
                    step(dve.tensor_tensor(work[:, :, :], work[:, :, :], over_j(e_code), ALU.mult))
                    step(dve.tensor_reduce(code[:, :], work[:, :, :], AX.X, ALU.min))
                    step(dve.tensor_tensor(pick[t][:, :, :], over_e(code), over_j(e_code), ALU.is_equal))
                    step(dve.tensor_tensor(pick[t][:, :, :], pick[t][:, :, :],
                                           self.row_valid[:, :, :].rearrange("p g (q a) -> p (g q) a", a=1).to_broadcast([128, RT, E]),
                                           ALU.mult))
                    if t < TOPK - 1:
                        step(dve.scalar_tensor_tensor(out=score[:, :, :], in0=pick[t][:, :, :], scalar=-3.0e38,
                                                      in1=score[:, :, :], op0=ALU.mult, op1=ALU.add))
                if TOPK == 2:
                    step(dve.tensor_tensor(best[1][:, :], best[1][:, :], best[0][:, :], ALU.subtract))
                    dve.sem_inc(exp_needed, 1)
                    dve.wait_ge(exp_made, 1)
                    step(dve.tensor_scalar(best[0][:, :], weight[1][:, :], 1.0, None, ALU.add))
                    step(dve.reciprocal(weight[0][:, :], best[0][:, :]))
                    step(dve.tensor_tensor(weight[1][:, :], weight[1][:, :], weight[0][:, :], ALU.mult))
                    dve.tensor_tensor(chosen[:, :, :], pick[0][:, :, :], pick[1][:, :, :], ALU.add).then_inc(picked, 1)
                else:
                    dve.tensor_copy(chosen[:, :, :], pick[0][:, :, :]).then_inc(picked, 1)
                dve.wait_ge(counted, 1)
                flat = lambda m: m[:, :, :].rearrange("p j e -> p (j e)")
                step(dve.tensor_copy(flat(sums[0]), psC[:, 0:RT * E]))
                src, d = 0, 1
                while d < RT:
                    a, b = sums[src], sums[1 - src]
                    step(dve.tensor_copy(b[:, 0:d, :], a[:, 0:d, :]))
                    step(dve.tensor_tensor(b[:, d:RT, :], a[:, d:RT, :], a[:, 0:RT - d, :], ALU.add))
                    src, d = 1 - src, 2 * d
                total = sums[src]
                step(dve.tensor_scalar(n_tiles_i[:, :], total[:, RT - 1, :], 127.0, None, ALU.add))
                step(dve.tensor_scalar(n_tiles_i[:, :], n_tiles_i[:, :], 7, None, ALU.logical_shift_right))
                step(dve.tensor_copy(n_tiles[:, :], n_tiles_i[:, :]))
                step(dve.tensor_copy(ends[0][:, :], n_tiles[:, :]))
                es, d = 0, 1
                while d < E:
                    a, b = ends[es], ends[1 - es]
                    step(dve.tensor_copy(b[:, 0:d], a[:, 0:d]))
                    step(dve.tensor_tensor(b[:, d:E], a[:, d:E], a[:, 0:E - d], ALU.add))
                    es, d = 1 - es, 2 * d
                end = ends[es]
                step(dve.tensor_tensor(starts[:, :], end[:, :], n_tiles[:, :], ALU.subtract))
                step(dve.tensor_scalar(starts[:, :], starts[:, :], 128.0, None, ALU.mult))
                step(dve.tensor_tensor(flat(row_of), flat(total), psC[:, 0:RT * E], ALU.subtract))
                step(dve.tensor_tensor(flat(row_of), flat(row_of), psP[:, 0:RT * E], ALU.add))
                step(dve.tensor_tensor(row_of[:, :, :], row_of[:, :, :], over_j(starts), ALU.add))
                for t in range(TOPK):
                    step(dve.tensor_tensor(work[:, :, :], row_of[:, :, :], pick[t][:, :, :], ALU.mult))
                    step(dve.tensor_reduce(pos_f[:, :], work[:, :, :], AX.X, ALU.add))
                    dve.tensor_copy(pos[t][:, :], pos_f[:, :]).then_inc(placed, 1)
                    dve.wait_ge(placed, t + 1)
                in_t = [128, tiles, E]
                step(dve.tensor_tensor(passed[:, :, :], t_index[:, :].rearrange("p (t a) -> p t a", a=1).to_broadcast(in_t),
                                       end[:, :].rearrange("p (a e) -> p a e", a=1).to_broadcast(in_t), ALU.is_ge))
                step(dve.tensor_reduce(count_of[:, :], passed[:, :, :], AX.X, ALU.add))
                step(dve.tensor_scalar(expert_of[:, :], count_of[:, :], float(E - 1), None, ALU.min))

    def run_experts(self, name, E, tiles, func, w1, w2, b2, expert_of, weights_in, sorted_x, sorted_y):
        nc = self.nc
        BODY = (tiles - 2) // 2
        with ExitStack() as ctx:
            sb = lambda n, shape, dt=F32: ctx.enter_context(nc.sbuf_tensor(f"{name}_{n}", shape, dt))
            ps = lambda n, shape: ctx.enter_context(nc.psum_tensor(f"{name}_ps_{n}", shape, F32))
            sem = lambda n: self.semaphore(ctx, f"{name}_{n}")
            x_in_buf = [sb(f"x_tile{s}", [128, C]) for s in range(2)]
            xt = [sb(f"xt{s}", [97, 2, 128]) for s in range(2)]
            hid = [sb(f"hid{s}", [128, F]) for s in range(2)]
            hidT = sb("hidT", [128, FC, 128])
            y = [sb(f"y{s}", [128, C]) for s in range(2)]
            psX, psY = ps("x_turned", [128, 2, 256]), ps("y", [128, 2, 256])
            psH = [ps(f"hid{s}", [128, 2, 512]) for s in range(2)]
            psT = ps("hid_turned", [128, 2, 512])
            ones_made = sem("ones_made")
            x_in = [sem(f"x_in{s}") for s in range(2)]
            x_turned = [sem(f"x_turned{s}") for s in range(2)]
            x_kept = [sem(f"x_kept{s}") for s in range(2)]
            h_done = [sem(f"h_done{s}") for s in range(2)]
            h_kept = [sem(f"h_kept{s}") for s in range(2)]
            t_done = [sem(f"t_done{s}") for s in range(2)]
            t_kept = [sem(f"t_kept{s}") for s in range(2)]
            y_done = [sem(f"y_done{s}") for s in range(2)]
            y_kept = [sem(f"y_kept{s}") for s in range(2)]
            y_out = [sem(f"y_out{s}") for s in range(2)]
            block = ctx.enter_context(nc.Block())

            def over_tiles(eng, first, step, fori_to, peeled_to):
                with eng.Fori(0, fori_to) as i:
                    for s in range(2):
                        step(i, s)
                for t in range(2 * fori_to, peeled_to):
                    step(t // 2, t % 2)

            @block.sync
            def _(sp):
                def load(n, s, ahead=0):
                    sp.dma_start(x_in_buf[s][:, :], sorted_x[bass.ds((n * 2 + s + ahead) * 128, 128), :]).then_inc(x_in[s], 16)

                def store(n, s):
                    sp.wait_ge(y_kept[s], n + 2)
                    sp.dma_start(sorted_y[bass.ds((n * 2 + s) * 128, 128), :], y[s][:, :]).then_inc(y_out[s], 16)

                def reload(n, s):
                    sp.wait_ge(x_turned[s], n + 1)
                    load(n, s, 2)

                for ahead in (0, 1):
                    load(0, ahead)
                for t in (0, 1):
                    reload(0, t)
                with sp.Fori(0, BODY - 1) as i:
                    for s in range(2):
                        reload(i + 1, s)
                        store(i, s)
                for t in range(2 * BODY, tiles - 2):
                    reload(t // 2, t % 2)
                    store(t // 2 - 1, t % 2)
                for t in range(tiles - 4, tiles):
                    store(t // 2, t % 2)
                for s in range(2):
                    sp.wait_ge(y_out[s], 16 + 16 * ((tiles + 1 - s) // 2))

            @block.gpsimd
            def _(pool):
                for s in range(2):
                    pool.memset(xt[s][CA:CA + 1, 1, :], 1.0).then_inc(ones_made, 1)

            @block.tensor
            def _(pe):
                def turn_x(n, s):
                    pe.wait_ge(x_in[s], n * 16 + 16)
                    for k in range(2):
                        mm = pe.transpose(psX[0:CA, s, 128 * k:128 * k + 128], x_in_buf[s][:, CA * k:CA * k + CA], self.ident[:, :])
                    mm.then_inc(x_turned[s], 1)

                def expert(n, s):
                    return pe.value_load(expert_of[0:1, bass.ds(n * 2 + s, 1)], min_val=0, max_val=E - 1)

                def first_product(n, s):
                    e = expert(n, s)
                    pe.wait_ge(x_kept[s], n + 1)
                    for half in range(2):
                        for k in range(2):
                            r = CA + k
                            mm = pe.matmul(psH[s][:, half, 0:F // 2], xt[s][0:r, k, :],
                                           w1[k][0:r, :, :].rearrange("c e f -> c (e f)")[:, bass.ds(e * F + half * (F // 2), F // 2)],
                                           start=(k == 0), stop=(k == 1))
                    mm.then_inc(h_done[s], 1)

                def turn_hidden(n, s):
                    pe.wait_ge(h_kept[s], n + 1)
                    for q in range(FC):
                        mm = pe.transpose(psT[:, q // 3, 128 * (q % 3):128 * (q % 3) + 128], hid[s][:, 128 * q:128 * q + 128],
                                          self.ident[:, :])
                    mm.then_inc(t_done[s], 1)

                def second_product(n, s):
                    e = expert(n, s)
                    pe.wait_ge(y_kept[1 - s], n + 1 + s)
                    pe.wait_ge(t_kept[s], n + 1)
                    for q in range(FC):
                        pe.matmul(psY[:, s, 0:C], hidT[:, q, :],
                                  w2[:, :, :, :].rearrange("p e q c -> p (e q c)")[:, bass.ds(e * (FC * C) + q * C, C)],
                                  start=(q == 0), stop=False)
                    pe.matmul(psY[:, s, 0:C], self.ones[0:1, 0:128], b2[:, :, :].rearrange("a e c -> a (e c)")[:, bass.ds(e * C, C)],
                              start=False, stop=True).then_inc(y_done[s], 1)

                pe.wait_ge(weights_in, 16 * (4 + E))
                pe.wait_ge(ones_made, 2)
                turn_x(0, 0)
                pe.wait_ge(x_kept[0], 1)
                turn_x(0, 1)
                first_product(0, 0)

                def step(n, s):
                    turn_hidden(n, s)
                    first_product(n + s, 1 - s)
                    turn_x(n + 1, s)
                    second_product(n, s)

                over_tiles(pe, 0, step, BODY, tiles - 2)
                for t in range(tiles - 2, tiles):
                    n, s = t // 2, t % 2
                    turn_hidden(n, s)
                    if t + 1 < tiles:
                        first_product(n + s, 1 - s)
                    second_product(n, s)

            @block.scalar
            def _(act):
                def step(n, s):
                    act.wait_ge(h_done[s], n + 1)
                    act.activation(hid[s][:, :].rearrange("p (a f) -> p a f", a=2), psH[s][:, :, 0:F // 2], func).then_inc(h_kept[s], 1)

                over_tiles(act, 0, step, tiles // 2, tiles)

            @block.vector
            def _(dve):
                def keep_x(n, s):
                    dve.wait_ge(x_turned[s], n + 1)
                    dve.tensor_copy(xt[s][0:CA, :, :], psX[0:CA, s, :].rearrange("c (k p) -> c k p", k=2)).then_inc(x_kept[s], 1)

                def keep_hidden(n, s):
                    dve.wait_ge(t_done[s], n + 1)
                    dve.tensor_copy(hidT[:, :, :].rearrange("f (a q) p -> f a (q p)", a=2), psT[:, :, 0:384]).then_inc(t_kept[s], 1)

                def keep_y(n, s):
                    dve.wait_ge(y_done[s], n + 1)
                    dve.wait_ge(y_out[s], n * 16 + 16)
                    dve.tensor_copy(y[s][:, :], psY[:, s, 0:C]).then_inc(y_kept[s], 1)

                for s in range(2):
                    dve.sem_inc(y_kept[s], 1)
                    dve.sem_inc(y_out[s], 16)
                keep_x(0, 0)
                keep_x(0, 1)

                def step(n, s):
                    keep_hidden(n, s)
                    keep_x(n + 1, s)
                    keep_y(n, s)

                over_tiles(dve, 0, step, BODY, tiles - 2)
                for t in range(tiles - 2, tiles):
                    keep_hidden(t // 2, t % 2)
                    keep_y(t // 2, t % 2)

    def gather(self, name, TOPK, pos, weight, h_rows, sorted_y):
        nc, hT = self.nc, self.hT
        with ExitStack() as ctx:
            sb = lambda n, shape, dt=F32: ctx.enter_context(nc.sbuf_tensor(f"{name}_{n}", shape, dt))
            sem = lambda n: self.semaphore(ctx, f"{name}_{n}")
            got = [sb(f"got{t}", [128, RT, C]) for t in range(TOPK)]
            psG = [ctx.enter_context(nc.psum_tensor(f"{name}_back{s}", [128, 512], F32)) for s in range(2)]
            back = [sem(f"back{s}") for s in range(2)]
            added = [sem(f"added{s}") for s in range(2)]
            mixed, summed, stored = sem("mixed"), sem("summed"), sem("stored")
            ready = self.gather_ready[name]
            block = ctx.enter_context(nc.Block())
            per_group = 16 * Q3 * TOPK

            @block.gpsimd
            def _(pool):
                for j in range(RT):
                    for t in range(TOPK):
                        r = ROWS[j % Q3]
                        pool.indirect_dma_start(out=got[t][0:r, j, :], out_offset=None, in_=sorted_y,
                                                in_offset=bass.IndirectOffsetOnAxis(ap=pos[t][0:r, j:j + 1], axis=0))\
                            .then_inc(ready[j // Q3], 16)

            if h_rows is None:
                @block.tensor
                def _(pe):
                    for j in range(RT):
                        s, r = j % 2, ROWS[j % Q3]
                        if j % Q3 == 0:
                            pe.wait_ge(ready[j // Q3], per_group)
                        if j >= 2:
                            pe.wait_ge(added[s], 2 * (j // 2))
                        for k in range(2):
                            mm = pe.transpose(psG[s][0:CA, 128 * k:128 * k + r], got[0][0:r, j, CA * k:CA * k + CA],
                                              self.ident[0:r, 0:r])
                        mm.then_inc(back[s], 1)

                @block.vector
                def _(dve):
                    for j in range(RT):
                        s, r = j % 2, ROWS[j % Q3]
                        at = GT * (j // Q3) + 128 * (j % Q3)
                        dve.wait_ge(back[s], j // 2 + 1)
                        for k in range(2):
                            dve.tensor_tensor(hT[k][0:CA, at:at + r], hT[k][0:CA, at:at + r], psG[s][0:CA, 128 * k:128 * k + r],
                                              ALU.add).then_inc(added[s], 1)
            else:
                @block.vector
                def _(dve):
                    for j in range(RT):
                        r = ROWS[j % Q3]
                        if j % Q3 == 0:
                            dve.wait_ge(ready[j // Q3], per_group)
                        dve.scalar_tensor_tensor(out=got[0][0:r, j, :], in0=got[0][0:r, j, :], scalar=weight[0][0:r, j:j + 1],
                                                 in1=h_rows[0:r, j, :], op0=ALU.mult, op1=ALU.add).then_inc(mixed, 1)
                        if j >= 1:
                            finish = j - 1
                            rf = ROWS[finish % Q3]
                            dve.wait_ge(mixed, finish + 1)
                            dve.scalar_tensor_tensor(out=got[1][0:rf, finish, :], in0=got[1][0:rf, finish, :],
                                                     scalar=weight[1][0:rf, finish:finish + 1],
                                                     in1=got[0][0:rf, finish, :], op0=ALU.mult, op1=ALU.add).then_inc(summed, 1)
                    dve.wait_ge(mixed, RT)
                    dve.scalar_tensor_tensor(out=got[1][0:ROWS[2], RT - 1, :], in0=got[1][0:ROWS[2], RT - 1, :],
                                             scalar=weight[1][0:ROWS[2], RT - 1:RT],
                                             in1=got[0][0:ROWS[2], RT - 1, :], op0=ALU.mult, op1=ALU.add).then_inc(summed, 1)

                @block.sync
                def _(sp):
                    rows = self.out.rearrange("b n c -> (b n) c")
                    for g in range(G):
                        sp.wait_ge(summed, Q3 * (g + 1))
                        full = rows[GT * g:GT * g + 256, :].rearrange("(q p) c -> p q c", p=128)
                        sp.dma_start(full, got[1][:, Q3 * g:Q3 * g + 2, :]).then_inc(stored, 16)
                        sp.dma_start(rows[GT * g + 256:GT * g + GT, :], got[1][0:ROWS[2], Q3 * g + 2, :]).then_inc(stored, 16)
                    sp.wait_ge(stored, 32 * G)


def build(nc, inp, out):
    with ExitStack() as ctx:
        t = Tower(nc, inp, out)
        sb = lambda name, shape, dt=F32: ctx.enter_context(nc.sbuf_tensor(name, shape, dt))
        t.scattered, t.gather_ready = {}, {}
        for name in ("ffn0", "ffn1"):
            t.scattered[name] = ctx.enter_context(nc.semaphore(f"{name}_scattered"))
            t.gather_ready[name] = [ctx.enter_context(nc.semaphore(f"{name}_ready{g}")) for g in range(G)]
        t.hT = [sb("hT0", [CA, TOK]), sb("hT1", [CB, TOK])]
        t.xT = [sb("xT0", [CA, TOK]), sb("xT1", [CB + 1, TOK])]
        t.ident = sb("ident", [128, 128])
        t.head_mask = sb("head_mask", [128, 8])
        t.half_mask = sb("half_mask", [128, 2])
        t.pair_rows = sb("pair_rows", [2, NN])
        t.ones = sb("ones", [128, 128])
        t.mean_w = sb("mean_w", [128, 128])
        t.below = sb("below", [128, 128])
        t.zeros = sb("zeros", [128, C])
        t.eps = sb("eps", [128, 1])
        t.row_valid = sb("row_valid", [128, G, Q3])
        t.constants()
        t.embed()
        t.layernorm("norm1")
        t.attention0()
        t.layernorm("norm2")
        t.experts("ffn0", ["L0_ffn_gate_w", "L0_ffn_gate_b", "L0_ffn_gate_center", "L0_ffn_w1", "L0_ffn_b1", "L0_ffn_w2",
                           "L0_ffn_b2"], TILES0, last=False)
        t.layernorm("norm3")
        t.clear_semaphores()
        t.attention1()
        t.layernorm("norm4")
        t.experts("ffn1", ["L1_ffn_Wg", "L1_ffn_bg", None, "L1_ffn_W1", "L1_ffn_b1", "L1_ffn_W2", "L1_ffn_b2"],
                  TILES1, last=True)


_INS = ['x', 'L0_tok_W', 'L0_tok_b', 'L0_attn_qkv_weight', 'L0_attn_qkv_bias', 'L0_attn_proj_weight',
        'L0_attn_proj_bias', 'L0_ffn_gate_w', 'L0_ffn_gate_b', 'L0_ffn_gate_center', 'L0_ffn_w1', 'L0_ffn_b1',
        'L0_ffn_w2', 'L0_ffn_b2', 'L1_attn_wq', 'L1_attn_bq', 'L1_attn_wk', 'L1_attn_bk', 'L1_attn_wv',
        'L1_attn_bv', 'L1_attn_w1', 'L1_attn_b1', 'L1_attn_w2', 'L1_attn_b2', 'L1_attn_w3', 'L1_attn_b3',
        'L1_attn_w4', 'L1_attn_b4', 'L1_ffn_Wg', 'L1_ffn_bg', 'L1_ffn_W1', 'L1_ffn_b1', 'L1_ffn_W2', 'L1_ffn_b2']


def kernel(**inputs):
    import numpy as _np
    import concourse.bacc as _bacc
    from concourse import mybir as _mybir
    from concourse.bass_utils import run_bass_kernel_spmd as _run

    nc = _bacc.Bacc("TRN2", target_bir_lowering=False, num_devices=1)
    arrays, inp = {}, {}
    for name in _INS:
        a = _np.ascontiguousarray(inputs[name])
        arrays[f"in_{name}"] = a
        inp[name] = nc.dram_tensor(f"in_{name}", a.shape, _mybir.dt.from_np(a.dtype), kind="ExternalInput").ap()
    out = nc.dram_tensor("out_0", (B, N, C), F32, kind="ExternalOutput").ap()
    build(nc, inp, out)
    r = _run(nc, [arrays], core_ids=[0])
    return r.results[0]["out_0"]
```

```python
from contextlib import ExitStack

import concourse.bass as bass
from concourse import mybir

F32 = mybir.dt.float32
F32R = mybir.dt.float32r
I32 = mybir.dt.int32
U32 = mybir.dt.uint32
ALU = mybir.AluOpType
ACT = mybir.ActivationFunctionType
AX = mybir.AxisListType

B, CH, T_IN = 64, 90, 750
PATCH, N = 16, 46
C = 192
CA, CB = C // 2, C // 2
TOK = B * N
GB = 8
G = B // GB
GT = GB * N
H, HD = 12, 16
PAIRS = H // 2
PB = PAIRS // 2
NN = 2 * N
F = 768
FC = F // 128
EPS = 1e-5
CONSTANTS = 17
O1, O3 = 8, 4
MIX_CONSTS = O1 + 1 + 3 * O3 + 1
Q3 = 3
ROWS = [128, 128, GT - 256]
RT = G * Q3
TILES0 = (TOK + 4 * 127) // 128
TILES1 = (2 * TOK + 8 * 127) // 128


def seg(block):
    return (slice(0, CA), CA) if block == 0 else (slice(CA, C), CB)


class Tower:

    def __init__(self, nc, inp, out):
        self.nc, self.inp, self.out = nc, inp, out
        self.used = []

    def semaphore(self, scope, name):
        handle = scope.enter_context(self.nc.semaphore(name))
        self.used.append(handle)
        return handle

    def clear_semaphores(self):
        with self.nc.Block() as block:
            @block.gpsimd
            def _(pool):
                for handle in self.used:
                    pool.sem_clear(handle)
        self.used = []

    def write_constants(self, pool, made):
        ident, head, pairsel = self.ident, self.head_mask, self.pair_rows
        steps = 0

        def after(ins):
            nonlocal steps
            ins.then_inc(made, 1)
            steps += 1
            pool.wait_ge(made, steps)

        after(pool.memset(ident[:, :], 0.0))
        after(pool.affine_select(out=ident[:, :], in_=ident[:, :], compare_op=ALU.not_equal, fill=1.0,
                                 base=0, pattern=[[-1, 128]], channel_multiplier=1))
        after(pool.memset(head[:, :], 1.0))
        after(pool.affine_select(out=head[:, :], in_=head[:, :], compare_op=ALU.is_ge, fill=0.0,
                                 base=0, pattern=[[-HD, 8]], channel_multiplier=1))
        after(pool.affine_select(out=head[:, :], in_=head[:, :], compare_op=ALU.is_ge, fill=0.0,
                                 base=HD - 1, pattern=[[HD, 8]], channel_multiplier=-1))
        after(pool.memset(pairsel[:, :], 1.0))
        after(pool.affine_select(out=pairsel[:, :], in_=pairsel[:, :], compare_op=ALU.is_ge, fill=0.0,
                                 base=0, pattern=[[1, NN]], channel_multiplier=-N))
        after(pool.affine_select(out=pairsel[:, :], in_=pairsel[:, :], compare_op=ALU.is_ge, fill=0.0,
                                 base=N - 1, pattern=[[-1, NN]], channel_multiplier=N))
        after(pool.memset(self.ones[:, :], 1.0))
        after(pool.memset(self.mean_w[:, :], 1.0 / C))
        after(pool.memset(self.below[:, :], 1.0))
        after(pool.affine_select(out=self.below[:, :], in_=self.below[:, :], compare_op=ALU.is_gt, fill=0.0,
                                 base=0, pattern=[[1, 128]], channel_multiplier=-1))
        after(pool.memset(self.xT[1][CB:CB + 1, :], 1.0))
        after(pool.memset(self.zeros[:, :], 0.0))
        after(pool.memset(self.eps[:, :], EPS))
        after(pool.memset(self.row_valid[:, :, :], 1.0))
        after(pool.affine_select(out=self.row_valid[:, :, Q3 - 1:Q3], in_=self.row_valid[:, :, Q3 - 1:Q3],
                                 compare_op=ALU.is_ge, fill=0.0, base=ROWS[2] - 1,
                                 pattern=[[0, G], [0, 1]], channel_multiplier=-1))
        assert steps == CONSTANTS

    def embed(self):
        nc, inp, hT = self.nc, self.inp, self.hT
        x_d = inp["x"][:, :, 0:N * PATCH]
        HB = GB // 2
        with ExitStack() as ctx:
            sb = lambda name, shape, dt=F32: ctx.enter_context(nc.sbuf_tensor(name, shape, dt))
            sem = lambda name: self.semaphore(ctx, name)
            w_nat = sb("tok_w", [96, 2, CH * PATCH])
            wT_high, wT_low = sb("tok_wT_high", [96, PATCH, C], F32R), sb("tok_wT_low", [96, PATCH, C], F32R)
            bias = sb("tok_bias", [128, 2])
            xs = [sb(f"x_half{a}", [96, HB, N * PATCH]) for a in range(2)]
            high = [sb(f"x_high{i}", [96, GB, N * PATCH], F32R) for i in range(2)]
            low = [sb(f"x_low{i}", [96, GB, N * PATCH], F32R) for i in range(2)]
            psT = [ctx.enter_context(nc.psum_tensor(f"tok_psT{i}", [128, 512], F32)) for i in range(2)]
            psY = [[ctx.enter_context(nc.psum_tensor(f"tok_y{i}{k}", [128, 512], F32)) for k in range(2)]
                   for i in range(2)]
            w_in, b_in = sem("tok_w_in"), sem("tok_b_in")
            x_in = [sem(f"x_in{a}") for a in range(2)]
            turned, wT_high_made, wT_made = sem("tok_turned"), sem("tok_wT_high_made"), sem("tok_wT_made")
            wT_padded = sem("tok_wT_padded")
            padded, const_made = sem("tok_padded"), sem("const_made")
            high_made = [sem(f"x_high_made{i}") for i in range(2)]
            low_made = [sem(f"x_low_made{i}") for i in range(2)]
            split_done = [sem(f"x_split{a}") for a in range(2)]
            y_done = [sem(f"y_done{i}") for i in range(2)]
            y_kept_act = [sem(f"y_kept_act{i}") for i in range(2)]
            y_kept_dve = [sem(f"y_kept_dve{i}") for i in range(2)]
            block = ctx.enter_context(nc.Block())
            half = lambda a: slice(HB * a, HB * a + HB)

            @block.sync
            def _(sp):
                sp.dma_start(w_nat[:, :, :], inp["L0_tok_W"].rearrange("(h e) f -> e h f", h=2)).then_inc(w_in, 16)
                sp.dma_start(bias[0:CA, 0:1], inp["L0_tok_b"][0:CA].rearrange("(e a) -> e a", a=1)).then_inc(b_in, 16)
                sp.dma_start(bias[0:CB, 1:2], inp["L0_tok_b"][CA:C].rearrange("(e a) -> e a", a=1)).then_inc(b_in, 16)
                for a in range(2):
                    sp.wait_ge(padded, a + 1)
                    sp.dma_start(xs[a][0:CH, :, :], x_d[HB * a:HB * a + HB].rearrange("b c t -> c b t")).then_inc(x_in[a], 16)
                with sp.Fori(0, G - 1) as g:
                    for a in range(2):
                        sp.wait_ge(split_done[a], g + 1)
                        sp.dma_start(xs[a][0:CH, :, :], x_d[bass.ds((g + 1) * GB + HB * a, HB)].rearrange("b c t -> c b t"))\
                          .then_inc(x_in[a], 16)

            @block.gpsimd
            def _(pool):
                self.write_constants(pool, const_made)

            @block.tensor
            def _(pe):
                pe.wait_ge(const_made, 2)
                pe.wait_ge(w_in, 16)
                for k in range(PATCH // 2):
                    if k >= 2:
                        pe.wait_ge(wT_made, k - 1)
                    for j in range(4):
                        p, side = 2 * k + j // 2, j % 2
                        src = w_nat[:, side, :].rearrange("e (c p) -> e p c", p=PATCH)[:, p, :]
                        mm = pe.transpose(psT[k % 2][0:CH, 96 * j:96 * j + 96], src, self.ident[0:96, 0:96])
                    mm.then_inc(turned, 1)
                pe.wait_ge(wT_made, PATCH // 2)
                for s in range(2):
                    pe.sem_inc(y_done[s], 1)
                with pe.Fori(0, G // 2) as i:
                    for s in range(2):
                        pe.wait_ge(low_made[s], i * 2 + 2)
                        pe.wait_ge(y_kept_act[s], i + 1)
                        pe.wait_ge(y_kept_dve[s], i + 1)
                        parts = ((wT_high, low[s]), (wT_low, high[s]), (wT_high, high[s]))
                        for n, (w, x) in enumerate(parts):
                            for k in range(2):
                                cols, rows = seg(k)
                                for p in range(PATCH):
                                    mm = pe.matmul(psY[s][k][0:rows, 0:GT], w[:, p, cols], x[:, :, p:N * PATCH:PATCH],
                                                   start=(n == 0 and p == 0), stop=(n == 2 and p == PATCH - 1))
                        mm.then_inc(y_done[s], 1)

            def over_groups(eng, split, keep):
                split(0, 0)
                with eng.Fori(0, G // 2 - 1) as i:
                    split(i, 1)
                    keep(i, 0)
                    split(i + 1, 0)
                    keep(i, 1)
                split(G // 2 - 1, 1)
                keep(G // 2 - 1, 0)
                keep(G // 2 - 1, 1)

            two_weights = lambda w, k: w[0:CH, 2 * k:2 * k + 2, :].rearrange("c p e -> c (p e)")

            @block.vector
            def _(dve):
                for a in range(2):
                    dve.memset(xs[a][64:96, :, :], 0.0).then_inc(padded, 1)
                dve.wait_ge(const_made, 5)
                dve.tensor_reduce(self.half_mask[:, :], self.head_mask[:, :].rearrange("p (r s) -> p s r", s=2), AX.X, ALU.add)
                dve.wait_ge(const_made, CONSTANTS)
                for w in (wT_high, wT_low):
                    dve.tensor_copy(w[64:96, :, :], self.zeros[64:96, :].rearrange("c (a e) -> c a e", a=1).to_broadcast([32, PATCH, C]))\
                       .then_inc(wT_padded, 1)
                dve.wait_ge(wT_padded, 2)
                for k in range(PATCH // 2):
                    dve.wait_ge(wT_high_made, k + 1)
                    dve.tensor_tensor(two_weights(wT_low, k), psT[k % 2][0:CH, 0:384], two_weights(wT_high, k).bitcast(F32),
                                      ALU.subtract).then_inc(wT_made, 1)
                dve.wait_ge(b_in, 32)
                for s in range(2):
                    dve.sem_inc(y_kept_dve[s], 1)

                def split(i, s):
                    for a in range(2):
                        dve.wait_ge(high_made[s], i * 2 + a + 1)
                        dve.tensor_tensor(low[s][:, half(a), :], xs[a][:, :, :], high[s][:, half(a), :].bitcast(F32),
                                          ALU.subtract).then_inc(low_made[s], 1)
                        dve.wait_ge(low_made[s], i * 2 + a + 1)
                        dve.sem_inc(split_done[a], 1)

                def keep(i, s):
                    dve.wait_ge(y_done[s], i + 2)
                    dve.tensor_scalar(hT[1][0:CB, bass.ds((i * 2 + s) * GT, GT)], psY[s][1][0:CB, 0:GT],
                                      bias[0:CB, 1:2], None, ALU.add).then_inc(y_kept_dve[s], 1)

                over_groups(dve, split, keep)

            @block.scalar
            def _(act):
                act.wait_ge(wT_padded, 2)
                for k in range(PATCH // 2):
                    act.wait_ge(turned, k + 1)
                    act.activation(two_weights(wT_high, k), psT[k % 2][0:CH, 0:384], ACT.Copy).then_inc(wT_high_made, 1)
                act.wait_ge(b_in, 32)
                for s in range(2):
                    act.sem_inc(y_kept_act[s], 1)

                def split(i, s):
                    act.wait_ge(y_done[s], i + 1)
                    for a in range(2):
                        act.wait_ge(x_in[a], (i * 2 + s) * 16 + 16)
                        act.activation(high[s][:, half(a), :], xs[a][:, :, :], ACT.Copy).then_inc(high_made[s], 1)

                def keep(i, s):
                    act.wait_ge(y_done[s], i + 2)
                    act.activation(hT[0][:, bass.ds((i * 2 + s) * GT, GT)], psY[s][0][0:CA, 0:GT], ACT.Identity,
                                   bias=bias[0:CA, 0:1]).then_inc(y_kept_act[s], 1)

                over_groups(act, split, keep)

    def layernorm(self, name, load_next=None):
        nc, hT, xT = self.nc, self.hT, self.xT
        SLOTS = 4
        TC, TT = GT // 4, 4
        with ExitStack() as ctx:
            sb = lambda n, shape, dt=F32: ctx.enter_context(nc.sbuf_tensor(f"{name}_{n}", shape, dt))
            sem = lambda n: self.semaphore(ctx, f"{name}_{n}")
            cen = [sb(f"centred{s}", [CA, 2, GT]) for s in range(SLOTS)]
            sq = [sb(f"square{s}", [CA, 2, GT]) for s in range(SLOTS)]
            dev = [sb(f"dev{s}", [TC, TT]) for s in range(SLOTS)]
            inv = [sb(f"inv{s}", [TC, TT]) for s in range(SLOTS)]
            diag = [sb(f"diag{s}", [96, TT, TC]) for s in range(SLOTS)]
            psM = [ctx.enter_context(nc.psum_tensor(f"{name}_mean{s}", [128, 512], F32)) for s in range(SLOTS)]
            psV = [ctx.enter_context(nc.psum_tensor(f"{name}_var{s}", [128, 512], F32)) for s in range(SLOTS)]
            zeroed, mean, centred, squared = sem("zeroed"), sem("mean"), sem("centred"), sem("squared")
            var, rooted, inverted, spread, normed = sem("var"), sem("rooted"), sem("inverted"), sem("spread"), sem("normed")
            block = ctx.enter_context(nc.Block())

            def turn(i, s, rounds):
                return (i + rounds) * SLOTS + s

            if load_next is not None:
                @block.sync
                def _(sp):
                    load_next(sp)

            @block.tensor
            def _(pe):
                pe.sem_inc(spread, SLOTS)
                pe.sem_inc(var, SLOTS)
                with pe.Fori(0, G // SLOTS) as i:
                    for s in range(SLOTS):
                        pe.wait_ge(centred, 2 * turn(i, s, 0) + 2)
                        for k in range(2):
                            mm = pe.matmul(psM[s][0:CA, 0:GT], self.mean_w[0:CA, 0:CA],
                                           hT[k][0:CA, bass.ds((i * SLOTS + s) * GT, GT)], start=(k == 0), stop=(k == 1))
                        mm.then_inc(mean, 1)
                    for s in range(SLOTS):
                        pe.wait_ge(squared, turn(i, s, 1) + 1)
                        pe.wait_ge(normed, 2 * turn(i, s, 0) + 2)
                        for t in range(TT):
                            for k in range(2):
                                mm = pe.matmul(psV[s][0:TC, GT + t:GT + t + 1], sq[s][:, k, TC * t:TC * t + TC],
                                               self.mean_w[0:CA, 0:1], start=(k == 0), stop=(k == 1))
                        mm.then_inc(var, 1)
                    for s in range(SLOTS):
                        pe.wait_ge(inverted, 2 * turn(i, s, 1) + 2)
                        pe.matmul(psV[s][0:CA, 0:GT], self.ones[0:96, 0:CA], diag[s][:, :, :], start=True, stop=True)\
                          .then_inc(spread, 1)

            @block.vector
            def _(dve):
                dve.sem_inc(centred, 2 * SLOTS)
                dve.sem_inc(inverted, 2 * SLOTS)
                dve.sem_inc(normed, 2 * SLOTS)
                dve.wait_ge(zeroed, SLOTS)
                with dve.Fori(0, G // SLOTS) as i:
                    for s in range(SLOTS):
                        dve.wait_ge(mean, turn(i, s, 0) + 1)
                        dve.wait_ge(squared, turn(i, s, 0) + 1)
                        dve.wait_ge(normed, 2 * turn(i, s, 0) + 2)
                        for k in range(2):
                            dve.tensor_tensor(cen[s][:, k, :], hT[k][0:CA, bass.ds((i * SLOTS + s) * GT, GT)],
                                              psM[s][0:CA, 0:GT], ALU.subtract).then_inc(centred, 1)
                    for s in range(SLOTS):
                        dve.wait_ge(rooted, turn(i, s, 1) + 1)
                        dve.reciprocal(inv[s][:, :], dev[s][:, :]).then_inc(inverted, 1)
                        dve.wait_ge(inverted, 2 * turn(i, s, 1) + 1)
                        dve.wait_ge(spread, turn(i, s, 0) + 1)
                        dve.tensor_tensor(diag[s][0:TC, :, :],
                                          self.ident[0:TC, 0:TC].rearrange("p (a t) -> p a t", a=1).to_broadcast([TC, TT, TC]),
                                          inv[s][:, :].rearrange("p (t a) -> p t a", a=1).to_broadcast([TC, TT, TC]),
                                          ALU.mult).then_inc(inverted, 1)
                    for s in range(SLOTS):
                        dve.wait_ge(spread, turn(i, s, 1) + 1)
                        for k in range(2):
                            dve.tensor_tensor(xT[k][0:CA, bass.ds((i * SLOTS + s) * GT, GT)], cen[s][:, k, :],
                                              psV[s][0:CA, 0:GT], ALU.mult).then_inc(normed, 1)

            @block.gpsimd
            def _(pool):
                for s in range(SLOTS):
                    pool.memset(diag[s][64:96, :, :], 0.0).then_inc(zeroed, 1)

            @block.scalar
            def _(act):
                act.sem_inc(squared, SLOTS)
                act.sem_inc(rooted, SLOTS)
                with act.Fori(0, G // SLOTS) as i:
                    for s in range(SLOTS):
                        act.wait_ge(centred, 2 * turn(i, s, 1) + 2)
                        act.wait_ge(var, turn(i, s, 0) + 1)
                        act.activation(sq[s][:, :, :], cen[s][:, :, :], ACT.Square).then_inc(squared, 1)
                    for s in range(SLOTS):
                        act.wait_ge(var, turn(i, s, 1) + 1)
                        act.wait_ge(inverted, 2 * turn(i, s, 0) + 2)
                        act.activation(dev[s][:, :], psV[s][0:TC, GT:GT + TT], ACT.Sqrt, bias=self.eps[0:TC, 0:1])\
                           .then_inc(rooted, 1)

    def turn_blocks(self, pe, bank, src, cols):
        for j in range(len(src)):
            mm = pe.transpose(bank[0:CA, 96 * j:96 * j + 96], src[j], self.ident[0:96, 0:96])
        return mm

    def attention0(self):
        nc, inp, hT, xT = self.nc, self.inp, self.hT, self.xT
        ROUNDS = 4
        JOBS = 10
        HALF = GB // 2
        with ExitStack() as ctx:
            sb = lambda n, shape, dt=F32: ctx.enter_context(nc.sbuf_tensor(f"a0_{n}", shape, dt))
            ps = lambda n, shape: ctx.enter_context(nc.psum_tensor(f"a0_{n}", shape, F32))
            sem = lambda n: self.semaphore(ctx, f"a0_{n}")
            w_nat = sb("w_nat", [96, 8, C])
            wT = [sb(f"wT{k}", [97, 4, C]) for k in range(2)]
            wmax, gmax = sb("wmax", [96, 2]), sb("gmax", [96, 2])
            lnw, lng = sb("lnw", [96, 2]), sb("lng", [96, 2])
            expo, raw = sb("expo", [96, 2]), sb("raw", [96, 2])
            pow2, above, below = sb("pow2", [96, 2]), sb("above", [96, 2]), sb("below", [96, 2])
            up, scale, inv_scale = sb("up", [96, 2]), sb("scale", [96, 2]), sb("inv_scale", [96, 2])
            xg = sb("xg", [97, 2, GT])
            qT, kT = sb("qT", [96, 2, GT]), sb("kT", [96, 2, GT])
            qm = sb("q_masked", [96, 2, 3, GB, NN])
            v = sb("v", [96, GB, C])
            shifted = [sb(f"shifted{e}", [NN, 2, PAIRS, N]) for e in range(2)]
            top = [sb(f"top{e}", [NN, 2, PAIRS]) for e in range(2)]
            total = [sb(f"total{e}", [NN, 2, PAIRS]) for e in range(2)]
            inv_total = [sb(f"inv_total{e}", [NN, 2, PAIRS]) for e in range(2)]
            pT = [[sb(f"pT{k}{e}", [96, 3, NN]) for e in range(2)] for k in range(2)]
            oT = sb("oT", [97, 2, GT])
            ring = [ps(f"ring{s}", [128, 2, 512]) for s in range(2)]
            psT = [ps(f"turn{e}", [128, 512]) for e in range(2)]
            psO = [ps(f"o{k}", [128, 512]) for k in range(2)]

            w_in, rows_in, w_turned, wT_made = sem("w_in"), sem("rows_in"), sem("w_turned"), sem("wT_made")
            maxed, scale_step, logs, raised2 = sem("maxed"), sem("scale_step"), sem("logs"), sem("raised2")
            zeroed, w_scaled, x_scaled = sem("zeroed"), sem("w_scaled"), sem("x_scaled")
            full = [sem(f"ring_full{s}") for s in range(2)]
            kept = [sem(f"ring_kept{s}") for s in range(2)]
            xg_made, k_kept, q_masked = sem("xg_made"), sem("k_kept"), sem("q_masked")
            soft = [sem(f"soft_step{e}") for e in range(2)]
            raised = [sem(f"raised{e}") for e in range(2)]
            p_made = [sem(f"p_made{e}") for e in range(2)]
            p_turned = [sem(f"p_turned{k}") for k in range(2)]
            pT_made = [sem(f"pT_made{k}") for k in range(2)]
            pT_used = [sem(f"pT_used{k}") for k in range(2)]
            o_half, o_kept = sem("o_half"), sem("o_kept")
            block = ctx.enter_context(nc.Block())
            TURNED = 3
            SJOB, QJOB, KJOB, VJOB, NJOB, PJOB = 0, 2, 3, 4, 6, 8
            FIRST = 6
            per = JOBS // 2
            first_job = {QJOB: 0, KJOB: 1, VJOB: 2, VJOB + 1: 3, NJOB: 4, NJOB + 1: 5}

            def place(i, job):
                if isinstance(i, int) and i < 0:
                    return first_job[job] % 2, first_job[job] // 2
                return job % 2, FIRST // 2 + i * per + job // 2

            def score_place(i, bb):
                return place(i - 1, NJOB + bb) if bb < 2 else place(i, SJOB + bb - 2)

            def projection_job(m, more):
                return (PJOB if more else SJOB + 2) + m

            @block.sync
            def _(sp):
                sp.dma_start(w_nat[:, 0:6, :], inp["L0_attn_qkv_weight"].rearrange("(r e) c -> e r c", e=96)).then_inc(w_in, 16)
                sp.dma_start(w_nat[:, 6:8, :], inp["L0_attn_proj_weight"].rearrange("(r e) c -> e r c", e=96)).then_inc(w_in, 16)
                sp.dma_start(wT[1][96:97, 0:3, :], inp["L0_attn_qkv_bias"].rearrange("(a r c) -> a r c", a=1, r=3)).then_inc(rows_in, 16)
                sp.dma_start(wT[1][96:97, 3, :], inp["L0_attn_proj_bias"].rearrange("(a c) -> a c", a=1)).then_inc(rows_in, 16)

            @block.gpsimd
            def _(pool):
                pool.memset(v[:, :, :], 0.0).then_inc(zeroed, 1)
                for k in range(2):
                    for e in range(2):
                        pool.memset(pT[k][e][:, :, :], 0.0).then_inc(zeroed, 1)
                pool.wait_ge(zeroed, 5)
                pool.memset(oT[96:97, 1, :], 1.0).then_inc(zeroed, 1)
                pool.memset(xg[96:97, 1, :], 1.0).then_inc(zeroed, 1)
                pool.wait_ge(zeroed, 7)
                for s in range(2):
                    pool.sem_inc(kept[s], 1)
                pool.wait_ge(x_scaled, 2)
                for k in range(2):
                    pool.tensor_copy(xg[0:CA, k, :], xT[k][0:CA, 0:GT]).then_inc(xg_made, 1)
                for d in range(2):
                    pool.wait_ge(kept[d], place(-1, VJOB + d)[1] + 2)
                for k in range(2):
                    pool.tensor_copy(xg[0:CA, k, :], xT[k][0:CA, GT:2 * GT]).then_inc(xg_made, 1)
                with pool.Fori(0, G - 2) as i:
                    for d in range(2):
                        pool.wait_ge(kept[d], place(i, VJOB + d)[1] + 2)
                    for k in range(2):
                        pool.tensor_copy(xg[0:CA, k, :], xT[k][0:CA, bass.ds((i + 2) * GT, GT)]).then_inc(xg_made, 1)

            @block.tensor
            def _(pe):
                pe.wait_ge(w_in, 32)
                for r in range(ROUNDS):
                    if r >= 2:
                        pe.wait_ge(wT_made, 2 * r - 2)
                    srcs = [w_nat[:, 2 * r + a, CA * k:CA * k + CA] for k in range(2) for a in range(2)]
                    self.turn_blocks(pe, psT[r % 2], srcs, 96).then_inc(w_turned, 1)
                pe.wait_ge(w_scaled, 2)
                pe.wait_ge(x_scaled, 2)
                pe.wait_ge(wT_made, 2 * ROUNDS)
                pe.wait_ge(rows_in, 32)
                pe.wait_ge(zeroed, 7)
                for k in range(2):
                    pe.sem_inc(p_turned[k], TURNED)
                    pe.sem_inc(pT_used[k], 2)
                def project(i, what):
                    s, before = place(i, QJOB + what)
                    pe.wait_ge(kept[s], before + 1)
                    for m in range(2):
                        for k in range(2):
                            r = CA + k
                            mm = pe.matmul(ring[s][0:CA, m, 0:GT], wT[k][0:r, what, CA * m:CA * m + CA],
                                           xT[k][0:r, bass.ds((i + 1) * GT, GT)], start=(k == 0), stop=(k == 1))
                    mm.then_inc(full[s], 1)

                def values(i):
                    pe.wait_ge(xg_made, i * 2 + 4)
                    for d in range(2):
                        s, before = place(i, VJOB + d)
                        pe.wait_ge(kept[s], before + 1)
                        for n in range(4):
                            b = 4 * d + n
                            for k in range(2):
                                r = CA + k
                                mm = pe.matmul(ring[s][0:N, n // 2, C * (n % 2):C * (n % 2) + C],
                                               xg[0:r, k, N * b:N * b + N], wT[k][0:r, 2, :],
                                               start=(k == 0), stop=(k == 1))
                        mm.then_inc(full[s], 1)

                def scores(i, bb):
                    s, before = score_place(i, bb)
                    pe.wait_ge(kept[s], before + 1)
                    for j in range(2):
                        b = 2 * bb + j
                        for pr in range(PAIRS):
                            mm = pe.matmul(ring[s][0:NN, j, N * pr:N * pr + N], qm[:, pr // 3, pr % 3, b, :],
                                           kT[:, pr // 3, N * b:N * b + N], start=True, stop=True)
                    mm.then_inc(full[s], 1)

                def first_scores(i):
                    pe.wait_ge(k_kept, i + 1)
                    pe.wait_ge(q_masked, i * H + H)
                    scores(i, 0)
                    scores(i, 1)

                def turn(b, k):
                    bb = b // 2
                    for r in range(3):
                        mm = pe.transpose(psT[k][0:N, NN * r:NN * r + NN],
                                          shifted[bb % 2][:, b % 2, 3 * k + r, :], self.ident[0:NN, 0:NN])
                    mm.then_inc(p_turned[k], 1)

                def group(i, more):
                    for k in range(2):
                        pe.wait_ge(pT_made[k], i * GB + 1)
                    pe.wait_ge(p_made[0], i * 2 + 1)
                    scores(i, 2)
                    for k in range(2):
                        turn(0, k)
                    scores(i, 3)
                    for b in range(GB):
                        if more and b in (2, 4):
                            project(i, b // 2 - 1)
                        if b % 4 == 0:
                            pe.wait_ge(o_kept, i * 4 + b // 2 + 2)
                        for k in range(2):
                            pe.wait_ge(pT_made[k], i * GB + b + 2)
                            for r in range(3):
                                if b % 2 == 1 and b + 1 < GB and (k, r) == (0, 2):
                                    bb = (b + 1) // 2
                                    pe.wait_ge(p_made[bb % 2], i * 2 + bb // 2 + 1)
                                mm = pe.matmul(psO[k][32 * r:32 * r + 32, NN * (b % 4):NN * (b % 4) + NN],
                                               v[:, b, CA * k + 32 * r:CA * k + 32 * r + 32], pT[k][b % 2][:, r, :],
                                               start=True, stop=True)
                            mm.then_inc(pT_used[k], 1)
                            if b + 1 < GB:
                                turn(b + 1, k)
                    if more:
                        values(i)
                        first_scores(i + 1)
                    pe.wait_ge(o_kept, i * 4 + 6)
                    for m in range(2):
                        s, before = place(i, projection_job(m, more))
                        pe.wait_ge(kept[s], before + 1)
                        for k in range(2):
                            r = CA + k
                            mm = pe.matmul(ring[s][0:CA, 0, 0:GT], wT[k][0:r, 3, CA * m:CA * m + CA], oT[0:r, k, :],
                                           start=(k == 0), stop=(k == 1))
                        mm.then_inc(full[s], 1)

                for what in range(2):
                    project(-1, what)
                values(-1)
                first_scores(0)
                with pe.Fori(0, G - 1) as i:
                    group(i, True)
                group(G - 1, False)

            @block.scalar
            def _(act):
                act.wait_ge(maxed, 2)
                act.activation(lng[:, :], gmax[:, :], ACT.Ln).then_inc(logs, 1)
                act.wait_ge(maxed, 4)
                act.activation(lnw[:, :], wmax[:, :], ACT.Ln).then_inc(logs, 1)
                act.wait_ge(scale_step, 2)
                act.activation(raw[:, :], expo[:, :], ACT.Exp).then_inc(raised2, 1)
                for k in range(2):
                    act.sem_inc(pT_made[k], 1)
                act.wait_ge(zeroed, 7)
                def keep_queries(i):
                    s, before = place(i, QJOB)
                    act.wait_ge(full[s], before + 1)
                    act.activation(qT[:, :, :], ring[s][0:CA, :, 0:GT], ACT.Copy, scale=HD ** -0.5).then_inc(kept[s], 1)

                def keep_values(i):
                    for d in range(2):
                        s, before = place(i, VJOB + d)
                        act.wait_ge(full[s], before + 1)
                        act.activation(v[0:N, 4 * d:4 * d + 4, :].rearrange("n (j a) c -> n j (a c)", j=2),
                                       ring[s][0:N, :, 0:2 * C], ACT.Copy).then_inc(kept[s], 1)

                def raise_(i, bb):
                    s, before = score_place(i, bb)
                    act.wait_ge(kept[s], before + 2)
                    act.activation(shifted[bb % 2][:, :, :, :], shifted[bb % 2][:, :, :, :], ACT.Exp)\
                       .then_inc(raised[bb % 2], 1)

                def group(i, more):
                    for b in range(GB):
                        for k in range(2):
                            act.wait_ge(p_turned[k], i * GB + b + 1 + TURNED)
                            act.wait_ge(pT_used[k], i * GB + b + 1)
                            act.activation(pT[k][b % 2][0:N, :, :].rearrange("n r m -> n (r m)"), psT[k][0:N, 0:3 * NN], ACT.Copy)\
                               .then_inc(pT_made[k], 1)
                        if b == 1:
                            raise_(i, 2)
                        if b == 2 and more:
                            keep_queries(i)
                        if b == 4:
                            raise_(i, 3)
                    if more:
                        keep_values(i)
                        raise_(i + 1, 0)
                        raise_(i + 1, 1)

                keep_queries(-1)
                keep_values(-1)
                raise_(0, 0)
                raise_(0, 1)
                with act.Fori(0, G - 1) as i:
                    group(i, True)
                group(G - 1, False)

            @block.vector
            def _(dve):
                for k in range(2):
                    dve.tensor_reduce(gmax[:, k:k + 1], xT[k][0:CA, :], AX.X, ALU.max, apply_absolute_value=True)\
                       .then_inc(maxed, 1)
                for r in range(ROUNDS):
                    dve.wait_ge(w_turned, r + 1)
                    for k in range(2):
                        dve.tensor_copy(wT[k][0:CA, r, :], psT[r % 2][0:CA, C * k:C * k + C]).then_inc(wT_made, 1)
                dve.wait_ge(wT_made, 6)
                for k in range(2):
                    dve.tensor_reduce(wmax[:, k:k + 1], wT[k][0:CA, 0:3, :], AX.XY, ALU.max, apply_absolute_value=True)\
                       .then_inc(maxed, 1)
                dve.wait_ge(logs, 2)
                dve.tensor_scalar(expo[:, :], lnw[:, :], -0.65, None, ALU.mult).then_inc(scale_step, 1)
                dve.wait_ge(scale_step, 1)
                dve.scalar_tensor_tensor(out=expo[:, :], in0=lng[:, :], scalar=0.35, in1=expo[:, :], op0=ALU.mult,
                                         op1=ALU.add).then_inc(scale_step, 1)
                dve.wait_ge(raised2, 1)
                dve.tensor_scalar(pow2[:, :].bitcast(I32), raw[:, :].bitcast(I32), 0x7F800000, None, ALU.bitwise_and)\
                   .then_inc(scale_step, 1)
                dve.wait_ge(scale_step, 3)
                dve.tensor_tensor(above[:, :], raw[:, :], pow2[:, :], ALU.subtract).then_inc(scale_step, 1)
                dve.scalar_tensor_tensor(out=below[:, :], in0=pow2[:, :], scalar=2.0, in1=raw[:, :], op0=ALU.mult,
                                         op1=ALU.subtract).then_inc(scale_step, 1)
                dve.wait_ge(scale_step, 5)
                dve.tensor_tensor(up[:, :], above[:, :], below[:, :], ALU.is_gt).then_inc(scale_step, 1)
                dve.wait_ge(scale_step, 6)
                dve.scalar_tensor_tensor(out=scale[:, :], in0=up[:, :], scalar=1.0, in1=pow2[:, :], op0=ALU.add,
                                         op1=ALU.mult).then_inc(scale_step, 1)
                dve.wait_ge(scale_step, 7)
                dve.reciprocal(inv_scale[:, :], scale[:, :]).then_inc(scale_step, 1)
                for k in range(2):
                    dve.tensor_scalar(wT[k][0:CA, 0:3, :], wT[k][0:CA, 0:3, :], scale[:, k:k + 1], None, ALU.mult)\
                       .then_inc(w_scaled, 1)
                dve.wait_ge(scale_step, 8)
                for k in range(2):
                    dve.tensor_scalar(xT[k][0:CA, :], xT[k][0:CA, :], inv_scale[:, k:k + 1], None, ALU.mult)\
                       .then_inc(x_scaled, 1)
                dve.sem_inc(o_kept, 2)
                def keep_keys(i):
                    s, before = place(i, KJOB)
                    dve.wait_ge(full[s], before + 1)
                    dve.tensor_copy(kT[:, :, :], ring[s][0:CA, :, 0:GT]).then_inc(kept[s], 1)
                    dve.wait_ge(kept[s], before + 2)
                    dve.sem_inc(k_kept, 1)
                    s, before = place(i, QJOB)
                    dve.wait_ge(kept[s], before + 2)
                    for k in range(2):
                        for h in range(PAIRS):
                            dve.tensor_scalar(
                                qm[:, k, h // 2, :, :].rearrange("c b (s n) -> c b s n", s=2)[:, :, h % 2, :],
                                qT[:, k, :].rearrange("c (b n) -> c b n", b=GB), self.head_mask[0:96, h:h + 1], None,
                                ALU.mult).then_inc(q_masked, 1)

                def shift(i, bb):
                    e, n = bb % 2, (i * 2 + bb // 2) * 3
                    s, before = score_place(i, bb)
                    src = ring[s][0:NN, :, 0:PAIRS * N].rearrange("m j (p n) -> m j p n", p=PAIRS)
                    dve.wait_ge(full[s], before + 1)
                    dve.wait_ge(p_turned[1], i * GB + 2 * bb + 1)
                    dve.tensor_reduce(top[e][:, :, :], src, AX.X, ALU.max).then_inc(soft[e], 1)
                    dve.wait_ge(soft[e], n + 1)
                    dve.tensor_tensor(shifted[e][:, :, :, :], src,
                                      top[e][:, :, :].rearrange("m j (p a) -> m j p a", a=1).to_broadcast([NN, 2, PAIRS, N]),
                                      ALU.subtract).then_inc(kept[s], 1)

                def normalise(i, bb):
                    e, n = bb % 2, (i * 2 + bb // 2) * 3
                    dve.wait_ge(raised[e], i * 2 + bb // 2 + 1)
                    dve.tensor_reduce(total[e][:, :, :], shifted[e][:, :, :, :], AX.X, ALU.add).then_inc(soft[e], 1)
                    dve.wait_ge(soft[e], n + 2)
                    dve.reciprocal(inv_total[e][:, :, :], total[e][:, :, :]).then_inc(soft[e], 1)
                    dve.wait_ge(soft[e], n + 3)
                    dve.tensor_tensor(shifted[e][:, :, :, :], shifted[e][:, :, :, :],
                                      inv_total[e][:, :, :].rearrange("m j (p a) -> m j p a", a=1).to_broadcast([NN, 2, PAIRS, N]),
                                      ALU.mult).then_inc(p_made[e], 1)

                def keep_outputs(i, d):
                    for k in range(2):
                        src = psO[k][0:CA, 0:4 * NN].rearrange("c (b s n) -> c b s n", b=4, s=2)
                        dst = oT[0:CA, k, 4 * N * d:4 * N * d + 4 * N].rearrange("c (b n) -> c b n", b=4)
                        dve.wait_ge(pT_used[k], i * GB + 4 * d + 4 + 2)
                        dve.tensor_scalar(dst, src[:, :, 0, :], self.half_mask[0:CA, 0:1], None, ALU.mult)\
                           .then_inc(o_half, 1)
                        dve.wait_ge(o_half, i * 4 + 2 * d + k + 1)
                        dve.scalar_tensor_tensor(out=dst, in0=src[:, :, 1, :], scalar=self.half_mask[0:CA, 1:2],
                                                 in1=dst, op0=ALU.mult, op1=ALU.add).then_inc(o_kept, 1)

                def group(i, more):
                    normalise(i, 1)
                    shift(i, 2)
                    normalise(i, 2)
                    shift(i, 3)
                    keep_outputs(i, 0)
                    normalise(i, 3)
                    if more:
                        keep_keys(i)
                    keep_outputs(i, 1)
                    if more:
                        shift(i + 1, 0)
                        shift(i + 1, 1)
                        normalise(i + 1, 0)
                    for m in range(2):
                        s, before = place(i, projection_job(m, more))
                        dve.wait_ge(full[s], before + 1)
                        h_at = hT[m][0:CA, bass.ds(i * GT, GT)]
                        dve.tensor_tensor(h_at, h_at, ring[s][0:CA, 0, 0:GT], ALU.add).then_inc(kept[s], 1)

                keep_keys(-1)
                shift(0, 0)
                shift(0, 1)
                normalise(0, 0)
                with dve.Fori(0, G - 1) as i:
                    group(i, True)
                group(G - 1, False)

    def attention1_loads(self, scope):
        nc, inp = self.nc, self.inp
        HB, KR = H // 2, 96 + H // 2
        sb = lambda n, shape, dt=F32: scope.enter_context(nc.sbuf_tensor(f"a1_{n}", shape, dt))
        wT = [sb(f"wT{k}", [97, 2, C]) for k in range(2)]
        w_nat = sb("w_nat", [96, 4, C])
        wk_nat = sb("wk_nat", [96, 2, C + 1])
        w1_nat = sb("w1_nat", [96, H])
        b1_rows = sb("b1_rows", [KR, 2, O1])
        conv = sb("conv", [2, PAIRS, MIX_CONSTS])
        w_in, rows_in, conv_in, b1_in = [self.semaphore(scope, f"a1_{n}") for n in ("w_in", "rows_in", "conv_in", "b1_in")]

        def start(sp):
            for a, n in enumerate(("q", "v")):
                sp.dma_start(w_nat[:, 2 * a:2 * a + 2, :], inp[f"L1_attn_w{n}"].rearrange("(r e) c -> e r c", e=96)).then_inc(w_in, 16)
                sp.dma_start(wT[1][96:97, a, :], inp[f"L1_attn_b{n}"].rearrange("(a c) -> a c", a=1)).then_inc(rows_in, 16)
            sp.dma_start(wk_nat[:, :, 0:C], inp["L1_attn_wk"].rearrange("(r e) c -> e r c", e=96)).then_inc(w_in, 16)
            with nc.allow_non_contiguous_dma(reason="one bias value for each row"):
                sp.dma_start(wk_nat[:, :, C:C + 1], inp["L1_attn_bk"].rearrange("(r e a) -> e r a", e=96, a=1)).then_inc(w_in, 16)
                sp.dma_start(w1_nat[:, :], inp["L1_attn_w1"]).then_inc(w_in, 16)
                sp.dma_start(b1_rows[96:KR, :, :], inp["L1_attn_b1"].rearrange("(k h o) -> h k o", k=2, o=O1)).then_inc(b1_in, 16)
                at = 0
                for n, width in (("w2", 8), ("b2", 1), ("w3", 4), ("b3", 4), ("w4", 4), ("b4", 1)):
                    src = inp[f"L1_attn_{n}"]
                    if len(src.shape) == 2:
                        src = src.rearrange("a b -> (a b)")
                    sp.dma_start(conv[:, :, at:at + width], src.rearrange("(r s o) -> s r o", s=2, o=width)).then_inc(conv_in, 16)
                    at += width

        return start, (wT, w_nat, wk_nat, w1_nat, b1_rows, conv), (w_in, rows_in, conv_in, b1_in)

    def attention1(self, loaded):
        nc, hT, xT = self.nc, self.hT, self.xT
        JOBS = 36
        QJOB, VJOB = 0, 22
        KJOB = [2, 3, 4, 5, 10, 11, 16, 17]
        AJOB = [6, 12, 18, 24, 28, 32]
        NC = MIX_CONSTS
        W2, B2, W3, B3, W4, B4 = 0, 8, 9, 13, 17, 21
        HB = H // 2
        KR = 96 + HB
        LAG = 3
        with ExitStack() as ctx:
            sb = lambda n, shape, dt=F32: ctx.enter_context(nc.sbuf_tensor(f"a1_{n}", shape, dt))
            ps = lambda n, shape: ctx.enter_context(nc.psum_tensor(f"a1_ps_{n}", shape, F32))
            sem = lambda n: self.semaphore(ctx, f"a1_{n}")
            wT = loaded[1][0]
            kmixT = [sb(f"kmixT{k}", [97, O1, C]) for k in range(2)]
            wide = sb("conv_wide", [NN, PAIRS, NC])
            kmix = sb("kmix", [KR, 2, GB, O1, N])
            qm = sb("q_masked", [KR, 2, 3, GB, NN])
            qT, xg = sb("qT", [96, 2, GT]), sb("xg", [97, 2, GT])
            v, aT = sb("v", [96, GB, C]), sb("aT", [96, GB, NN])
            ring = [ps(f"ring{s}", [128, 2, 512]) for s in range(2)]
            psT = [ps(f"turn{h}", [128, 512]) for h in range(2)]
            psO = ps("o", [128, 2, 512])
            self.attention1_weights(loaded, kmixT, wide, kmix, qm, qT, xg, v, aT, ring, psT)

            maps = [sb(f"maps{s}", [NN, GB, O1, N]) for s in range(2)]
            mid = [sb(f"mid{s}", [NN, GB, N]) for s in range(2)]
            fine = [sb(f"fine{s}", [NN, O3, GT]) for s in range(2)]
            amap = [sb(f"amap{s}", [NN, GB, N]) for s in range(2)]
            full = [sem(f"ring_full{s}") for s in range(2)]
            kept = [sem(f"ring_kept{s}") for s in range(2)]
            xg_made, q_masked = sem("xg_made"), sem("q_masked")
            mid_step, mid_made = sem("mid_step"), sem("mid_made")
            fine_made = sem("fine_made")
            amap_step, amap_made = sem("amap_step"), sem("amap_made")
            turned = [sem(f"turned{h}") for h in range(2)]
            aT_made = [sem(f"aT_made{h}") for h in range(2)]
            o_done = [sem(f"o_done{h}") for h in range(2)]
            o_half, o_kept = sem("o_half"), sem("o_kept")
            block = ctx.enter_context(nc.Block())
            per = JOBS // 2
            slot_free = lambda i, job: i * per + job // 2 + 1
            job_full = lambda i, job: i * per + job // 2 + 1
            job_kept = lambda i, job: i * per + job // 2 + 2
            const = lambda p, c: wide[:, p, c:c + 1]

            @block.gpsimd
            def _(pool):
                for s in range(2):
                    pool.sem_inc(kept[s], 1)
                for k in range(2):
                    pool.tensor_copy(xg[0:CA, k, :], xT[k][0:CA, 0:GT]).then_inc(xg_made, 1)
                with pool.Fori(0, G - 1) as i:
                    for s in range(2):
                        pool.wait_ge(kept[s], job_kept(i, VJOB + s))
                    for k in range(2):
                        pool.tensor_copy(xg[0:CA, k, :], xT[k][0:CA, bass.ds((i + 1) * GT, GT)]).then_inc(xg_made, 1)

            @block.tensor
            def _(pe):
                for h in range(2):
                    pe.sem_inc(turned[h], 2)
                    pe.sem_inc(o_done[h], 1)
                def queries(i):
                    for m in range(2):
                        job = QJOB + m
                        pe.wait_ge(kept[job % 2], slot_free(i, job))
                        for k in range(2):
                            r = CA + k
                            mm = pe.matmul(ring[job % 2][0:CA, 0, 0:GT], wT[k][0:r, 0, CA * m:CA * m + CA],
                                           xT[k][0:r, bass.ds(i * GT, GT)], start=(k == 0), stop=(k == 1))
                        mm.then_inc(full[job % 2], 1)

                def mixed_keys(i, kj):
                    job, m = KJOB[kj], kj // 4
                    pe.wait_ge(kept[job % 2], slot_free(i, job))
                    for j in range(2):
                        o = 2 * (kj % 4) + j
                        for k in range(2):
                            r = CA + k
                            mm = pe.matmul(ring[job % 2][0:CA, j, 0:GT], kmixT[k][0:r, o, CA * m:CA * m + CA],
                                           xT[k][0:r, bass.ds(i * GT, GT)], start=(k == 0), stop=(k == 1))
                    mm.then_inc(full[job % 2], 1)

                def values(i):
                    pe.wait_ge(xg_made, i * 2 + 2)
                    for d in range(2):
                        job = VJOB + d
                        pe.wait_ge(kept[job % 2], slot_free(i, job))
                        for n in range(4):
                            b = 4 * d + n
                            for k in range(2):
                                r = CA + k
                                mm = pe.matmul(ring[job % 2][0:N, n // 2, C * (n % 2):C * (n % 2) + C],
                                               xg[0:r, k, N * b:N * b + N], wT[k][0:r, 1, :],
                                               start=(k == 0), stop=(k == 1))
                        mm.then_inc(full[job % 2], 1)

                def first_maps(i, p, bb):
                    job = AJOB[p] + bb
                    pe.wait_ge(kept[job % 2], slot_free(i, job))
                    for j in range(2):
                        b = 2 * bb + j
                        mm = pe.matmul(ring[job % 2][0:NN, j, 0:O1 * N], qm[:, p // 3, p % 3, b, :],
                                       kmix[:, p // 3, b, :, :], start=True, stop=True)
                    mm.then_inc(full[job % 2], 1)

                def turn_waits(i, p):
                    pe.wait_ge(amap_made, i * PAIRS + p + 1 + 2)
                    for h in range(2):
                        pe.wait_ge(aT_made[h], i * PAIRS + p + 1)

                def turn(p):
                    for h in range(2):
                        for b in range(4 * h, 4 * h + 4):
                            mm = pe.transpose(psT[h][0:N, NN * (b % 4):NN * (b % 4) + NN], amap[p % 2][:, b, :],
                                              self.ident[0:NN, 0:NN])
                        mm.then_inc(turned[h], 1)

                def outputs(i, p):
                    k, r = p // 3, p % 3
                    if r == 0:
                        pe.wait_ge(o_kept, i * 4 + 2 * k + 2)
                    for h in range(2):
                        pe.wait_ge(aT_made[h], i * PAIRS + p + 2)
                        for b in range(4 * h, 4 * h + 4):
                            mm = pe.matmul(psO[32 * r:32 * r + 32, h, NN * (b % 4):NN * (b % 4) + NN],
                                           v[:, b, 32 * p:32 * p + 32], aT[:, b, :], start=True, stop=True)
                        mm.then_inc(o_done[h], 1)

                def group(i, before):
                    def late(p, todo):
                        if p >= LAG:
                            todo(i, p - LAG)
                        elif before is not None:
                            todo(before, PAIRS + p - LAG)

                    queries(i)
                    mixed_keys(i, 0)
                    if before is not None:
                        turn_waits(before, PAIRS - LAG)
                    mixed_keys(i, 1)
                    if before is not None:
                        turn(PAIRS - LAG)
                    mixed_keys(i, 2)
                    mixed_keys(i, 3)
                    for k in range(2):
                        pe.wait_ge(kept[k], job_kept(i, KJOB[2 + k]))
                    for p in range(PAIRS):
                        if p % 3 == 0:
                            pe.wait_ge(q_masked, i * H + HB * (p // 3 + 1))
                        if p > 0:
                            late(p, turn_waits)
                        first_maps(i, p, 0)
                        if p > 0:
                            late(p, lambda _, q: turn(q))
                        for bb in range(1, 4):
                            first_maps(i, p, bb)
                        late(p, outputs)
                        if p < 2:
                            for kj in (4 + 2 * p, 5 + 2 * p):
                                mixed_keys(i, kj)
                        if p == 2:
                            values(i)

                group(0, None)
                with pe.Fori(0, G - 1) as i:
                    group(i + 1, i)
                for p in range(PAIRS - LAG, PAIRS):
                    turn_waits(G - 1, p)
                    turn(p)
                    outputs(G - 1, p)

            @block.scalar
            def _(act):
                act.sem_inc(fine_made, 2 * O3)
                def keep_queries(i):
                    for m in range(2):
                        job = QJOB + m
                        act.wait_ge(full[job % 2], job_full(i, job))
                        act.activation(qT[:, m, :], ring[job % 2][0:CA, 0, 0:GT], ACT.Copy, scale=C ** -0.5)\
                           .then_inc(kept[job % 2], 1)

                def keep_keys(i, kj):
                    job, m, o = KJOB[kj], kj // 4, 2 * (kj % 4)
                    act.wait_ge(full[job % 2], job_full(i, job))
                    act.activation(kmix[0:CA, m, :, o:o + 2, :].rearrange("c b o n -> c o b n"),
                                   ring[job % 2][0:CA, :, 0:GT].rearrange("c o (b n) -> c o b n", b=GB),
                                   ACT.Copy).then_inc(kept[job % 2], 1)

                def keep_values(i):
                    for d in range(2):
                        job = VJOB + d
                        act.wait_ge(full[job % 2], job_full(i, job))
                        act.activation(v[0:N, 4 * d:4 * d + 4, :].rearrange("n (j a) c -> n j (a c)", j=2),
                                       ring[job % 2][0:N, :, 0:2 * C], ACT.Copy).then_inc(kept[job % 2], 1)

                def third(i, p):
                    act.wait_ge(mid_made, i * PAIRS + p + 1 + 2)
                    act.wait_ge(amap_made, i * PAIRS + p + 1)
                    for j in range(O3):
                        act.activation(fine[p % 2][:, j, :], mid[p % 2][:, :, :].rearrange("m b n -> m (b n)"), ACT.Relu,
                                       bias=const(p, B3 + j), scale=const(p, W3 + j)).then_inc(fine_made, 1)

                def group(i, before):
                    keep_queries(i)
                    for kj in range(4):
                        keep_keys(i, kj)
                        if kj == 1 and before is not None:
                            third(before, PAIRS - 1)
                    for p in range(PAIRS):
                        act.wait_ge(mid_made, i * PAIRS + p + 1)
                        for bb in range(4):
                            job = AJOB[p] + bb
                            act.wait_ge(full[job % 2], job_full(i, job))
                            act.activation(maps[p % 2][:, 2 * bb:2 * bb + 2, :, :].rearrange("m j o n -> m j (o n)"),
                                           ring[job % 2][0:NN, :, 0:O1 * N], ACT.Relu).then_inc(kept[job % 2], 1)
                        if p >= 1:
                            third(i, p - 1)
                        if p < 2:
                            for kj in (4 + 2 * p, 5 + 2 * p):
                                keep_keys(i, kj)
                        if p == 2:
                            keep_values(i)

                group(0, None)
                with act.Fori(0, G - 1) as i:
                    group(i + 1, i)
                third(G - 1, PAIRS - 1)

            @block.vector
            def _(dve):
                dve.sem_inc(mid_made, 2)
                dve.sem_inc(amap_made, 2)
                dve.sem_inc(o_kept, 2)
                for h in range(2):
                    dve.sem_inc(aT_made[h], 1)
                def mask_queries(i):
                    for k in range(2):
                        dve.wait_ge(kept[(QJOB + k) % 2], job_kept(i, QJOB + k))
                        for h in range(HB):
                            dve.tensor_scalar(
                                qm[0:CA, k, h // 2, :, :].rearrange("c b (s n) -> c b s n", s=2)[:, :, h % 2, :],
                                qT[:, k, :].rearrange("c (b n) -> c b n", b=GB), self.head_mask[0:96, h:h + 1], None,
                                ALU.mult).then_inc(q_masked, 1)

                def second(i, p):
                    m = maps[p % 2]
                    for s in range(2):
                        dve.wait_ge(kept[s], job_kept(i, AJOB[p] + 2 + s))
                    dve.wait_ge(fine_made, (i * PAIRS + p) * O3 + O3)
                    for o in range(O1):
                        n = (i * PAIRS + p) * (O1 - 1) + o
                        if o == 0:
                            ins = dve.tensor_scalar(mid[p % 2][:, :, :], m[:, :, 0, :], const(p, W2), const(p, B2), ALU.mult, ALU.add)
                        else:
                            dve.wait_ge(mid_step, n)
                            ins = dve.scalar_tensor_tensor(out=mid[p % 2][:, :, :], in0=m[:, :, o, :], scalar=const(p, W2 + o),
                                                           in1=mid[p % 2][:, :, :], op0=ALU.mult, op1=ALU.add)
                        ins.then_inc(mid_step if o < O1 - 1 else mid_made, 1)

                def fourth(i, p):
                    f = fine[p % 2]
                    out = amap[p % 2][:, :, :].rearrange("m b n -> m (b n)")
                    dve.wait_ge(fine_made, (i * PAIRS + p) * O3 + O3 + 2 * O3)
                    dve.wait_ge(turned[1], i * PAIRS + p + 1)
                    for j in range(O3):
                        n = (i * PAIRS + p) * (O3 - 1) + j
                        if j == 0:
                            ins = dve.tensor_scalar(out, f[:, 0, :], const(p, W4), const(p, B4), ALU.mult, ALU.add)
                        else:
                            dve.wait_ge(amap_step, n)
                            ins = dve.scalar_tensor_tensor(out=out, in0=f[:, j, :], scalar=const(p, W4 + j), in1=out,
                                                           op0=ALU.mult, op1=ALU.add)
                        ins.then_inc(amap_step if j < O3 - 1 else amap_made, 1)

                def keep_turned(i, p):
                    for h in range(2):
                        dve.wait_ge(turned[h], i * PAIRS + p + 1 + 2)
                        dve.wait_ge(o_done[h], i * PAIRS + p + 1)
                        dve.tensor_copy(aT[0:N, 4 * h:4 * h + 4, :].rearrange("n b m -> n (b m)"), psT[h][0:N, 0:4 * NN])\
                           .then_inc(aT_made[h], 1)

                def keep_outputs(i, k):
                    for h in range(2):
                        src = psO[0:CA, h, 0:4 * NN].rearrange("c (b s n) -> c b s n", b=4, s=2)
                        dst = hT[k][0:CA, bass.ds(i * GT + h * (GT // 2), GT // 2)].rearrange("c (b n) -> c b n", b=4)
                        dve.wait_ge(o_done[h], i * PAIRS + 3 * k + 3 + 1)
                        dve.scalar_tensor_tensor(out=dst, in0=src[:, :, 0, :], scalar=self.half_mask[0:CA, 0:1], in1=dst,
                                                 op0=ALU.mult, op1=ALU.add).then_inc(o_half, 1)
                        dve.wait_ge(o_half, i * 4 + 2 * k + h + 1)
                        dve.scalar_tensor_tensor(out=dst, in0=src[:, :, 1, :], scalar=self.half_mask[0:CA, 1:2], in1=dst,
                                                 op0=ALU.mult, op1=ALU.add).then_inc(o_kept, 1)

                def group(i, before):
                    mask_queries(i)
                    if before is not None:
                        keep_turned(before, PAIRS - LAG)
                        fourth(before, PAIRS - 1)
                    for p in range(PAIRS):
                        second(i, p)
                        if p == 2 and before is not None:
                            keep_outputs(before, 1)
                        if p == PAIRS - 1:
                            keep_outputs(i, 0)
                        elif p >= 2:
                            keep_turned(i, p - 2)
                        elif before is not None:
                            keep_turned(before, PAIRS + p - 2)
                        if p >= 1:
                            fourth(i, p - 1)

                group(0, None)
                with dve.Fori(0, G - 1) as i:
                    group(i + 1, i)
                keep_turned(G - 1, PAIRS - LAG)
                fourth(G - 1, PAIRS - 1)
                for p in (PAIRS - 2, PAIRS - 1):
                    keep_turned(G - 1, p)
                keep_outputs(G - 1, 1)

    def attention1_weights(self, loaded, kmixT, wide, kmix, qm, qT, xg, v, aT, ring, psT):
        nc, inp = self.nc, self.inp
        HB, KR = H // 2, 96 + H // 2
        NC = MIX_CONSTS
        wT, w_nat, wk_nat, w1_nat, b1_rows, conv = loaded[1]
        w_in, rows_in, conv_in, b1_in = loaded[2]
        with ExitStack() as ctx:
            sb = lambda n, shape, dt=F32: ctx.enter_context(nc.sbuf_tensor(f"a1w_{n}", shape, dt))
            sem = lambda n: self.semaphore(ctx, f"a1w_{n}")
            small = sb("small", [HB, 3, 96])
            spread = sb("spread", [96, 2, H, O1])
            diag = sb("diag", [96, HD])
            mixer = sb("mixer", [96, 2, O1, H, HD])
            zeroed, turned, small_made, spread_done = sem("zeroed"), sem("turned"), sem("small_made"), sem("spread_done")
            wT_made, diag_made, spread_made, mixer_made = sem("wT_made"), sem("diag_made"), sem("spread_made"), sem("mixer_made")
            folded, folded_kept, wide_made, rows_made = sem("folded"), sem("folded_kept"), sem("wide_made"), sem("rows_made")
            block = ctx.enter_context(nc.Block())

            @block.gpsimd
            def _(pool):
                pool.memset(v[:, :, :], 0.0).then_inc(zeroed, 1)
                pool.memset(aT[:, :, :], 0.0).then_inc(zeroed, 1)
                pool.memset(xg[96:97, 1, :], 1.0).then_inc(zeroed, 1)

            @block.tensor
            def _(pe):
                pe.wait_ge(w_in, 16 * 5)
                pe.wait_ge(rows_in, 32)
                for r in range(2):
                    srcs = [w_nat[:, 2 * r + a, CA * k:CA * k + CA] for k in range(2) for a in range(2)]
                    self.turn_blocks(pe, psT[r], srcs, 96).then_inc(turned, 1)
                bank = ring[0]
                pe.transpose(bank[0:HB, 0, 0:96], self.head_mask[0:96, 0:HB], self.ident[0:96, 0:96])
                for k in range(2):
                    mm = pe.transpose(bank[0:HB, 0, 96 + 96 * k:192 + 96 * k], w1_nat[:, HB * k:HB * k + HB], self.ident[0:96, 0:96])
                mm.then_inc(turned, 1)
                pe.wait_ge(small_made, 1)
                for k in range(2):
                    mm = pe.matmul(bank[0:96, 1, 96 * k:96 * k + 96], small[:, 0, :], small[:, 1 + k, :], start=True, stop=True)
                mm.then_inc(spread_done, 1)
                pe.wait_ge(conv_in, 16 * 6)
                pe.matmul(ring[1][0:NN, 0, 0:PAIRS * NC], self.pair_rows[:, :], conv[:, :, :], start=True, stop=True)\
                  .then_inc(spread_done, 1)
                pe.wait_ge(mixer_made, 2 * O1)
                pe.wait_ge(wT_made, 4)
                for o in range(O1):
                    if o >= 2:
                        pe.wait_ge(folded_kept, 2 * (o - 1))
                    for m in range(2):
                        rows = CA + m
                        for k in range(2):
                            mm = pe.matmul(psT[o % 2][0:rows, C * m:C * m + C], wk_nat[:, k, CA * m:CA * m + rows],
                                           mixer[:, k, o, :, :], start=(k == 0), stop=(k == 1))
                    mm.then_inc(folded, 1)

            @block.vector
            def _(dve):
                dve.tensor_reduce(diag[:, :], self.ident[0:96, 0:96].rearrange("p (h d) -> p d h", d=HD), AX.X, ALU.add).then_inc(diag_made, 1)
                for r in range(2):
                    dve.wait_ge(turned, r + 1)
                    for k in range(2):
                        dve.tensor_copy(wT[k][0:CA, r, :], psT[r][0:CA, C * k:C * k + C]).then_inc(wT_made, 1)
                dve.wait_ge(turned, 3)
                dve.tensor_copy(small[:, :, :].rearrange("h a e -> h (a e)"), ring[0][0:HB, 0, 0:288]).then_inc(small_made, 1)
                dve.wait_ge(spread_done, 1)
                dve.tensor_copy(spread[:, :, :, :].rearrange("e k g o -> e (k g o)"), ring[0][0:96, 1, 0:192]).then_inc(spread_made, 1)
                dve.wait_ge(spread_done, 2)
                dve.tensor_copy(wide[:, :, :].rearrange("m p c -> m (p c)"), ring[1][0:NN, 0, 0:PAIRS * NC]).then_inc(wide_made, 1)
                dve.wait_ge(spread_made, 1)
                dve.wait_ge(diag_made, 1)
                for k in range(2):
                    for o in range(O1):
                        ins = dve.tensor_tensor(mixer[:, k, o, :, :], spread[:, k, :, o:o + 1].to_broadcast([96, H, HD]),
                                                diag[:, :].rearrange("p (a d) -> p a d", a=1).to_broadcast([96, H, HD]), ALU.mult)
                        ins.then_inc(mixer_made, 1)
                dve.wait_ge(b1_in, 16)
                for k in range(2):
                    for b in range(GB):
                        dve.tensor_copy(kmix[96:KR, k, b, :, :],
                                        b1_rows[96:KR, k, :].rearrange("h (o n) -> h o n", n=1).to_broadcast([HB, O1, N])).then_inc(rows_made, 1)
                    for h in range(HB):
                        dve.tensor_copy(qm[96:KR, k, h // 2, :, :].rearrange("c b (s n) -> c b s n", s=2)[:, :, h % 2, :],
                                        self.ident[96:KR, 96 + h:97 + h].rearrange("c (b n) -> c b n", b=1).to_broadcast([HB, GB, N]))\
                           .then_inc(rows_made, 1)
                for o in range(O1):
                    dve.wait_ge(folded, o + 1)
                    dve.tensor_copy(kmixT[0][0:CA, o, :], psT[o % 2][0:CA, 0:C]).then_inc(folded_kept, 1)
                    dve.tensor_copy(kmixT[1][0:CA + 1, o, :], psT[o % 2][0:CA + 1, C:2 * C]).then_inc(folded_kept, 1)

    def experts(self, name, gate, tiles, last):
        nc, inp = self.nc, self.inp
        gate_w, gate_b, centre, w1_d, b1_d, w2_d, b2_d = [None if n is None else inp[n] for n in gate]
        E = gate_w.shape[1]
        TOPK = 2 if last else 1
        func = ACT.Relu if last else ACT.Gelu
        sorted_x = nc.dram_tensor(f"{name}_sorted_x", (tiles * 128, C), F32, kind="Internal").ap()
        sorted_y = nc.dram_tensor(f"{name}_sorted_y", (tiles * 128, C), F32, kind="Internal").ap()
        with ExitStack() as outer:
            sb0 = lambda n, shape, dt=F32: outer.enter_context(nc.sbuf_tensor(f"{name}_{n}", shape, dt))
            w1 = [sb0(f"w1_{k}", [97, E, F]) for k in range(2)]
            w2 = sb0("w2", [128, E, FC, C])
            b2 = sb0("b2", [1, E, C])
            pos = [sb0(f"pos{t}", [128, RT], U32) for t in range(TOPK)]
            weight = [sb0(f"weight{t}", [128, RT]) for t in range(TOPK)]
            expert_of = sb0("expert_of", [128, tiles], I32)
            h_rows = sb0("h_rows", [128, RT, C]) if last else None
            x_rows = sb0("x_rows", [128, RT, C]) if last else None
            load_need = sb0("load_need", [128, tiles], I32) if last else None
            gather_need = sb0("gather_need", [128, 2], I32) if last else None
            weights_in = self.semaphore(outer, f"{name}_weights_in")
            early = (x_rows, load_need, gather_need)
            self.route(name, E, TOPK, tiles, gate_w, gate_b, centre, pos, weight, expert_of, h_rows, sorted_x, sorted_y, early,
                       (w1, w2, b2, w1_d, b1_d, w2_d, b2_d, weights_in))
            self.run_experts(name, E, tiles, func, w1, w2, b2, expert_of, weights_in, sorted_x, sorted_y,
                             pos, early)
            self.gather(name, TOPK, pos, weight, h_rows, x_rows, sorted_y)

    def route(self, name, E, TOPK, tiles, gate_w, gate_b, centre, pos, weight, expert_of, h_rows, sorted_x, sorted_y, early, loads):
        nc, hT, xT = self.nc, self.hT, self.xT
        w1, w2, b2, w1_d, b1_d, w2_d, b2_d, weights_in = loads
        sources = [xT, hT] if h_rows is not None else [xT]
        S = len(sources)
        with ExitStack() as ctx:
            sb = lambda n, shape, dt=F32: ctx.enter_context(nc.sbuf_tensor(f"{name}_{n}", shape, dt))
            ps = lambda n, shape: ctx.enter_context(nc.psum_tensor(f"{name}_ps_{n}", shape, F32))
            sem = lambda n: self.semaphore(ctx, f"{name}_{n}")
            gw = [sb(f"gate{k}", [97, E]) for k in range(2)]
            centre_row = sb("centre", [97, E])
            staged = [[sb(f"staged{s}_{a}", [97, 2, GT]) for a in range(S)] for s in range(2)]
            x_rows, load_need, gather_need = early
            if x_rows is None:
                x_rows = sb("x_rows", [128, RT, C])
            rows = [x_rows, h_rows]
            score = sb("score", [128, RT, E])
            e_code = sb("e_code", [128, E])
            t_index = sb("t_index", [128, tiles])
            e_int, t_int = sb("e_int", [128, E], I32), sb("t_int", [128, tiles], I32)
            best = [sb(f"best{t}", [128, RT]) for t in range(TOPK)]
            code = sb("code", [128, RT])
            pick = [sb(f"pick{t}", [128, RT, E]) for t in range(TOPK)]
            chosen, work = sb("chosen", [128, RT, E]), sb("work", [128, RT, E])
            sums = [sb(f"sums{a}", [128, RT, E]) for a in range(2)]
            row_of = sb("row_of", [128, RT, E])
            n_tiles_i, n_tiles = sb("n_tiles_i", [128, E], I32), sb("n_tiles", [128, E])
            ends = [sb(f"ends{a}", [128, E]) for a in range(2)]
            starts = sb("starts", [128, E])
            passed, count_of = sb("passed", [128, tiles, E]), sb("count_of", [128, tiles])
            pos_f = [sb(f"pos_f{t}", [128, RT]) for t in range(TOPK)]
            swap, stay, by = sb("swap", [128, RT]), sb("stay", [128, RT]), [sb(f"by{t}", [128, RT]) for t in range(TOPK)]
            need_f, need_i = sb("need_f", [128, tiles]), sb("need_i", [128, 2], I32)
            psS = [ps(f"scores{s}", [128, 512]) for s in range(2)]
            psR = [ps(f"rows{u}", [128, 2, 512]) for u in range(2)]
            psP, psC = ps("before", [128, 512]), ps("counts", [128, 512])
            gate_in, centre_in, y_cleared = sem("gate_in"), sem("centre_in"), sem("y_cleared")
            zeroed, cleared, iota_made, gate_made = sem("zeroed"), sem("cleared"), sem("iota_made"), sem("gate_made")
            staged_in = [sem(f"staged_in{s}") for s in range(2)]
            turned = [[sem(f"turned{s}_{a}") for a in range(S)] for s in range(2)]
            rows_kept = [sem(f"rows_kept{u}") for u in range(2)]
            score_kept = [sem(f"score_kept{s}") for s in range(2)]
            scored = [sem(f"scored{s}") for s in range(2)]
            step_done, picked, counted = sem("step_done"), sem("picked"), sem("counted")
            exp_needed, exp_made, placed, scattered = sem("exp_needed"), sem("exp_made"), sem("placed"), self.scattered[name]
            block = ctx.enter_context(nc.Block())

            bank = lambda s, a: (s + a) % 2 if S == 1 else a
            bank_uses = lambda i, s: i if S == 1 else i * 2 + s

            @block.sync
            def _(sp):
                for k in range(2):
                    sp.dma_start(gw[k][0:CA, :], gate_w[CA * k:CA * k + CA, :]).then_inc(gate_in, 16)
                sp.dma_start(gw[1][CA:CA + 1, :], gate_b.rearrange("(a e) -> a e", a=1)).then_inc(gate_in, 16)
                if centre is not None:
                    sp.dma_start(centre_row[CA:CA + 1, :], centre.rearrange("(a e) -> a e", a=1)).then_inc(centre_in, 16)
                sp.dma_start(sorted_x.rearrange("(t p) c -> p t c", p=128),
                             self.zeros[:, :].rearrange("p (t c) -> p t c", t=1).to_broadcast([128, tiles, C])).then_inc(cleared, 16)
                for k in range(2):
                    sp.dma_start(w1[k][0:CA, :, :], w1_d[:, CA * k:CA * k + CA, :].rearrange("e c f -> c e f")).then_inc(weights_in, 16)
                sp.dma_start(w1[1][CA:CA + 1, :, :], b1_d.rearrange("(a e) f -> a e f", a=1)).then_inc(weights_in, 16)
                for e in range(E):
                    sp.dma_start(w2[:, e, :, :], w2_d[e].rearrange("(q p) c -> p q c", p=128)).then_inc(weights_in, 16)
                sp.dma_start(b2[:, :, :], b2_d.rearrange("(a e) c -> a e c", a=1)).then_inc(weights_in, 16)
                if TOPK == 2:
                    sp.dma_start(sorted_y.rearrange("(t p) c -> p t c", p=128),
                                 self.zeros[:, :].rearrange("p (t c) -> p t c", t=1).to_broadcast([128, tiles, C])).then_inc(y_cleared, 16)
                    sp.wait_ge(y_cleared, 16)

            @block.gpsimd
            def _(pool):
                pool.iota(e_int[:, :], pattern=[[1, E]], base=-100, channel_multiplier=0).then_inc(iota_made, 1)
                pool.iota(t_int[:, :], pattern=[[1, tiles]], base=0, channel_multiplier=0).then_inc(iota_made, 1)
                pool.memset(score[:, :, :], 0.0).then_inc(zeroed, 1)
                pool.wait_ge(zeroed, 1)
                pool.wait_ge(iota_made, 2)
                for s in range(2):
                    pool.memset(staged[s][0][CA:CA + 1, 1, :], 1.0).then_inc(zeroed, 1)
                pool.wait_ge(zeroed, 3)
                pool.wait_ge(iota_made, 2)
                pool.wait_ge(cleared, 16)
                pool.wait_ge(placed, TOPK)
                for s in range(2):
                    pool.wait_ge(rows_kept[s], S * (G // 2) + 1)
                for j in range(RT):
                    r = ROWS[j % Q3]
                    pool.indirect_dma_start(out=sorted_x, out_offset=bass.IndirectOffsetOnAxis(ap=pos[0][0:r, j:j + 1], axis=0),
                                            in_=x_rows[0:r, j, :], in_offset=None).then_inc(scattered, 16)
                if TOPK == 1:
                    pool.wait_ge(scattered, 16 * RT)

            @block.tensor
            def _(pe):
                pe.wait_ge(gate_made, 1)
                pe.wait_ge(zeroed, 3)
                with pe.Fori(0, G // 2) as i:
                    for s in range(2):
                        pe.wait_ge(score_kept[s], i + 1)
                        pe.wait_ge(staged_in[s], i * 2 * S + 2 * S)
                        for q in range(Q3):
                            for k in range(2):
                                r = CA + k
                                mm = pe.matmul(psS[s][0:ROWS[q], E * q:E * q + E], staged[s][0][0:r, k, 128 * q:128 * q + ROWS[q]],
                                               gw[k][0:r, :], start=(k == 0), stop=(k == 1))
                        for a in range(S):
                            pe.wait_ge(rows_kept[bank(s, a)], bank_uses(i, s) + 1)
                            for q in range(Q3):
                                for k in range(2):
                                    mm = pe.transpose(psR[bank(s, a)][0:ROWS[q], q // 2, C * (q % 2) + CA * k:C * (q % 2) + CA * k + CA],
                                                      staged[s][a][0:CA, k, 128 * q:128 * q + ROWS[q]], self.ident[0:CA, 0:CA])
                            mm.then_inc(scored[s] if a == S - 1 else turned[s][a], 1)
                pe.wait_ge(picked, 1)
                pe.matmul(psP[:, 0:RT * E], self.below[:, :], chosen[:, :, :], start=True, stop=True)
                pe.matmul(psC[:, 0:RT * E], self.ones[:, :], chosen[:, :, :], start=True, stop=True).then_inc(counted, 1)

            @block.scalar
            def _(act):
                for s in range(2):
                    act.sem_inc(rows_kept[s], 1)
                with act.Fori(0, G // 2) as i:
                    for s in range(2):
                        for a in range(S):
                            if a == S - 1:
                                act.wait_ge(scored[s], i + 1)
                            else:
                                act.wait_ge(turned[s][a], i + 1)
                            act.activation(rows[a][:, bass.ds((i * 2 + s) * Q3, 2), :].rearrange("p q c -> p (q c)"),
                                           psR[bank(s, a)][:, 0, 0:2 * C], ACT.Copy)
                            act.activation(rows[a][0:ROWS[2], bass.ds((i * 2 + s) * Q3 + 2, 1), :].rearrange("p q c -> p (q c)"),
                                           psR[bank(s, a)][0:ROWS[2], 1, 0:C], ACT.Copy)\
                               .then_inc(rows_kept[bank(s, a)], 1)
                if TOPK == 2:
                    act.wait_ge(exp_needed, 1)
                    act.activation(weight[1][:, :], best[1][:, :], ACT.Exp).then_inc(exp_made, 1)

            @block.vector
            def _(dve):
                steps = 0

                def step(ins):
                    nonlocal steps
                    ins.then_inc(step_done, 1)
                    steps += 1
                    dve.wait_ge(step_done, steps)

                over_e = lambda m: m[:, :].rearrange("p (j a) -> p j a", a=1).to_broadcast([128, RT, E])
                over_j = lambda m: m[:, :].rearrange("p (a e) -> p a e", a=1).to_broadcast([128, RT, E])
                dve.wait_ge(gate_in, 48)
                if centre is not None:
                    dve.wait_ge(centre_in, 16)
                    dve.tensor_tensor(gw[1][CA:CA + 1, :], gw[1][CA:CA + 1, :], centre_row[CA:CA + 1, :], ALU.subtract)\
                       .then_inc(gate_made, 1)
                else:
                    dve.sem_inc(gate_made, 1)
                dve.wait_ge(iota_made, 2)
                step(dve.tensor_copy(e_code[:, :], e_int[:, :]))
                step(dve.tensor_copy(t_index[:, :], t_int[:, :]))
                dve.wait_ge(zeroed, 3)

                def stage(i, s):
                    for a in range(S):
                        for k in range(2):
                            dve.tensor_copy(staged[s][a][0:CA, k, :], sources[a][k][0:CA, bass.ds((i * 2 + s) * GT, GT)])\
                               .then_inc(staged_in[s], 1)

                def keep_scores(i, s):
                    j = (i * 2 + s) * Q3
                    dve.wait_ge(scored[s], i + 1)
                    dve.tensor_copy(score[:, bass.ds(j, 2), :].rearrange("p q e -> p (q e)"), psS[s][:, 0:2 * E])
                    dve.tensor_copy(score[0:ROWS[2], bass.ds(j + 2, 1), :].rearrange("p q e -> p (q e)"),
                                    psS[s][0:ROWS[2], 2 * E:3 * E]).then_inc(score_kept[s], 1)

                for s in range(2):
                    dve.sem_inc(score_kept[s], 1)
                    stage(0, s)
                with dve.Fori(0, G // 2 - 1) as i:
                    for s in range(2):
                        keep_scores(i, s)
                        stage(i + 1, s)
                for s in range(2):
                    keep_scores(G // 2 - 1, s)
                for s in range(2):
                    dve.wait_ge(score_kept[s], G // 2 + 1)
                for t in range(TOPK):
                    step(dve.tensor_reduce(best[t][:, :], score[:, :, :], AX.X, ALU.max))
                    step(dve.tensor_tensor(work[:, :, :], score[:, :, :], over_e(best[t]), ALU.is_equal))
                    step(dve.tensor_tensor(work[:, :, :], work[:, :, :], over_j(e_code), ALU.mult))
                    step(dve.tensor_reduce(code[:, :], work[:, :, :], AX.X, ALU.min))
                    step(dve.tensor_tensor(pick[t][:, :, :], over_e(code), over_j(e_code), ALU.is_equal))
                    step(dve.tensor_tensor(pick[t][:, :, :], pick[t][:, :, :],
                                           self.row_valid[:, :, :].rearrange("p g (q a) -> p (g q) a", a=1).to_broadcast([128, RT, E]),
                                           ALU.mult))
                    if t < TOPK - 1:
                        step(dve.scalar_tensor_tensor(out=score[:, :, :], in0=pick[t][:, :, :], scalar=-3.0e38,
                                                      in1=score[:, :, :], op0=ALU.mult, op1=ALU.add))
                if TOPK == 2:
                    step(dve.tensor_tensor(best[1][:, :], best[1][:, :], best[0][:, :], ALU.subtract))
                    dve.sem_inc(exp_needed, 1)
                    dve.wait_ge(exp_made, 1)
                    step(dve.tensor_scalar(best[0][:, :], weight[1][:, :], 1.0, None, ALU.add))
                    step(dve.reciprocal(weight[0][:, :], best[0][:, :]))
                    step(dve.tensor_tensor(weight[1][:, :], weight[1][:, :], weight[0][:, :], ALU.mult))
                    dve.tensor_tensor(chosen[:, :, :], pick[0][:, :, :], pick[1][:, :, :], ALU.add).then_inc(picked, 1)
                else:
                    dve.tensor_copy(chosen[:, :, :], pick[0][:, :, :]).then_inc(picked, 1)
                dve.wait_ge(counted, 1)
                flat = lambda m: m[:, :, :].rearrange("p j e -> p (j e)")
                step(dve.tensor_copy(flat(sums[0]), psC[:, 0:RT * E]))
                src, d = 0, 1
                while d < RT:
                    a, b = sums[src], sums[1 - src]
                    step(dve.tensor_copy(b[:, 0:d, :], a[:, 0:d, :]))
                    step(dve.tensor_tensor(b[:, d:RT, :], a[:, d:RT, :], a[:, 0:RT - d, :], ALU.add))
                    src, d = 1 - src, 2 * d
                total = sums[src]
                step(dve.tensor_scalar(n_tiles_i[:, :], total[:, RT - 1, :], 127.0, None, ALU.add))
                step(dve.tensor_scalar(n_tiles_i[:, :], n_tiles_i[:, :], 7, None, ALU.logical_shift_right))
                step(dve.tensor_copy(n_tiles[:, :], n_tiles_i[:, :]))
                step(dve.tensor_copy(ends[0][:, :], n_tiles[:, :]))
                es, d = 0, 1
                while d < E:
                    a, b = ends[es], ends[1 - es]
                    step(dve.tensor_copy(b[:, 0:d], a[:, 0:d]))
                    step(dve.tensor_tensor(b[:, d:E], a[:, d:E], a[:, 0:E - d], ALU.add))
                    es, d = 1 - es, 2 * d
                end = ends[es]
                step(dve.tensor_tensor(starts[:, :], end[:, :], n_tiles[:, :], ALU.subtract))
                step(dve.tensor_scalar(starts[:, :], starts[:, :], 128.0, None, ALU.mult))
                step(dve.tensor_tensor(flat(row_of), flat(total), psC[:, 0:RT * E], ALU.subtract))
                step(dve.tensor_tensor(flat(row_of), flat(row_of), psP[:, 0:RT * E], ALU.add))
                step(dve.tensor_tensor(row_of[:, :, :], row_of[:, :, :], over_j(starts), ALU.add))
                for t in range(TOPK):
                    step(dve.tensor_tensor(work[:, :, :], row_of[:, :, :], pick[t][:, :, :], ALU.mult))
                    step(dve.tensor_reduce(pos_f[t][:, :], work[:, :, :], AX.X, ALU.add))
                if TOPK == 1:
                    dve.tensor_copy(pos[0][:, :], pos_f[0][:, :]).then_inc(placed, 1)
                else:
                    dve.tensor_tensor(pos[0][:, :], pos_f[0][:, :], pos_f[1][:, :], ALU.min).then_inc(placed, 1)
                    dve.tensor_tensor(pos[1][:, :], pos_f[0][:, :], pos_f[1][:, :], ALU.max).then_inc(placed, 1)
                    step(dve.tensor_tensor(swap[:, :], pos_f[0][:, :], pos_f[1][:, :], ALU.is_gt))
                    step(dve.tensor_tensor(stay[:, :], pos_f[0][:, :], pos_f[1][:, :], ALU.is_le))
                    step(dve.tensor_tensor(by[0][:, :], weight[0][:, :], swap[:, :], ALU.mult))
                    step(dve.tensor_tensor(by[1][:, :], weight[1][:, :], swap[:, :], ALU.mult))
                    for t in range(2):
                        step(dve.tensor_tensor(weight[t][:, :], weight[t][:, :], stay[:, :], ALU.mult))
                        step(dve.tensor_tensor(weight[t][:, :], weight[t][:, :], by[1 - t][:, :], ALU.add))
                in_t = [128, tiles, E]
                step(dve.tensor_tensor(passed[:, :, :], t_index[:, :].rearrange("p (t a) -> p t a", a=1).to_broadcast(in_t),
                                       end[:, :].rearrange("p (a e) -> p a e", a=1).to_broadcast(in_t), ALU.is_ge))
                step(dve.tensor_reduce(count_of[:, :], passed[:, :, :], AX.X, ALU.add))
                step(dve.tensor_scalar(expert_of[:, :], count_of[:, :], float(E - 1), None, ALU.min))
                if TOPK == 2:
                    step(dve.tensor_copy(need_f[:, :], passed[:, :, 0]))
                    step(dve.tensor_scalar(load_need[:, :], need_f[:, :], 16.0 * RT, 16.0 * RT, ALU.mult, ALU.add))
                    for s in range(2):
                        step(dve.tensor_scalar(need_i[:, s:s + 1], end[:, E - 2:E - 1], float(1 - s), None, ALU.add))
                    step(dve.tensor_scalar(need_i[:, :], need_i[:, :], 1, None, ALU.logical_shift_right))
                    step(dve.tensor_copy(need_f[:, 0:2], need_i[:, :]))
                    step(dve.tensor_scalar(gather_need[:, :], need_f[:, 0:2], 16.0, 16.0, ALU.mult, ALU.add))

    def run_experts(self, name, E, tiles, func, w1, w2, b2, expert_of, weights_in, sorted_x, sorted_y, pos, early):
        nc = self.nc
        BODY = (tiles - 2) // 2
        x_rows, load_need, gather_need = early
        with ExitStack() as ctx:
            sb = lambda n, shape, dt=F32: ctx.enter_context(nc.sbuf_tensor(f"{name}_{n}", shape, dt))
            ps = lambda n, shape: ctx.enter_context(nc.psum_tensor(f"{name}_ps_{n}", shape, F32))
            sem = lambda n: self.semaphore(ctx, f"{name}_{n}")
            x_in_buf = [sb(f"x_tile{s}", [128, C]) for s in range(2)]
            xt = [sb(f"xt{s}", [97, 2, 128]) for s in range(2)]
            hid = [sb(f"hid{s}", [128, F]) for s in range(2)]
            hidT = sb("hidT", [128, FC, 128])
            y = [sb(f"y{s}", [128, C]) for s in range(2)]
            wait_mark = sb("wait_mark", [128, 2, 8])
            psX, psY = ps("x_turned", [128, 2, 256]), ps("y", [128, 2, 256])
            psH = [ps(f"hid{s}", [128, 2, 512]) for s in range(2)]
            psT = ps("hid_turned", [128, 2, 512])
            ones_made = sem("ones_made")
            x_in = [sem(f"x_in{s}") for s in range(2)]
            x_turned = [sem(f"x_turned{s}") for s in range(2)]
            x_kept = [sem(f"x_kept{s}") for s in range(2)]
            h_done = [sem(f"h_done{s}") for s in range(2)]
            h_kept = [sem(f"h_kept{s}") for s in range(2)]
            t_done = [sem(f"t_done{s}") for s in range(2)]
            t_kept = [sem(f"t_kept{s}") for s in range(2)]
            y_done = [sem(f"y_done{s}") for s in range(2)]
            y_kept = [sem(f"y_kept{s}") for s in range(2)]
            y_out = [sem(f"y_out{s}") for s in range(2)]
            block = ctx.enter_context(nc.Block())

            def over_tiles(eng, first, step, fori_to, peeled_to):
                with eng.Fori(0, fori_to) as i:
                    for s in range(2):
                        step(i, s)
                for t in range(2 * fori_to, peeled_to):
                    step(t // 2, t % 2)

            @block.sync
            def _(sp):
                def load(n, s, ahead=0):
                    if load_need is not None:
                        need = sp.value_load(load_need[0:1, bass.ds(n * 2 + s + ahead, 1)], min_val=16 * RT, max_val=32 * RT)
                        sp.wait_ge(self.scattered[name], need)
                    sp.dma_start(x_in_buf[s][:, :], sorted_x[bass.ds((n * 2 + s + ahead) * 128, 128), :]).then_inc(x_in[s], 16)

                def store(n, s):
                    sp.wait_ge(y_kept[s], n + 2)
                    sp.dma_start(sorted_y[bass.ds((n * 2 + s) * 128, 128), :], y[s][:, :]).then_inc(y_out[s], 16)

                def reload(n, s):
                    sp.wait_ge(x_turned[s], n + 1)
                    load(n, s, 2)

                for ahead in (0, 1):
                    load(0, ahead)
                for t in (0, 1):
                    reload(0, t)
                with sp.Fori(0, BODY - 1) as i:
                    for s in range(2):
                        reload(i + 1, s)
                        store(i, s)
                for t in range(2 * BODY, tiles - 2):
                    reload(t // 2, t % 2)
                    store(t // 2 - 1, t % 2)
                for t in range(tiles - 4, tiles):
                    store(t // 2, t % 2)
                for s in range(2):
                    sp.wait_ge(y_out[s], 16 + 16 * ((tiles + 1 - s) // 2))

            @block.gpsimd
            def _(pool):
                for s in range(2):
                    pool.memset(xt[s][CA:CA + 1, 1, :], 1.0).then_inc(ones_made, 1)
                if gather_need is None:
                    return
                pool.wait_ge(self.scattered[name], 16 * RT)
                for j in range(RT):
                    r = ROWS[j % Q3]
                    pool.indirect_dma_start(out=sorted_x, out_offset=bass.IndirectOffsetOnAxis(ap=pos[1][0:r, j:j + 1], axis=0),
                                            in_=x_rows[0:r, j, :], in_offset=None).then_inc(self.scattered[name], 16)
                pool.wait_ge(self.scattered[name], 32 * RT)
                needs = [pool.value_load(gather_need[0:1, s:s + 1], min_val=16, max_val=16 + 16 * ((tiles + 1) // 2))
                         for s in range(2)]
                for s in range(2):
                    pool.wait_ge(y_out[s], needs[s])
                    pool.tensor_tensor(wait_mark[:, s, :], self.zeros[:, 0:8], self.zeros[:, 0:8], ALU.add)
                for j in range(RT):
                    r = ROWS[j % Q3]
                    pool.indirect_dma_start(out=x_rows[0:r, j, :], out_offset=None, in_=sorted_y,
                                            in_offset=bass.IndirectOffsetOnAxis(ap=pos[0][0:r, j:j + 1], axis=0))\
                        .then_inc(self.gather_ready[name][j // Q3], 16)

            @block.tensor
            def _(pe):
                def turn_x(n, s):
                    pe.wait_ge(x_in[s], n * 16 + 16)
                    for k in range(2):
                        mm = pe.transpose(psX[0:CA, s, 128 * k:128 * k + 128], x_in_buf[s][:, CA * k:CA * k + CA], self.ident[:, :])
                    mm.then_inc(x_turned[s], 1)

                def expert(n, s):
                    return pe.value_load(expert_of[0:1, bass.ds(n * 2 + s, 1)], min_val=0, max_val=E - 1)

                def first_product(n, s):
                    e = expert(n, s)
                    pe.wait_ge(x_kept[s], n + 1)
                    for half in range(2):
                        for k in range(2):
                            r = CA + k
                            mm = pe.matmul(psH[s][:, half, 0:F // 2], xt[s][0:r, k, :],
                                           w1[k][0:r, :, :].rearrange("c e f -> c (e f)")[:, bass.ds(e * F + half * (F // 2), F // 2)],
                                           start=(k == 0), stop=(k == 1))
                    mm.then_inc(h_done[s], 1)

                def turn_hidden(n, s):
                    pe.wait_ge(h_kept[s], n + 1)
                    for q in range(FC):
                        mm = pe.transpose(psT[:, q // 3, 128 * (q % 3):128 * (q % 3) + 128], hid[s][:, 128 * q:128 * q + 128],
                                          self.ident[:, :])
                    mm.then_inc(t_done[s], 1)

                def second_product(n, s):
                    e = expert(n, s)
                    pe.wait_ge(y_kept[1 - s], n + 1 + s)
                    pe.wait_ge(t_kept[s], n + 1)
                    for q in range(FC):
                        pe.matmul(psY[:, s, 0:C], hidT[:, q, :],
                                  w2[:, :, :, :].rearrange("p e q c -> p (e q c)")[:, bass.ds(e * (FC * C) + q * C, C)],
                                  start=(q == 0), stop=False)
                    pe.matmul(psY[:, s, 0:C], self.ones[0:1, 0:128], b2[:, :, :].rearrange("a e c -> a (e c)")[:, bass.ds(e * C, C)],
                              start=False, stop=True).then_inc(y_done[s], 1)

                pe.wait_ge(weights_in, 16 * (4 + E))
                pe.wait_ge(ones_made, 2)
                turn_x(0, 0)
                pe.wait_ge(x_kept[0], 1)
                turn_x(0, 1)
                first_product(0, 0)

                def step(n, s):
                    turn_hidden(n, s)
                    first_product(n + s, 1 - s)
                    turn_x(n + 1, s)
                    second_product(n, s)

                over_tiles(pe, 0, step, BODY, tiles - 2)
                for t in range(tiles - 2, tiles):
                    n, s = t // 2, t % 2
                    turn_hidden(n, s)
                    if t + 1 < tiles:
                        first_product(n + s, 1 - s)
                    second_product(n, s)

            @block.scalar
            def _(act):
                def step(n, s):
                    act.wait_ge(h_done[s], n + 1)
                    act.activation(hid[s][:, :].rearrange("p (a f) -> p a f", a=2), psH[s][:, :, 0:F // 2], func).then_inc(h_kept[s], 1)

                over_tiles(act, 0, step, tiles // 2, tiles)

            @block.vector
            def _(dve):
                def keep_x(n, s):
                    dve.wait_ge(x_turned[s], n + 1)
                    dve.tensor_copy(xt[s][0:CA, :, :], psX[0:CA, s, :].rearrange("c (k p) -> c k p", k=2)).then_inc(x_kept[s], 1)

                def keep_hidden(n, s):
                    dve.wait_ge(t_done[s], n + 1)
                    dve.tensor_copy(hidT[:, :, :].rearrange("f (a q) p -> f a (q p)", a=2), psT[:, :, 0:384]).then_inc(t_kept[s], 1)

                def keep_y(n, s):
                    dve.wait_ge(y_done[s], n + 1)
                    dve.wait_ge(y_out[s], n * 16 + 16)
                    dve.tensor_copy(y[s][:, :], psY[:, s, 0:C]).then_inc(y_kept[s], 1)

                for s in range(2):
                    dve.sem_inc(y_kept[s], 1)
                    dve.sem_inc(y_out[s], 16)
                keep_x(0, 0)
                keep_x(0, 1)

                def step(n, s):
                    keep_hidden(n, s)
                    keep_x(n + 1, s)
                    keep_y(n, s)

                over_tiles(dve, 0, step, BODY, tiles - 2)
                for t in range(tiles - 2, tiles):
                    keep_hidden(t // 2, t % 2)
                    keep_y(t // 2, t % 2)

    def gather(self, name, TOPK, pos, weight, h_rows, got_lower, sorted_y):
        nc, hT = self.nc, self.hT
        with ExitStack() as ctx:
            sb = lambda n, shape, dt=F32: ctx.enter_context(nc.sbuf_tensor(f"{name}_{n}", shape, dt))
            sem = lambda n: self.semaphore(ctx, f"{name}_{n}")
            got = ([] if got_lower is None else [got_lower]) + [sb("got", [128, RT, C])]
            psG = [ctx.enter_context(nc.psum_tensor(f"{name}_back{s}", [128, 512], F32)) for s in range(2)]
            back = [sem(f"back{s}") for s in range(2)]
            added = [sem(f"added{s}") for s in range(2)]
            mixed, summed, stored = sem("mixed"), sem("summed"), sem("stored")
            ready = self.gather_ready[name]
            block = ctx.enter_context(nc.Block())
            per_group = 16 * Q3 * TOPK

            @block.gpsimd
            def _(pool):
                t = TOPK - 1
                if TOPK == 2:
                    for g in range(G):
                        pool.wait_ge(ready[g], 16 * Q3)
                for j in range(RT):
                    r = ROWS[j % Q3]
                    pool.indirect_dma_start(out=got[t][0:r, j, :], out_offset=None, in_=sorted_y,
                                            in_offset=bass.IndirectOffsetOnAxis(ap=pos[t][0:r, j:j + 1], axis=0))\
                        .then_inc(ready[j // Q3], 16)

            if h_rows is None:
                @block.tensor
                def _(pe):
                    for j in range(RT):
                        s, r = j % 2, ROWS[j % Q3]
                        if j % Q3 == 0:
                            pe.wait_ge(ready[j // Q3], per_group)
                        if j >= 2:
                            pe.wait_ge(added[s], 2 * (j // 2))
                        for k in range(2):
                            mm = pe.transpose(psG[s][0:CA, 128 * k:128 * k + r], got[0][0:r, j, CA * k:CA * k + CA],
                                              self.ident[0:r, 0:r])
                        mm.then_inc(back[s], 1)

                @block.vector
                def _(dve):
                    for j in range(RT):
                        s, r = j % 2, ROWS[j % Q3]
                        at = GT * (j // Q3) + 128 * (j % Q3)
                        dve.wait_ge(back[s], j // 2 + 1)
                        for k in range(2):
                            dve.tensor_tensor(hT[k][0:CA, at:at + r], hT[k][0:CA, at:at + r], psG[s][0:CA, 128 * k:128 * k + r],
                                              ALU.add).then_inc(added[s], 1)
            else:
                @block.vector
                def _(dve):
                    for j in range(RT):
                        r = ROWS[j % Q3]
                        if j % Q3 == 0:
                            dve.wait_ge(ready[j // Q3], 16 * Q3)
                        dve.scalar_tensor_tensor(out=got[0][0:r, j, :], in0=got[0][0:r, j, :], scalar=weight[0][0:r, j:j + 1],
                                                 in1=h_rows[0:r, j, :], op0=ALU.mult, op1=ALU.add).then_inc(mixed, 1)
                    for j in range(RT):
                        r = ROWS[j % Q3]
                        if j % Q3 == 0:
                            dve.wait_ge(ready[j // Q3], per_group)
                        dve.wait_ge(mixed, j + 1)
                        dve.scalar_tensor_tensor(out=got[1][0:r, j, :], in0=got[1][0:r, j, :], scalar=weight[1][0:r, j:j + 1],
                                                 in1=got[0][0:r, j, :], op0=ALU.mult, op1=ALU.add).then_inc(summed, 1)

                @block.sync
                def _(sp):
                    rows = self.out.rearrange("b n c -> (b n) c")
                    for g in range(G):
                        sp.wait_ge(summed, Q3 * (g + 1))
                        full = rows[GT * g:GT * g + 256, :].rearrange("(q p) c -> p q c", p=128)
                        sp.dma_start(full, got[1][:, Q3 * g:Q3 * g + 2, :]).then_inc(stored, 16)
                        sp.dma_start(rows[GT * g + 256:GT * g + GT, :], got[1][0:ROWS[2], Q3 * g + 2, :]).then_inc(stored, 16)
                    sp.wait_ge(stored, 32 * G)


def build(nc, inp, out):
    with ExitStack() as ctx:
        t = Tower(nc, inp, out)
        sb = lambda name, shape, dt=F32: ctx.enter_context(nc.sbuf_tensor(name, shape, dt))
        t.scattered, t.gather_ready = {}, {}
        for name in ("ffn0", "ffn1"):
            t.scattered[name] = ctx.enter_context(nc.semaphore(f"{name}_scattered"))
            t.gather_ready[name] = [ctx.enter_context(nc.semaphore(f"{name}_ready{g}")) for g in range(G)]
        t.hT = [sb("hT0", [CA, TOK]), sb("hT1", [CB, TOK])]
        t.xT = [sb("xT0", [CA, TOK]), sb("xT1", [CB + 1, TOK])]
        t.ident = sb("ident", [128, 128])
        t.head_mask = sb("head_mask", [128, 8])
        t.half_mask = sb("half_mask", [128, 2])
        t.pair_rows = sb("pair_rows", [2, NN])
        t.ones = sb("ones", [128, 128])
        t.mean_w = sb("mean_w", [128, 128])
        t.below = sb("below", [128, 128])
        t.zeros = sb("zeros", [128, C])
        t.eps = sb("eps", [128, 1])
        t.row_valid = sb("row_valid", [128, G, Q3])
        t.embed()
        t.layernorm("norm1")
        t.attention0()
        t.layernorm("norm2")
        t.experts("ffn0", ["L0_ffn_gate_w", "L0_ffn_gate_b", "L0_ffn_gate_center", "L0_ffn_w1", "L0_ffn_b1", "L0_ffn_w2",
                           "L0_ffn_b2"], TILES0, last=False)
        t.clear_semaphores()
        with ExitStack() as scope:
            loaded = t.attention1_loads(scope)
            t.layernorm("norm3", load_next=loaded[0])
            t.attention1(loaded)
        t.layernorm("norm4")
        t.experts("ffn1", ["L1_ffn_Wg", "L1_ffn_bg", None, "L1_ffn_W1", "L1_ffn_b1", "L1_ffn_W2", "L1_ffn_b2"],
                  TILES1, last=True)


_INS = ['x', 'L0_tok_W', 'L0_tok_b', 'L0_attn_qkv_weight', 'L0_attn_qkv_bias', 'L0_attn_proj_weight',
        'L0_attn_proj_bias', 'L0_ffn_gate_w', 'L0_ffn_gate_b', 'L0_ffn_gate_center', 'L0_ffn_w1', 'L0_ffn_b1',
        'L0_ffn_w2', 'L0_ffn_b2', 'L1_attn_wq', 'L1_attn_bq', 'L1_attn_wk', 'L1_attn_bk', 'L1_attn_wv',
        'L1_attn_bv', 'L1_attn_w1', 'L1_attn_b1', 'L1_attn_w2', 'L1_attn_b2', 'L1_attn_w3', 'L1_attn_b3',
        'L1_attn_w4', 'L1_attn_b4', 'L1_ffn_Wg', 'L1_ffn_bg', 'L1_ffn_W1', 'L1_ffn_b1', 'L1_ffn_W2', 'L1_ffn_b2']


def kernel(**inputs):
    import numpy as _np
    import concourse.bacc as _bacc
    from concourse import mybir as _mybir
    from concourse.bass_utils import run_bass_kernel_spmd as _run

    nc = _bacc.Bacc("TRN2", target_bir_lowering=False, num_devices=1)
    arrays, inp = {}, {}
    for name in _INS:
        a = _np.ascontiguousarray(inputs[name])
        arrays[f"in_{name}"] = a
        inp[name] = nc.dram_tensor(f"in_{name}", a.shape, _mybir.dt.from_np(a.dtype), kind="ExternalInput").ap()
    out = nc.dram_tensor("out_0", (B, N, C), F32, kind="ExternalOutput").ap()
    build(nc, inp, out)
    r = _run(nc, [arrays], core_ids=[0])
    return r.results[0]["out_0"]
```
